# Optimizing a Trainium2 kernel written in Bass

```python
import numpy as np
import jax
import jax.numpy as jnp

def _softmax(x, axis=-1):
    return jax.nn.softmax(x, axis=axis)

def _gelu(x):
    return jax.nn.gelu(x, approximate=True)

def _silu(x):
    return jax.nn.silu(x)

def _sigmoid(x):
    return jax.nn.sigmoid(x)

def _layernorm(x, axis=-1, eps=1e-05):
    m = jnp.mean(x, axis=axis, keepdims=True)
    v = jnp.var(x, axis=axis, keepdims=True)
    return (x - m) / jnp.sqrt(v + eps)

def _scatter_add(tgt, idx, src, axis=0):
    return tgt.at[idx].add(src)

def _segment_sum(src, seg, n):
    return jax.ops.segment_sum(src, seg, n)
kernel_name = 'mk_seq_preln_d1_jaxref_r4_23cd35'

def setup_inputs(seed: int=0):
    np.random.seed(seed)
    _w = jnp.asarray

    def _L0_attn_setup():
        import jax, jax.numpy as jnp
        import numpy as np
        import math
        D_MODEL = 256
        D_STATE = 128
        D_CONV = 4
        EXPAND = 2
        HEADDIM = 64
        NGROUPS = 1
        N_SCALES = 3
        D_INNER = D_MODEL * EXPAND
        D_SSM = D_INNER
        NHEADS = D_SSM // HEADDIM
        CONV_DIM = D_SSM + 2 * NGROUPS * D_STATE
        D_IN_PROJ = 2 * D_INNER + 2 * NGROUPS * D_STATE + NHEADS
        BATCH = 4
        SEQLEN = 512
        EPS = 1e-05
        key = jax.random.key(seed)
        ks = jax.random.split(key, 8)
        u = jax.random.normal(ks[0], (BATCH, SEQLEN, D_MODEL), dtype=jnp.float32)
        in_proj_w = jax.random.normal(ks[1], (D_IN_PROJ, D_MODEL), dtype=jnp.float32) * 0.02
        conv_w = jax.random.normal(ks[2], (CONV_DIM, 1, D_CONV), dtype=jnp.float32) * 0.3
        conv_b = jnp.zeros((CONV_DIM,), dtype=jnp.float32)
        dt_min, dt_max, dt_init_floor = (0.001, 0.1, 0.0001)
        r = jax.random.uniform(ks[3], (NHEADS,), dtype=jnp.float32)
        dt = jnp.exp(r * (math.log(dt_max) - math.log(dt_min)) + math.log(dt_min))
        dt = jnp.clip(dt, dt_init_floor)
        dt_bias = dt + jnp.log(-jnp.expm1(-dt))
        scales = jnp.arange(1, N_SCALES + 1, dtype=jnp.float32)[:, None]
        A = jax.random.uniform(ks[4], (N_SCALES, NHEADS), dtype=jnp.float32, minval=1.0, maxval=16.0) * scales
        A_log = jnp.log(A)
        D = jnp.ones((NHEADS,), dtype=jnp.float32)
        norm_w = jnp.ones((D_SSM,), dtype=jnp.float32)
        out_proj_w = jax.random.normal(ks[5], (D_MODEL, D_INNER), dtype=jnp.float32) * 0.02
        return {'u': u, 'in_proj_w': in_proj_w, 'conv_w': conv_w, 'conv_b': conv_b, 'dt_bias': dt_bias, 'A_log': A_log, 'D': D, 'norm_w': norm_w, 'out_proj_w': out_proj_w}
    _L0_attn_in = _L0_attn_setup()

    def _L0_ffn_setup():
        import jax, jax.numpy as jnp
        import numpy as np

        def _bitlinear(x, w_latent):
            scale = jax.lax.stop_gradient(jnp.clip(jnp.mean(jnp.abs(w_latent), axis=1, keepdims=True), 1e-05, None))
            tern = jnp.clip(jnp.round(w_latent / scale), -1.0, 1.0)
            w = w_latent + jax.lax.stop_gradient(tern - w_latent)
            return x @ (w * scale).T
        key = jax.random.key(seed)
        ks = jax.random.split(key, 6)
        dim, hidden, rank = (256, 1024, 16)
        B, S = (4, 1024)
        x = jax.random.normal(ks[0], (B, S, dim), dtype=jnp.float32)
        w_fc = 0.02 * jax.random.normal(ks[1], (hidden, dim), dtype=jnp.float32)
        w_proj = 0.02 * jax.random.normal(ks[2], (dim, hidden), dtype=jnp.float32)
        u = 0.02 * jax.random.normal(ks[3], (hidden, rank), dtype=jnp.float32)
        v = 0.02 * jax.random.normal(ks[4], (rank, dim), dtype=jnp.float32)
        fast_b = jax.random.normal(ks[5], (rank, rank), dtype=jnp.float32)
        gate = jnp.float32(0.05)
        return {'x': x, 'fast_b': fast_b, 'w_fc': w_fc, 'w_proj': w_proj, 'u': u, 'v': v, 'gate': gate}
    _L0_ffn_in = _L0_ffn_setup()
    _d = {'L0_attn_u': _L0_attn_in['u'], 'L0_attn_in_proj_w': _L0_attn_in['in_proj_w'], 'L0_attn_conv_w': _L0_attn_in['conv_w'], 'L0_attn_conv_b': _L0_attn_in['conv_b'], 'L0_attn_dt_bias': _L0_attn_in['dt_bias'], 'L0_attn_A_log': _L0_attn_in['A_log'], 'L0_attn_D': _L0_attn_in['D'], 'L0_attn_norm_w': _L0_attn_in['norm_w'], 'L0_attn_out_proj_w': _L0_attn_in['out_proj_w'], 'L0_ffn_fast_b': _L0_ffn_in['fast_b'], 'L0_ffn_w_fc': _L0_ffn_in['w_fc'], 'L0_ffn_w_proj': _L0_ffn_in['w_proj'], 'L0_ffn_u': _L0_ffn_in['u'], 'L0_ffn_v': _L0_ffn_in['v'], 'L0_ffn_gate': _L0_ffn_in['gate']}
    _x0 = _d['L0_attn_u']
    _d['L0_attn_u'] = jax.random.normal(jax.random.fold_in(jax.random.key(seed), 1), (16, 512, 256), dtype=_x0.dtype)
    del _x0
    return _d

def reference(L0_attn_u, L0_attn_in_proj_w, L0_attn_conv_w, L0_attn_conv_b, L0_attn_dt_bias, L0_attn_A_log, L0_attn_D, L0_attn_norm_w, L0_attn_out_proj_w, L0_ffn_fast_b, L0_ffn_w_fc, L0_ffn_w_proj, L0_ffn_u, L0_ffn_v, L0_ffn_gate):

    def _L0_attn_ref(u, in_proj_w, conv_w, conv_b, dt_bias, A_log, D, norm_w, out_proj_w):
        import jax, jax.numpy as jnp
        import numpy as np
        import math
        D_MODEL = 256
        D_STATE = 128
        D_CONV = 4
        EXPAND = 2
        HEADDIM = 64
        NGROUPS = 1
        N_SCALES = 3
        D_INNER = D_MODEL * EXPAND
        D_SSM = D_INNER
        NHEADS = D_SSM // HEADDIM
        CONV_DIM = D_SSM + 2 * NGROUPS * D_STATE
        D_IN_PROJ = 2 * D_INNER + 2 * NGROUPS * D_STATE + NHEADS
        BATCH = 4
        SEQLEN = 512
        EPS = 1e-05
        b, l, _ = u.shape
        zxbcdt = u @ in_proj_w.T
        A = -jnp.exp(A_log.astype(jnp.float32)).mean(axis=0)
        z, xBC, dt = jnp.split(zxbcdt, [D_INNER, D_INNER + CONV_DIM], axis=-1)
        conv = jax.lax.conv_general_dilated(xBC.transpose(0, 2, 1), conv_w, window_strides=(1,), padding=[(D_CONV - 1, 0)], feature_group_count=CONV_DIM, dimension_numbers=('NCH', 'OIH', 'NCH'))
        xBC = jax.nn.silu((conv + conv_b[None, :, None]).transpose(0, 2, 1))
        x, Bm, Cm = jnp.split(xBC, [D_SSM, D_SSM + NGROUPS * D_STATE], axis=-1)
        x = x.reshape(b, l, NHEADS, HEADDIM)
        Bm = Bm.reshape(b, l, NGROUPS, D_STATE)[:, :, 0]
        Cm = Cm.reshape(b, l, NGROUPS, D_STATE)[:, :, 0]
        dt = jax.nn.softplus(dt + dt_bias)
        dA = jnp.exp(dt * A)
        dB = dt[..., None] * Bm[:, :, None, :]

        def step(h, inp):
            dA_t, x_t, dB_t, C_t = inp
            h = h * dA_t[:, :, None, None] + x_t[..., None] * dB_t[:, :, None, :]
            y_t = jnp.einsum('bhpn,bn->bhp', h, C_t)
            return (h, y_t)
        h0 = jnp.zeros((b, NHEADS, HEADDIM, D_STATE), dtype=x.dtype)
        xs = (dA.transpose(1, 0, 2), x.transpose(1, 0, 2, 3), dB.transpose(1, 0, 2, 3), Cm.transpose(1, 0, 2))
        _, ys = jax.lax.scan(step, h0, xs)
        y = ys.transpose(1, 0, 2, 3)
        y = y + D[None, None, :, None] * x
        y = y.reshape(b, l, D_SSM)
        y = norm_w * y * jax.lax.rsqrt(jnp.mean(y * y, axis=-1, keepdims=True) + EPS)
        y = y * jax.nn.silu(z)
        return y @ out_proj_w.T

    def _L0_ffn_ref(x, fast_b, w_fc, w_proj, u, v, gate):
        import jax, jax.numpy as jnp
        import numpy as np

        def _bitlinear(x, w_latent):
            scale = jax.lax.stop_gradient(jnp.clip(jnp.mean(jnp.abs(w_latent), axis=1, keepdims=True), 1e-05, None))
            tern = jnp.clip(jnp.round(w_latent / scale), -1.0, 1.0)
            w = w_latent + jax.lax.stop_gradient(tern - w_latent)
            return x @ (w * scale).T
        h = _bitlinear(x, w_fc) + gate * (x @ v.T @ fast_b.T @ u.T)
        r = jnp.maximum(h, 0.0)
        return _bitlinear(r * r, w_proj)
    x = L0_attn_u
    x = x + _L0_attn_ref(_layernorm(x, axis=-1), L0_attn_in_proj_w, L0_attn_conv_w, L0_attn_conv_b, L0_attn_dt_bias, L0_attn_A_log, L0_attn_D, L0_attn_norm_w, L0_attn_out_proj_w)
    x = x + _L0_ffn_ref(_layernorm(x, axis=-1), L0_ffn_fast_b, L0_ffn_w_fc, L0_ffn_w_proj, L0_ffn_u, L0_ffn_v, L0_ffn_gate)
    return x

_drawn_inputs = setup_inputs


def setup_inputs(seed=0):
    import zlib

    import numpy as np

    out = dict(_drawn_inputs(seed))
    spreads = {'L0_attn_conv_b': (0.0, 0.1), 'L0_attn_D': (1.0, 0.6), 'L0_attn_norm_w': (1.0, 0.6)}
    factors = {'L0_attn_dt_bias': 8.0,
     'L0_attn_A_log': 8.0,
     'L0_ffn_fast_b': 8.0,
     'L0_ffn_u': 8.0,
     'L0_ffn_v': 8.0}
    for name, (base, spread) in spreads.items():
        noise = np.random.default_rng([zlib.crc32(name.encode()), seed]).standard_normal(out[name].shape)
        drawn = base * np.exp(spread * noise) if base else spread * noise
        out[name] = jnp.asarray(drawn.astype(out[name].dtype))
    for name, factor in factors.items():
        out[name] = (out[name] * factor).astype(out[name].dtype)
    return out
```

```python
from contextlib import ExitStack

import numpy as np
import concourse.bass as bass
from concourse import mybir

ALU = mybir.AluOpType
ACT = mybir.ActivationFunctionType
F32 = mybir.dt.float32
F16 = mybir.dt.float16
BF16 = mybir.dt.bfloat16
I32 = mybir.dt.int32
AX_X = mybir.AxisListType.X

P = 128
DM = 256
KD = DM // P
T = 512
NC = T // P
DI = 512
NH, HD = 8, 64
NST = 128
CONV = DI + 2 * NST
NM = CONV // P
TAPS = 4
NPROJ = 2 * DI + 2 * NST + NH
HID = 1024
NJ = HID // P
RANK = 16
EPS = 1e-5
XS = 1024.0
FLOOR = -104.0
ABOVE = -30000.0
HI, LO = 0, 1
PASSES = ((HI, HI), (HI, LO), (LO, HI))
PROJ = (("c", 4), ("c", 5), ("c", 0), ("c", 1), ("z", 0), ("c", 2), ("z", 1), ("c", 3), ("z", 2), ("z", 3))
CONV_ORDER = [m for kind, m in PROJ if kind == "c"]
NDT = 25

NLOAD = 15
POOL_CONST, POOL_ALL = 16, 17
ACT_SUMS, ACT_NORMS, ACT_GROUPS, ACT_ALL = 15, 23, 37, 38
PE_FV, PE_UT, PE_WO, PE_MX, PE_MXB = 1, 9, 18, 21, 22
DVE_UT, DVE_TERN, DVE_WEFF, DVE_MX, DVE_MXD, DVE_P2, DVE_SCALES, DVE_LOW, DVE_ALL = 4, 7, 39, 59, 61, 63, 65, 78, 89


def build(nc, u, in_proj_w, conv_w, conv_b, dt_bias, A_log, D, norm_w, out_proj_w,
          fast_b, w_fc, w_proj, lr_u, lr_v, gate, out):
    S = u.shape[0]
    with ExitStack() as ctx:
        def sb(name, shape, dt=F32):
            return ctx.enter_context(nc.sbuf_tensor(name, shape, dt))

        def sem(name):
            return ctx.enter_context(nc.semaphore(name))

        def bank(name):
            return ctx.enter_context(nc.psum_tensor(name, [P, 512], F32))
        ps_proj = [bank("ps_proj0"), bank("ps_proj1")]
        ps_t = [bank("ps_t0"), bank("ps_t1")]
        ps_d, ps_y, ps_i, ps_f = bank("ps_d"), bank("ps_y"), bank("ps_i"), bank("ps_f")
        def half(b, n):
            return b[:, :].bitcast(F16)[:, 0:n]

        w_in = sb("w_in", [P, 2, KD, NPROJ], F16)
        w_up = sb("w_up", [P, 2, KD, HID], F16)
        w_dn = sb("w_dn", [P, NJ, DM], F16)
        w_o = sb("w_o", [P, 2, DI // P, DM], F16)
        ident = sb("ident", [P, P])
        ident16 = sb("ident16", [P, P], F16)
        identb = sb("identb", [P, P], BF16)
        tri = sb("tri", [P, P])
        ones = sb("ones", [P, P])
        NR = 3 * NC * NH
        pick = sb("pick", [NR, NC * NH, P], BF16)
        above = sb("above", [P, 4, P], BF16)
        cw = sb("cw", [P, NM, TAPS])
        cwu = sb("cwu", [P, NM, TAPS])
        cb = sb("cb", [P, NM])
        dtb = sb("dtb", [P, NH])
        alog = sb("alog", [P, 3, NH])
        aexp = sb("aexp", [P, 3, NH])
        a_neg = sb("a_neg", [P, NH])
        d_bc = sb("d_bc", [P, NH])
        nw = sb("nw", [P, DI // P])
        gate_bc = sb("gate_bc", [P, 1])
        u_in = sb("u_in", [P, 1])
        u_relu = sb("u_relu", [P, 1])
        u_out = sb("u_out", [P, 1])
        g_gate = sb("g_gate", [P, 1])
        dn_bc = sb("dn_bc", [P, DM])
        mhalf = sb("mhalf", [P, NC])
        epsb = sb("epsb", [P, NC])
        xsb = sb("xsb", [P, NC])
        epsd = sb("epsd", [P, 1])
        pause = sb("pause", [P, 1])
        x_sb = sb("x_sb", [P, 2, NC, DM])
        st1 = sb("st1", [P, NC, 6])
        mv1 = sb("mv1", [P, NC, 2])
        va1 = sb("va1", [P, NC])
        rs1 = sb("rs1", [P, NC])
        rs1s = sb("rs1s", [P, NC])
        xn = sb("xn", [P, NC, DM])
        xh = sb("xh", [P, NC, DM], F16)
        xl = sb("xl", [P, NC, DM], F16)
        xnT = sb("xnT", [P, 2, KD, T], F16)
        dtw = sb("dtw", [P, 9, NC, NH])
        dt_ = sb("dt_", [P, 2, NC, NH])
        ecs = sb("ecs", [P, 2, 2, NC, NH])
        ede = sb("ede", [P, 2, NC, NH])
        cp3 = sb("cp3", [P, NC, 3, NH], BF16)
        cT = sb("cT", [NR, 2, P], BF16)
        ncT = sb("ncT", [NR, 2, P], BF16)
        acc = sb("acc", [P, 2, T])
        xc = sb("xc", [P, NM, T])
        sz = sb("sz", [P, NC, DI])
        Bt = sb("Bt", [P, NC, P])
        Gm = sb("Gm", [P, NC, P])
        tok = sb("tok", [P, 6, DI])
        Xdt, XD, Xst = tok[:, 0:2], tok[:, 2:4], tok[:, 4:6]
        Lb = sb("Lb", [P, 2, 512])
        Mb = sb("Mb", [P, 4, 4, P])
        hst = sb("hst", [P, 2, DI])
        hd = sb("hd", [P, DI])
        ti = sb("ti", [P, DI])
        ti2 = sb("ti2", [P, DI])
        yb = sb("yb", [P, 2, DI])
        ysq = sb("ysq", [P, DI])
        ssq = sb("ssq", [P, NC])
        rv = sb("rv", [P, 3, NC])
        yg = sb("yg", [P, 2, DI])
        ygh = sb("ygh", [P, 2, DI], F16)
        ygl = sb("ygl", [P, 2, DI], F16)
        ygT = sb("ygT", [P, 2, 2, DI // P, P], F16)
        x2 = sb("x2", [P, 2, NC, DM])
        st2 = sb("st2", [P, NC, 6])
        mv2 = sb("mv2", [P, NC, 2])
        rv2 = sb("rv2", [P, 3, NC])
        xn2 = sb("xn2", [P, 2, DM])
        x2h = sb("x2h", [P, 2, DM], F16)
        x2l = sb("x2l", [P, 2, DM], F16)
        xn2T = sb("xn2T", [P, 2, 2, KD, T], F16)
        r = sb("r", [P, 2, T])
        r2 = sb("r2", [P, 2, T])
        rT = sb("rT", [P, 2, NJ, T], F16)
        ot = sb("ot", [P, 2, DM])
        ob = sb("ob", [P, 2, DM])
        NT = NPROJ // P
        raw_in = tok[:, :, :].rearrange("p a b -> p (a b)")[:, 0:(NT + 1) * DM].rearrange("p (j n) -> p j n", n=DM)
        raw_out = Lb
        wo32 = Mb[:, 0:2, :, :].rearrange("p a b c -> p (a b c)").rearrange("p (m n) -> p m n", m=DI // P)
        raw_fc = sz[:, :, :].rearrange("p a b -> p (a b)").rearrange("p (j n) -> p j n", j=NJ)
        raw_dn = rT[:, 0, :, :].rearrange("p a b -> p (a b)").bitcast(F32).rearrange("p (j n) -> p j n", j=KD)
        weff = rT[:, 1, :, :].rearrange("p a b -> p (a b)").bitcast(F32).rearrange("p (j n) -> p j n", j=NJ)
        tern_a = xc[:, 0:4, :].rearrange("p a b -> p (a b)").rearrange("p (j n) -> p j n", j=NJ)
        raw_u = sb("raw_u", [P, NJ, RANK])
        raw_v = sb("raw_v", [RANK, DM])
        fbT = sb("fbT", [RANK, RANK])
        fv = sb("fv", [RANK, DM])
        uT = hst[0:RANK].rearrange("p a b -> p (a b)").rearrange("p (j n) -> p j n", j=NJ)
        NS = 5
        mx = sb("mx", [P, 8, 16])
        mxa = sb("mxa", [P, NS])
        mxT = sb("mxT", [NS, P])
        mxm = sb("mxm", [NS, 1])
        mxd = sb("mxd", [NS, NS])
        mxb = sb("mxb", [P, NS])
        p2 = sb("p2", [P, NS])
        ip2 = sb("ip2", [P, NS])
        rp = sb("rp", [P, NS])
        sw = sb("sw", [P, NS])
        fcs = sb("fcs", [P, 4, NJ])
        dns = sb("dns", [P, 6, KD])
        junk = r[:, :, :].rearrange("p a b -> p (a b)")
        tern_b = r2[:, :, :].rearrange("p a b -> p (a b)")
        dnd = sb("dnd", [P, KD, P])

        w_loaded, zeroed = sem("w_loaded"), sem("zeroed")
        x_loaded = [sem("x_loaded_even"), sem("x_loaded_odd")]
        stored = [sem("stored_even"), sem("stored_odd")]
        prep_pool, prep_act, prep_dve, prep_pe = sem("prep_pool"), sem("prep_act"), sem("prep_dve"), sem("prep_pe")
        st1_done, mv1_done, rs1_step, xn_done = sem("st1_done"), sem("mv1_done"), sem("rs1_step"), sem("xn_done")
        xh_done, xl_done = sem("xh_done"), sem("xl_done")
        xT_ready, xhT_copied, xlT_copied = sem("xT_ready"), sem("xhT_copied"), sem("xlT_copied")
        dt_mm, dt_mm2, dt_step, dt_exp = sem("dt_mm"), sem("dt_mm2"), sem("dt_step"), sem("dt_exp")
        proj_done, acc_init, conv_step, xc_done, z_done = (
            sem("proj_done"), sem("acc_init"), sem("conv_step"), sem("xc_done"), sem("z_done"))
        bt_mm, bt_copied, g_mm, g_done = sem("bt_mm"), sem("bt_copied"), sem("g_mm"), sem("g_done")
        d_mm, l_done, m_done = sem("d_mm"), sem("l_done"), sem("m_done")
        xt_mm, xdt_done, xst_done = sem("xt_mm"), sem("xdt_done"), sem("xst_done")
        intra_mm, inter_mm, state_mm = sem("intra_mm"), sem("inter_mm"), sem("state_mm")
        ti_done, ti2_done, h_done, hd_done = sem("ti_done"), sem("ti2_done"), sem("h_done"), sem("hd_done")
        y_done, ssq_done, rv_step, yg_done, ygh_done, ygl_done = (
            sem("y_done"), sem("ssq_done"), sem("rv_step"), sem("yg_done"), sem("ygh_done"), sem("ygl_done"))
        yT_mm, yT_copied, o_mm, x2_done = sem("yT_mm"), sem("yT_copied"), sem("o_mm"), sem("x2_done")
        st2_done, mv2_done, rv2_step, xn2_done = sem("st2_done"), sem("mv2_done"), sem("rv2_step"), sem("xn2_done")
        x2h_done, x2l_done, x2T_mm, x2T_copied = sem("x2h_done"), sem("x2l_done"), sem("x2T_mm"), sem("x2T_copied")
        up_mm, r_done, r2_done, rh_done, rl_done = (
            sem("up_mm"), sem("r_done"), sem("r2_done"), sem("rh_done"), sem("rl_done"))
        dn_mm, ot_done, ob_done = sem("dn_mm"), sem("ot_done"), sem("ob_done")

        xs = u.rearrange("s (c p) d -> s p c d", p=P)
        outs = out.rearrange("s (c p) d -> s c p d", p=P)

        groups = []
        for k in range(KD):
            for m0, m1 in ((0, 4), (4, 8), (8, NT + 1)):
                src = [raw_in[0:(P if m < NT else NPROJ - NT * P), m, k * P:(k + 1) * P] for m in range(m0, m1)]
                e = min(m1 * P, NPROJ)
                groups.append((src, e - m0 * P, w_in[:, HI, k, m0 * P:e], w_in[:, LO, k, m0 * P:e], 0))
        for k in range(KD):
            for j in range(0, NJ, 4):
                src = [weff[:, j + a, k * P:(k + 1) * P] for a in range(4)]
                groups.append((src, 4 * P, w_up[:, HI, k, j * P:(j + 4) * P], w_up[:, LO, k, j * P:(j + 4) * P], 3))
        for j in range(0, NJ, 2):
            src = [raw_dn[:, k, (j + a) * P:(j + a + 1) * P] for a in range(2) for k in range(KD)]
            groups.append((src, 4 * P, w_dn[:, j:j + 2, :].rearrange("p a b -> p (a b)"), None, None))
        prep_banks = ps_proj + ps_t
        NB = len(prep_banks)

        block = ctx.enter_context(nc.Block())

        def at(s, n, k):
            return s * n + (k + 1)

        @block.sync
        def _(sp):
            def load_x(s, q):
                sp.dma_start(x_sb[:, q], xs[s]).then_inc(x_loaded[q], 16)

            def store(s, c):
                sp.wait_ge(ob_done, at(s, NC, c))
                sp.dma_start(outs[s, c], ob[:, c % 2]).then_inc(stored[c % 2], 16)

            sp.wait_ge(zeroed, 1)
            with nc.allow_non_contiguous_dma(reason="small weights, once"):
                for dst, src in (
                    (raw_fc, w_fc.rearrange("(j p) n -> p j n", p=P)),
                    (raw_u[:, :, :], lr_u.rearrange("(j p) n -> p j n", p=P)),
                    (raw_v[:, :], lr_v),
                    (fbT[:, :], fast_b.rearrange("a b -> b a")),
                    (gate_bc[:, :], gate.rearrange("(a b) -> a b", a=1).to_broadcast([P, 1])),
                    (raw_in[:, 0:NT, :], in_proj_w[0:NT * P, :].rearrange("(j p) n -> p j n", p=P)),
                    (raw_in[0:NPROJ - NT * P, NT, :], in_proj_w[NT * P:NPROJ, :]),
                    (raw_out[:, :, :], out_proj_w.rearrange("(j p) n -> p j n", p=P)),
                    (raw_dn, w_proj.rearrange("(j p) n -> p j n", p=P)),
                    (nw[:, :], norm_w.rearrange("(j p) -> p j", p=P)),
                    (cw[:, :, :], conv_w.rearrange("(j p) o t -> p j (o t)", p=P)),
                    (cb[:, :], conv_b.rearrange("(j p) -> p j", p=P)),
                    (dtb[:, :], dt_bias.rearrange("(a b) -> a b", a=1).to_broadcast([P, NH])),
                    (alog[:, :, :].rearrange("p a b -> p (a b)"),
                     A_log.rearrange("a b -> (a b)").rearrange("(a b) -> a b", a=1).to_broadcast([P, 3 * NH])),
                    (d_bc[:, :], D.rearrange("(a b) -> a b", a=1).to_broadcast([P, NH])),
                ):
                    sp.dma_start(dst, src).then_inc(w_loaded, 16)
            load_x(0, 0)
            load_x(1, 1)
            with sp.Fori(0, S // 2 - 1) as i:
                for q in range(2):
                    s = i * 2 + q
                    sp.wait_ge(x2_done, at(s, NC, NC - 1))
                    load_x(s + 2, q)
                    for c in range(NC):
                        store(s, c)
            for s in range(S - 2, S):
                for c in range(NC):
                    store(s, c)
            for done in stored:
                sp.wait_ge(done, S * NC // 2 * 16)

        @block.gpsimd
        def _(pool):
            n = [0]

            def step(ins):
                n[0] += 1
                ins.then_inc(prep_pool, 1)
                pool.wait_ge(prep_pool, n[0])

            nc.gpsimd.memset(raw_in[:, NT, :], 0.0).then_inc(zeroed, 1)
            step(nc.gpsimd.memset(mhalf[:, :], -0.5))
            step(nc.gpsimd.memset(epsb[:, :], EPS))
            step(nc.gpsimd.memset(xsb[:, :], XS))
            step(nc.gpsimd.memset(epsd[:, :], EPS * DI))
            step(nc.gpsimd.memset(ones[:, :], 1.0))
            step(nc.gpsimd.memset(ident[:, :], 0.0))
            step(nc.gpsimd.affine_select(out=ident[:, :], in_=ident[:, :], compare_op=ALU.not_equal, fill=1.0,
                                         base=0, pattern=[[-1, P]], channel_multiplier=1))
            step(nc.gpsimd.affine_select(out=tri[:, :], in_=ones[:, :], compare_op=ALU.is_ge, fill=0.0,
                                         base=0, pattern=[[1, P]], channel_multiplier=-1))
            step(nc.gpsimd.tensor_copy(ident16[:, :], ident[:, :]))
            step(nc.gpsimd.tensor_copy(identb[:, :], ident[:, :]))
            step(nc.gpsimd.memset(above[:, :, :], 0.0))
            step(nc.gpsimd.affine_select(out=above[:, :, :], in_=above[:, :, :], compare_op=ALU.is_ge, fill=ABOVE,
                                         base=0, pattern=[[0, 4], [1, P]], channel_multiplier=-1))
            step(nc.gpsimd.memset(pick[:, :, :], 0.0))
            pk = pick[:, :, :].rearrange("k (c h) p -> k c h p", c=NC)
            for part in range(3):
                step(nc.gpsimd.affine_select(out=pk, in_=pk, compare_op=ALU.not_equal, fill=1.0,
                                             base=-part * NH, pattern=[[-3 * NH, NC], [-1, NH], [0, P]],
                                             channel_multiplier=1))
            pool.wait_ge(prep_dve, DVE_P2)
            step(nc.gpsimd.tensor_tensor(rp[:, :], p2[:, :], mhalf[:, 0:1].to_broadcast([P, NS]), ALU.pow))

            def input_stats(s):
                pool.wait_ge(mv1_done, at(s, NC, NC - 1))
                nc.gpsimd.tensor_tensor(va1[:, :], mv1[:, :, 1], epsb[:, :], ALU.add).then_inc(rs1_step, 1)
                pool.wait_ge(rs1_step, at(s, 3, 0))
                nc.gpsimd.tensor_tensor(rs1[:, :], va1[:, :], mhalf[:, :], ALU.pow).then_inc(rs1_step, 1)
                pool.wait_ge(rs1_step, at(s, 3, 1))
                nc.gpsimd.tensor_tensor(rs1s[:, :], rs1[:, :], xsb[:, :], ALU.mult).then_inc(rs1_step, 1)

            def input_low(s):
                pool.wait_ge(xh_done, at(s, 1, 0))
                nc.gpsimd.tensor_tensor(xl[:, :, :], xn[:, :, :], xh[:, :, :], ALU.subtract).then_inc(xl_done, 1)

            def x_state(s, q, c):
                if c == 0:
                    pool.wait_ge(dt_exp, at(s, 3, 2))
                pool.wait_ge(xdt_done, at(s, 2 * NC, 2 * c))
                nc.gpsimd.tensor_tensor(
                    Xst[:, c % 2].rearrange("p (h d) -> p h d", h=NH), Xdt[:, c % 2].rearrange("p (h d) -> p h d", h=NH),
                    ede[:, q, c].unsqueeze(2).to_broadcast([P, NH, HD]), ALU.mult).then_inc(xst_done, 1)

            def decay_state(s, q, c):
                pool.wait_ge(h_done, at(s, NC - 1, c - 1))
                nc.gpsimd.tensor_tensor(
                    hd[:, :].rearrange("p (h d) -> p h d", h=NH), hst[:, (c - 1) % 2].rearrange("p (h d) -> p h d", h=NH),
                    ecs[:, q, 1, c].unsqueeze(2).to_broadcast([P, NH, HD]), ALU.mult).then_inc(hd_done, 1)

            def add_skip(s, c):
                pool.wait_ge(ti_done, at(s, NC - 1, c - 1))
                pool.wait_ge(xdt_done, at(s, 2 * NC, 2 * c + 1))
                nc.gpsimd.tensor_tensor(ti2[:, :], ti[:, :], XD[:, c % 2], ALU.add).then_inc(ti2_done, 1)

            def rms(s, c):
                pool.wait_ge(ssq_done, at(s, NC, c))
                nc.gpsimd.tensor_tensor(rv[:, 0, c:c + 1], ssq[:, c:c + 1], epsd[:, :], ALU.add).then_inc(rv_step, 1)
                pool.wait_ge(rv_step, at(s, 3 * NC, 3 * c))
                nc.gpsimd.tensor_tensor(rv[:, 1, c:c + 1], rv[:, 0, c:c + 1], mhalf[:, 0:1], ALU.pow).then_inc(rv_step, 1)
                pool.wait_ge(rv_step, at(s, 3 * NC, 3 * c + 1))
                nc.gpsimd.tensor_tensor(rv[:, 2, c:c + 1], rv[:, 1, c:c + 1], g_gate[:, :], ALU.mult).then_inc(rv_step, 1)

            def gate_low(s, c):
                pool.wait_ge(ygh_done, at(s, NC, c))
                nc.gpsimd.tensor_tensor(ygl[:, c % 2], yg[:, c % 2], ygh[:, c % 2], ALU.subtract).then_inc(ygl_done, 1)

            def stats2(s, c):
                pool.wait_ge(mv2_done, at(s, NC, c))
                nc.gpsimd.tensor_tensor(rv2[:, 0, c:c + 1], mv2[:, c, 1:2], epsb[:, 0:1], ALU.add).then_inc(rv2_step, 1)
                pool.wait_ge(rv2_step, at(s, 3 * NC, 3 * c))
                nc.gpsimd.tensor_tensor(rv2[:, 1, c:c + 1], rv2[:, 0, c:c + 1], mhalf[:, 0:1], ALU.pow).then_inc(rv2_step, 1)
                pool.wait_ge(rv2_step, at(s, 3 * NC, 3 * c + 1))
                nc.gpsimd.tensor_tensor(rv2[:, 2, c:c + 1], rv2[:, 1, c:c + 1], xsb[:, 0:1], ALU.mult).then_inc(rv2_step, 1)

            def low2(s, c):
                pool.wait_ge(x2h_done, at(s, NC, c))
                nc.gpsimd.tensor_tensor(x2l[:, c % 2], xn2[:, c % 2], x2h[:, c % 2], ALU.subtract).then_inc(x2l_done, 1)

            def relu_low(s, j):
                pool.wait_ge(rh_done, at(s, NJ, j))
                nc.gpsimd.tensor_tensor(rT[:, LO, j], r2[:, j % 2], rT[:, HI, j], ALU.subtract).then_inc(rl_done, 1)

            def result(s, q, c):
                pool.wait_ge(ot_done, at(s, NC, c))
                if c >= 2:
                    pool.wait_ge(stored[c % 2], (s * (NC // 2) + c // 2) * 16)
                nc.gpsimd.tensor_tensor(ob[:, c % 2], ot[:, c % 2], x2[:, q, c], ALU.add).then_inc(ob_done, 1)

            def results_stored(s):
                for done in stored:
                    pool.wait_ge(done, (s + 1) * (NC // 2) * 16)

            def round_(s, q, ffn=True, nxt=True):
                if ffn:
                    stats2(s - 1, 3)
                    low2(s - 1, 3)
                    relu_low(s - 1, 0)
                    relu_low(s - 1, 1)
                if nxt:
                    input_stats(s + 1)
                if ffn:
                    relu_low(s - 1, 2)
                    relu_low(s - 1, 3)
                if nxt:
                    input_low(s + 1)
                if ffn:
                    relu_low(s - 1, 4)
                    relu_low(s - 1, 5)
                x_state(s, q, 0)
                if ffn:
                    relu_low(s - 1, 6)
                    relu_low(s - 1, 7)
                for c in range(NC):
                    if c:
                        add_skip(s, c)
                    if c == 1 or c == 2:
                        decay_state(s, q, c)
                    if c < NC - 2:
                        x_state(s, q, c + 1)
                    rms(s, c)
                    if c:
                        stats2(s, c - 1)
                        low2(s, c - 1)
                    if ffn:
                        result(s - 1, 1 - q, c)
                    gate_low(s, c)
                if ffn:
                    results_stored(s - 1)

            def finish(s, q):
                stats2(s, 3)
                low2(s, 3)
                for j in range(NJ):
                    relu_low(s, j)
                for c in range(NC):
                    result(s, q, c)

            input_stats(0)
            input_low(0)
            round_(0, 0, ffn=False)
            with pool.Fori(0, S // 2 - 1) as i:
                round_(i * 2 + 1, 1)
                round_(i * 2 + 2, 0)
            round_(S - 1, 1, nxt=False)
            finish(S - 1, 1)

        @block.scalar
        def _(act):
            n = [0]

            def step(ins):
                n[0] += 1
                ins.then_inc(prep_act, 1)

            act.wait_ge(w_loaded, 16 * NLOAD)
            for j in range(NJ):
                step(nc.scalar.activation(junk[:, 0:DM], raw_fc[:, j], ACT.Abs, accum_out=fcs[:, 0, j:j + 1]))
                act.wait_ge(prep_act, n[0])
            for j in range(KD):
                step(nc.scalar.activation(junk[:, 0:HID], raw_dn[:, j], ACT.Abs, accum_out=dns[:, 0, j:j + 1]))
                act.wait_ge(prep_act, n[0])
            for j in range(DI // P):
                step(nc.scalar.activation(junk[:, 0:DM], raw_in[:, j], ACT.Square, accum_out=mx[:, 1, j:j + 1]))
                act.wait_ge(prep_act, n[0])
            step(nc.scalar.activation(aexp[:, :, :].rearrange("p a b -> p (a b)"),
                                      alog[:, :, :].rearrange("p a b -> p (a b)"), ACT.Exp))
            assert n[0] == ACT_SUMS
            act.wait_ge(prep_dve, DVE_WEFF)
            for j in range(NJ):
                act.wait_ge(prep_act, n[0])
                step(nc.scalar.activation(junk[:, 0:DM], weff[:, j], ACT.Square, accum_out=mx[:, 4, j:j + 1]))
            assert n[0] == ACT_NORMS
            act.wait_ge(prep_dve, DVE_SCALES)
            for g, (_, w, high, _, sc) in enumerate(groups):
                act.wait_ge(prep_pe, PE_MXB + g + 1)
                if sc is None:
                    step(nc.scalar.activation(high, prep_banks[g % NB][:, 0:w], ACT.Copy))
                else:
                    step(nc.scalar.activation(high, prep_banks[g % NB][:, 0:w], ACT.Copy, scale=sw[:, sc:sc + 1]))
            assert n[0] == ACT_GROUPS
            step(nc.scalar.activation(w_o[:, HI, :, :].rearrange("p a b -> p (a b)"),
                                      wo32.rearrange("p a b -> p (a b)"), ACT.Copy, scale=sw[:, 2:3]))
            assert n[0] == ACT_ALL

            def input_high(s):
                act.wait_ge(xn_done, at(s, NC, NC - 1))
                nc.scalar.activation(xh[:, :, :].rearrange("p a b -> p (a b)"),
                                     xn[:, :, :].rearrange("p a b -> p (a b)"), ACT.Copy).then_inc(xh_done, 1)

            def input_copy(s):
                act.wait_ge(xT_ready, at(s, 2, HI))
                nc.scalar.activation(xnT[:, HI].rearrange("p a b -> p (a b)"), half(ps_t[1], KD * T),
                                     ACT.Copy).then_inc(xhT_copied, 1)

            def dt_exp_abs(s):
                act.wait_ge(dt_step, at(s, NDT, 1))
                nc.scalar.activation(dtw[:, 2], dtw[:, 1], ACT.Exp, scale=-1.0).then_inc(dt_exp, 1)

            def decays(s, q):
                act.wait_ge(dt_step, at(s, NDT, 18))
                nc.scalar.activation(ecs[:, q], ps_t[1][:, 0:2 * NC * NH].rearrange("p (a c h) -> p a c h", a=2, c=NC),
                                     ACT.Exp).then_inc(dt_exp, 1)
                nc.scalar.activation(ede[:, q], dtw[:, 6], ACT.Exp).then_inc(dt_exp, 1)

            def conv_init(s, k):
                m = CONV_ORDER[k]
                act.wait_ge(proj_done, at(s, len(PROJ), PROJ.index(("c", m))))
                if k >= 2:
                    act.wait_ge(xc_done, at(s, NM, k - 2))
                nc.scalar.activation(acc[:, k % 2], ps_proj[PROJ.index(("c", m)) % 2][:, :], ACT.Identity,
                                     scale=cwu[:, m, 3:4], bias=cb[:, m:m + 1]).then_inc(acc_init, 1)

            def conv_silu(s, k):
                act.wait_ge(conv_step, at(s, 3 * NM, 3 * k + 2))
                nc.scalar.activation(xc[:, CONV_ORDER[k]], acc[:, k % 2], ACT.Silu).then_inc(xc_done, 1)

            def gate_silu(s, c):
                act.wait_ge(proj_done, at(s, len(PROJ), PROJ.index(("z", c))))
                nc.scalar.activation(sz[:, c], ps_proj[PROJ.index(("z", c)) % 2][:, :], ACT.Silu,
                                     scale=u_in[:, :]).then_inc(z_done, 1)

            def b_copy(s):
                act.wait_ge(bt_mm, at(s, 1, 0))
                nc.scalar.activation(Bt[:, :, :].rearrange("p a b -> p (a b)"), ps_t[0][:, :], ACT.Copy).then_inc(bt_copied, 1)

            def decay_matrix(s, c, g):
                act.wait_ge(d_mm, at(s, 2 * NC, 2 * c + g))
                if c or g:
                    k = 2 * c + g
                    if k >= 2:
                        act.wait_ge(m_done, at(s, 2 * NC, k - 2))
                nc.scalar.activation(Lb[:, g], ps_d[:, :], ACT.Exp).then_inc(l_done, 1)

            def state_copy(s):
                act.wait_ge(state_mm, at(s, NC - 1, 0))
                nc.scalar.activation(hst[:, 0], ps_i[:, :], ACT.Copy).then_inc(h_done, 1)

            def square(s, c):
                act.wait_ge(y_done, at(s, NC, c))
                nc.scalar.activation(ysq[:, :], yb[:, c % 2], ACT.Square, accum_out=ssq[:, c:c + 1]).then_inc(ssq_done, 1)

            def gate_high(s, c):
                act.wait_ge(yg_done, at(s, NC, c))
                nc.scalar.activation(ygh[:, c % 2], yg[:, c % 2], ACT.Copy).then_inc(ygh_done, 1)

            def high2(s, c):
                act.wait_ge(xn2_done, at(s, NC, c))
                nc.scalar.activation(x2h[:, c % 2], xn2[:, c % 2], ACT.Copy).then_inc(x2h_done, 1)

            def copy2(s, q, c):
                act.wait_ge(x2T_mm, at(s, NC, c))
                nc.scalar.activation(xn2T[:, q, :, :, c * P:(c + 1) * P],
                                     half(ps_t[1], 2 * KD * P).rearrange("p (a b t) -> p a b t", a=2, b=KD),
                                     ACT.Copy).then_inc(x2T_copied, 1)

            def relu(s, j):
                act.wait_ge(up_mm, at(s, NJ, j))
                nc.scalar.activation(r[:, j % 2], ps_f[:, :], ACT.Relu, scale=u_relu[:, :]).then_inc(r_done, 1)

            def relu_high(s, j):
                act.wait_ge(r2_done, at(s, NJ, j))
                nc.scalar.activation(rT[:, HI, j], r2[:, j % 2], ACT.Copy).then_inc(rh_done, 1)

            def round_(s, q, ffn=True, nxt=True):
                conv_init(s, 0)
                if ffn:
                    copy2(s - 1, 1 - q, 2)
                conv_init(s, 1)
                conv_silu(s, 0)
                conv_init(s, 2)
                conv_silu(s, 1)
                if ffn:
                    high2(s - 1, 3)
                conv_init(s, 3)
                conv_silu(s, 2)
                gate_silu(s, 0)
                conv_silu(s, 3)
                conv_init(s, 4)
                if ffn:
                    copy2(s - 1, 1 - q, 3)
                    relu(s - 1, 0)
                gate_silu(s, 1)
                if ffn:
                    relu_high(s - 1, 0)
                    relu(s - 1, 1)
                conv_silu(s, 4)
                conv_init(s, 5)
                if ffn:
                    relu_high(s - 1, 1)
                    relu(s - 1, 2)
                gate_silu(s, 2)
                if ffn:
                    relu_high(s - 1, 2)
                conv_silu(s, 5)
                gate_silu(s, 3)
                if ffn:
                    relu(s - 1, 3)
                b_copy(s)
                if ffn:
                    relu_high(s - 1, 3)
                    relu(s - 1, 4)
                decay_matrix(s, 0, 0)
                if ffn:
                    relu_high(s - 1, 4)
                    relu(s - 1, 5)
                decay_matrix(s, 0, 1)
                if nxt:
                    input_high(s + 1)
                if ffn:
                    relu_high(s - 1, 5)
                    relu(s - 1, 6)
                for c in range(NC):
                    if c == 1 and nxt:
                        input_copy(s + 1)
                    if c == 3 and nxt:
                        decays(s + 1, 1 - q)
                    if c < NC - 1:
                        decay_matrix(s, c + 1, 0)
                    if c == 0 and ffn:
                        relu_high(s - 1, 6)
                        relu(s - 1, 7)
                    if c < NC - 1:
                        decay_matrix(s, c + 1, 1)
                    if c == 0 and ffn:
                        relu_high(s - 1, 7)
                    if c == 0:
                        state_copy(s)
                    square(s, c)
                    if c:
                        high2(s, c - 1)
                    if c > 1:
                        copy2(s, q, c - 2)
                    if c == 2 and nxt:
                        dt_exp_abs(s + 1)
                    gate_high(s, c)

            def finish(s, q):
                copy2(s, q, 2)
                high2(s, 3)
                copy2(s, q, 3)
                for j in range(NJ):
                    relu(s, j)
                    relu_high(s, j)

            act.wait_ge(prep_dve, DVE_ALL)
            input_high(0)
            input_copy(0)
            dt_exp_abs(0)
            decays(0, 0)
            round_(0, 0, ffn=False)
            with act.Fori(0, S // 2 - 1) as i:
                round_(i * 2 + 1, 1)
                round_(i * 2 + 2, 0)
            round_(S - 1, 1, nxt=False)
            finish(S - 1, 1)

        @block.vector
        def _(dve):
            n = [0]

            def step(ins):
                n[0] += 1
                ins.then_inc(prep_dve, 1)
                dve.wait_ge(prep_dve, n[0])

            V = nc.vector
            dve.wait_ge(w_loaded, 16 * NLOAD)
            dve.wait_ge(prep_pool, POOL_CONST)
            step(V.tensor_reduce(mx[:, 0, 0:1], raw_in[:, :, :].rearrange("p a b -> p (a b)"), AX_X, ALU.max,
                                 apply_absolute_value=True))
            dve.wait_ge(prep_pe, PE_FV)
            step(V.tensor_copy(fv[:, :], ps_f[0:RANK, 0:DM]))
            dve.wait_ge(prep_pe, PE_UT)
            step(V.tensor_copy(uT[:, 0:4, :].rearrange("p a b -> p (a b)"), ps_y[0:RANK, :]))
            step(V.tensor_copy(uT[:, 4:8, :].rearrange("p a b -> p (a b)"), ps_i[0:RANK, :]))
            assert n[0] == DVE_UT
            dve.wait_ge(prep_act, ACT_SUMS)
            step(V.tensor_scalar(fcs[:, 1, :], fcs[:, 0, :], 1.0 / DM, 1e-5, ALU.mult, ALU.max))
            step(V.tensor_scalar(fcs[:, 2, :], fcs[:, 1, :], 0.5, None, ALU.mult))
            step(V.tensor_scalar(fcs[:, 3, :], fcs[:, 1, :], -0.5, None, ALU.mult))
            for j in range(NJ):
                step(V.tensor_scalar(tern_a[:, j], raw_fc[:, j], fcs[:, 2, j:j + 1], fcs[:, 1, j:j + 1], ALU.is_gt, ALU.mult))
                step(V.tensor_scalar(tern_b[:, 0:DM], raw_fc[:, j], fcs[:, 3, j:j + 1], fcs[:, 1, j:j + 1], ALU.is_lt, ALU.mult))
                step(V.tensor_tensor(tern_a[:, j], tern_a[:, j], tern_b[:, 0:DM], ALU.subtract))
                dve.wait_ge(prep_pe, PE_UT + j + 1)
                step(V.scalar_tensor_tensor(weff[:, j], ps_proj[j % 2][:, 0:DM], gate_bc[:, :], tern_a[:, j], ALU.mult, ALU.add))
            assert n[0] == DVE_WEFF, n[0]
            step(V.tensor_reduce(mx[:, 3, 0:1], weff.rearrange("p a b -> p (a b)"), AX_X, ALU.max, apply_absolute_value=True))
            step(V.tensor_scalar(dns[:, 1, :], dns[:, 0, :], 1.0 / HID, 1e-5, ALU.mult, ALU.max))
            step(V.tensor_scalar(dns[:, 2, :], dns[:, 1, :], 0.5, None, ALU.mult))
            step(V.tensor_scalar(dns[:, 3, :], dns[:, 1, :], -0.5, None, ALU.mult))
            for j in range(KD):
                step(V.tensor_scalar(tern_b[:, 0:HID], raw_dn[:, j], dns[:, 3, j:j + 1], None, ALU.is_lt))
                step(V.scalar_tensor_tensor(raw_dn[:, j], raw_dn[:, j], dns[:, 2, j:j + 1], tern_b[:, 0:HID], ALU.is_gt, ALU.subtract))
                step(V.tensor_scalar(dnd[:, j], ident[:, :], dns[:, 1, j:j + 1], None, ALU.mult))
            for g in range(2):
                dve.wait_ge(prep_pe, PE_WO + g)
                for k in range(2):
                    m = 2 * g + k
                    step(V.tensor_scalar(wo32[:, m], [ps_y, ps_i][g][:, k * DM:(k + 1) * DM], nw[:, m:m + 1], None, ALU.mult))
            step(V.tensor_reduce(mx[:, 2, 0:1], wo32.rearrange("p a b -> p (a b)"), AX_X, ALU.max, apply_absolute_value=True))
            dve.wait_ge(prep_act, ACT_NORMS)
            for k in (0, 2, 3):
                step(V.tensor_copy(mxa[:, k:k + 1], mx[:, k, 0:1]))
            step(V.tensor_reduce(mxa[:, 1:2], mx[:, 1, 0:DI // P], AX_X, ALU.max))
            step(V.tensor_reduce(mxa[:, 4:5], mx[:, 4, 0:NJ], AX_X, ALU.max))
            assert n[0] == DVE_MX, n[0]
            dve.wait_ge(prep_pe, PE_MX)
            step(V.tensor_reduce(mxm[:, :], ps_d[0:NS, 0:P], AX_X, ALU.max))
            step(V.tensor_scalar(mxd[:, :], ident[0:NS, 0:NS], mxm[:, :], None, ALU.mult))
            assert n[0] == DVE_MXD, n[0]
            dve.wait_ge(prep_pe, PE_MXB)
            step(V.tensor_scalar(mxb[:, :], ps_d[:, 0:NS], 1e-30, None, ALU.max))
            step(V.tensor_scalar(p2[:, :].bitcast(I32), mxb[:, :].bitcast(I32), 0x7F800000, None, ALU.bitwise_and))
            assert n[0] == DVE_P2, n[0]
            step(V.reciprocal(ip2[:, :], p2[:, :]))
            step(V.tensor_scalar(sw[:, :], ip2[:, :], 8192.0, None, ALU.mult))
            assert n[0] == DVE_SCALES, n[0]
            step(V.tensor_scalar(u_in[:, :], p2[:, 0:1], 1.0 / 8192 / XS, None, ALU.mult))
            dve.wait_ge(prep_pool, POOL_ALL)
            step(V.tensor_scalar(g_gate[:, :], rp[:, 1:2], 64.0 * DI ** 0.5, None, ALU.mult))
            step(V.tensor_scalar(mx[:, 5, 0:1], g_gate[:, :], sw[:, 2:3], DI ** -0.5, ALU.mult, ALU.mult))
            step(V.reciprocal(u_out[:, :], mx[:, 5, 0:1]))
            step(V.tensor_scalar(mx[:, 5, 1:2], rp[:, 4:5], 8.0, None, ALU.mult))
            step(V.tensor_scalar(u_relu[:, :], p2[:, 3:4], 1.0 / 8192 / XS, mx[:, 5, 1:2], ALU.mult, ALU.mult))
            step(V.tensor_scalar(mx[:, 5, 2:3], mx[:, 5, 1:2], mx[:, 5, 1:2], None, ALU.mult))
            step(V.reciprocal(mx[:, 5, 3:4], mx[:, 5, 2:3]))
            step(V.tensor_scalar(dn_bc[:, :], ps_f[:, 0:DM], mx[:, 5, 3:4], None, ALU.mult))
            step(V.tensor_tensor(a_neg[:, :], aexp[:, 0, :], aexp[:, 1, :], ALU.add))
            step(V.tensor_tensor(a_neg[:, :], a_neg[:, :], aexp[:, 2, :], ALU.add))
            step(V.tensor_scalar(a_neg[:, :], a_neg[:, :], -1.0 / 3, None, ALU.mult))
            step(V.tensor_scalar(cwu[:, :, :].rearrange("p a b -> p (a b)"), cw[:, :, :].rearrange("p a b -> p (a b)"),
                                 u_in[:, :], None, ALU.mult))
            assert n[0] == DVE_LOW, n[0]
            for g, (_, w, high, low, sc) in enumerate(groups):
                if sc is not None:
                    dve.wait_ge(prep_act, ACT_NORMS + g + 1)
                    step(V.scalar_tensor_tensor(low, prep_banks[g % NB][:, 0:w], sw[:, sc:sc + 1], high,
                                                ALU.mult, ALU.subtract))
            dve.wait_ge(prep_act, ACT_ALL)
            step(V.scalar_tensor_tensor(w_o[:, LO, :, :].rearrange("p a b -> p (a b)"),
                                        wo32.rearrange("p a b -> p (a b)"), sw[:, 2:3],
                                        w_o[:, HI, :, :].rearrange("p a b -> p (a b)"), ALU.mult, ALU.subtract))
            assert n[0] == DVE_ALL, n[0]

            def input_stats(s, q):
                dve.wait_ge(x_loaded[q], s * 8 + (8 if q else 16))
                for c in range(NC):
                    V.bn_stats(st1[:, c], x_sb[:, q, c]).then_inc(st1_done, 1)
                dve.wait_ge(st1_done, at(s, NC, NC - 1))
                V.memset(pause[:, :], 0.0)
                for c in range(NC):
                    V.bn_aggr(mv1[:, c], st1[:, c]).then_inc(mv1_done, 1)

            def input_norm(s, q):
                dve.wait_ge(rs1_step, at(s, 3, 2))
                if type(s) is not int or s:
                    dve.wait_ge(xl_done, at(s - 1, 1, 0))
                for c in range(NC):
                    V.tensor_scalar(xn[:, c], x_sb[:, q, c], mv1[:, c, 0:1], rs1s[:, c:c + 1],
                                    ALU.subtract, ALU.mult).then_inc(xn_done, 1)

            def input_copy(s):
                dve.wait_ge(xT_ready, at(s, 2, LO))
                V.tensor_copy(xnT[:, LO].rearrange("p a b -> p (a b)"), half(ps_t[1], KD * T)).then_inc(xlT_copied, 1)

            def dt_link(s, k, ins):
                ins.then_inc(dt_step, 1)
                dve.wait_ge(dt_step, at(s, NDT, k))

            DX, AXX, EX, RX, S1, Q1, DE, PL, A1 = range(9)

            def w(k):
                return dtw[:, k]

            def heads(t):
                return t[:, :].unsqueeze(1).to_broadcast([P, NC, NH])

            def dt_start(s):
                dve.wait_ge(dt_mm, at(s, 1, 0))
                dt_link(s, 0, V.scalar_tensor_tensor(
                    w(DX), ps_t[0][:, 0:NC * NH].rearrange("p (c h) -> p c h", c=NC), u_in[:, :], heads(dtb),
                    ALU.mult, ALU.add))
                dt_link(s, 1, V.scalar_tensor_tensor(w(AXX), w(DX), -1.0, w(DX), ALU.mult, ALU.max))

            def dt_softplus(s, q):
                dt_link(s, 2, V.tensor_scalar(w(RX), w(DX), 0.0, None, ALU.max))
                dve.wait_ge(dt_exp, at(s, 3, 0))
                dt_link(s, 3, V.tensor_scalar(w(S1), w(EX), 2.0, None, ALU.add))
                dt_link(s, 4, V.reciprocal(w(Q1), w(S1)))
                dt_link(s, 5, V.tensor_tensor(w(S1), w(EX), w(Q1), ALU.mult))
                dt_link(s, 6, V.tensor_tensor(w(Q1), w(S1), w(S1), ALU.mult))
                dt_link(s, 7, V.tensor_scalar(w(PL), w(Q1), 1.0 / 13, None, ALU.mult))
                for k, d in enumerate((11, 9, 7, 5, 3)):
                    dt_link(s, 8 + k, V.scalar_tensor_tensor(w(PL), w(PL), 1.0 / d, w(Q1), ALU.add, ALU.mult))
                dt_link(s, 13, V.scalar_tensor_tensor(w(PL), w(PL), 1.0, w(S1), ALU.add, ALU.mult))
                dt_link(s, 14, V.scalar_tensor_tensor(dt_[:, q], w(PL), 2.0, w(RX), ALU.mult, ALU.add))
                dt_link(s, 15, V.tensor_tensor(w(A1), dt_[:, q], heads(a_neg), ALU.mult))
                dt_link(s, 16, V.tensor_scalar(w(A1), w(A1), FLOOR, None, ALU.max))

            def dt_decays(s):
                cum = ps_t[1][:, 0:NC * NH].rearrange("p (c h) -> p c h", c=NC)
                tot = ps_t[1][:, NC * NH:2 * NC * NH].rearrange("p (c h) -> p c h", c=NC)
                dve.wait_ge(dt_mm2, at(s, 2, 0))
                dt_link(s, 17, V.tensor_copy(w(PL), cum))
                dt_link(s, 18, V.tensor_tensor(w(DE), tot, w(PL), ALU.subtract))
                dt_link(s, 19, V.tensor_copy(cp3[:, :, 0, :], w(PL)))
                dt_link(s, 20, V.tensor_tensor(w(RX), w(PL), cp3[:, :, 0, :], ALU.subtract))
                dt_link(s, 21, V.tensor_copy(cp3[:, :, 1, :], w(RX)))
                dt_link(s, 22, V.tensor_tensor(cp3[:, :, 2, :], w(RX), cp3[:, :, 1, :], ALU.subtract))

            def dt_rows(s, q):
                dve.wait_ge(dt_mm2, at(s, 2, 1))
                rows = ps_t[0][:, :].bitcast(BF16)[0:NR, 0:P]
                dt_link(s, 23, V.tensor_copy(cT[:, q], rows))
                dt_link(s, 24, V.tensor_scalar(ncT[:, q], rows, -1.0, None, ALU.mult))

            def conv(s, k):
                m = CONV_ORDER[k]
                pr = ps_proj[PROJ.index(("c", m)) % 2]
                dve.wait_ge(acc_init, at(s, NM, k))
                for d in (1, 2, 3):
                    if d > 1:
                        dve.wait_ge(conv_step, at(s, 3 * NM, 3 * k + d - 2))
                    V.scalar_tensor_tensor(acc[:, k % 2, d:T], pr[:, 0:T - d], cwu[:, m, 3 - d:4 - d],
                                           acc[:, k % 2, d:T], ALU.mult, ALU.add).then_inc(conv_step, 1)

            def g_copy(s):
                dve.wait_ge(g_mm, at(s, 1, 0))
                V.tensor_copy(Gm[:, :, :].rearrange("p c t -> p (c t)"), ps_t[1][:, :]).then_inc(g_done, 1)

            def weigh(s, c, g):
                if c == 0 and g == 0:
                    dve.wait_ge(g_done, at(s, 1, 0))
                dve.wait_ge(l_done, at(s, 2 * NC, 2 * c + g))
                if c >= 2:
                    dve.wait_ge(intra_mm, at(s, NC, c - 2))
                V.tensor_tensor(Mb[:, 2 * (c % 2) + g], Lb[:, g].rearrange("p (h t) -> p h t", h=4),
                                Gm[:, c].unsqueeze(1).to_broadcast([P, 4, P]), ALU.mult).then_inc(m_done, 1)

            def x_tokens(s, q, c):
                xt = ps_t[0][:, :].rearrange("p (h d) -> p h d", h=NH)
                dve.wait_ge(xt_mm, at(s, NC, c))
                if c >= 2:
                    dve.wait_ge(intra_mm, at(s, NC, c - 2))
                    dve.wait_ge(xst_done, at(s, NC - 1, c - 2))
                V.tensor_tensor(Xdt[:, c % 2].rearrange("p (h d) -> p h d", h=NH), xt,
                                dt_[:, q, c].unsqueeze(2).to_broadcast([P, NH, HD]), ALU.mult).then_inc(xdt_done, 1)
                V.tensor_tensor(XD[:, c % 2].rearrange("p (h d) -> p h d", h=NH), xt,
                                d_bc[:, :].unsqueeze(2).to_broadcast([P, NH, HD]), ALU.mult).then_inc(xdt_done, 1)

            def from_state(s, q, c):
                dve.wait_ge(inter_mm, at(s, NC - 1, c - 1))
                V.tensor_tensor(ti[:, :].rearrange("p (h d) -> p h d", h=NH), ps_i[:, :].rearrange("p (h d) -> p h d", h=NH),
                                ecs[:, q, 0, c].unsqueeze(2).to_broadcast([P, NH, HD]), ALU.mult).then_inc(ti_done, 1)

            def y_sum(s, c):
                dve.wait_ge(intra_mm, at(s, NC, c))
                if c:
                    dve.wait_ge(ti2_done, at(s, NC - 1, c - 1))
                V.tensor_tensor(yb[:, c % 2], ps_y[:, :], ti2[:, :] if c else XD[:, 0], ALU.add).then_inc(y_done, 1)

            def next_state(s, c):
                dve.wait_ge(state_mm, at(s, NC - 1, c))
                dve.wait_ge(hd_done, at(s, NC - 2, c - 1))
                V.tensor_tensor(hst[:, c % 2], ps_i[:, :], hd[:, :], ALU.add).then_inc(h_done, 1)

            def gated(s, c):
                dve.wait_ge(rv_step, at(s, 3 * NC, 3 * c + 2))
                if c == 0:
                    dve.wait_ge(z_done, at(s, NC, NC - 1))
                V.scalar_tensor_tensor(yg[:, c % 2], yb[:, c % 2], rv[:, 2, c:c + 1], sz[:, c], ALU.mult,
                                       ALU.mult).then_inc(yg_done, 1)

            def gate_copy(s, c):
                dve.wait_ge(yT_mm, at(s, NC, c))
                V.tensor_copy(ygT[:, c % 2].rearrange("p a b t -> p (a b t)"), half(ps_t[1], 2 * DI)).then_inc(yT_copied, 1)

            def residual(s, q, c):
                dve.wait_ge(o_mm, at(s, NC, c))
                V.scalar_tensor_tensor(x2[:, q, c], ps_t[0][:, 0:DM], u_out[:, :], x_sb[:, q, c], ALU.mult,
                                       ALU.add).then_inc(x2_done, 1)
                dve.wait_ge(x2_done, at(s, NC, c))
                V.bn_stats(st2[:, c], x2[:, q, c]).then_inc(st2_done, 1)
                dve.wait_ge(st2_done, at(s, NC, c))
                V.memset(pause[:, :], 0.0)
                V.bn_aggr(mv2[:, c], st2[:, c]).then_inc(mv2_done, 1)

            def norm2(s, q, c):
                dve.wait_ge(rv2_step, at(s, 3 * NC, 3 * c + 2))
                V.tensor_scalar(xn2[:, c % 2], x2[:, q, c], mv2[:, c, 0:1], rv2[:, 2, c:c + 1],
                                ALU.subtract, ALU.mult).then_inc(xn2_done, 1)

            def relu_square(s, j):
                dve.wait_ge(r_done, at(s, NJ, j))
                if j >= 2:
                    dve.wait_ge(rl_done, at(s, NJ, j - 2))
                V.tensor_tensor(r2[:, j % 2], r[:, j % 2], r[:, j % 2], ALU.mult).then_inc(r2_done, 1)

            def down_scale(s, c):
                dve.wait_ge(dn_mm, at(s, NC, c))
                if c >= 2:
                    dve.wait_ge(ob_done, at(s, NC, c - 2))
                V.tensor_tensor(ot[:, c % 2], ps_f[:, 0:DM], dn_bc[:, :], ALU.mult).then_inc(ot_done, 1)

            def round_(s, q, ffn=True, nxt=True):
                p = 1 - q
                conv(s, 0)
                if ffn:
                    gate_copy(s - 1, 3)
                conv(s, 1)
                if ffn:
                    residual(s - 1, p, 3)
                conv(s, 2)
                if ffn:
                    norm2(s - 1, p, 3)
                conv(s, 3)
                conv(s, 4)
                if ffn:
                    relu_square(s - 1, 0)
                    relu_square(s - 1, 1)
                if nxt:
                    input_stats(s + 1, p)
                conv(s, 5)
                if ffn:
                    relu_square(s - 1, 2)
                if nxt:
                    input_norm(s + 1, p)
                if ffn:
                    relu_square(s - 1, 3)
                g_copy(s)
                if ffn:
                    relu_square(s - 1, 4)
                weigh(s, 0, 0)
                if ffn:
                    relu_square(s - 1, 5)
                weigh(s, 0, 1)
                x_tokens(s, q, 0)
                if ffn:
                    relu_square(s - 1, 6)
                for c in range(NC):
                    if c < NC - 1:
                        weigh(s, c + 1, 0)
                    if c == 0 and ffn:
                        relu_square(s - 1, 7)
                    if c < NC - 1:
                        weigh(s, c + 1, 1)
                    if c:
                        from_state(s, q, c)
                    if c == 3 and nxt:
                        dt_decays(s + 1)
                    if c < NC - 1:
                        x_tokens(s, q, c + 1)
                    y_sum(s, c)
                    if c:
                        gate_copy(s, c - 1)
                    if c == 1 or c == 2:
                        next_state(s, c)
                    if ffn:
                        down_scale(s - 1, c)
                    if c:
                        residual(s, q, c - 1)
                    gated(s, c)
                    if nxt:
                        if c == 1:
                            input_copy(s + 1)
                        if c == 2:
                            dt_start(s + 1)
                    if c:
                        norm2(s, q, c - 1)
                    if c == 2 and nxt:
                        dt_softplus(s + 1, p)
                if nxt:
                    dt_rows(s + 1, p)

            def finish(s, q):
                gate_copy(s, 3)
                residual(s, q, 3)
                norm2(s, q, 3)
                for j in range(NJ):
                    relu_square(s, j)
                for c in range(NC):
                    down_scale(s, c)

            input_stats(0, 0)
            input_norm(0, 0)
            input_copy(0)
            dt_start(0)
            dt_softplus(0, 0)
            dt_decays(0)
            dt_rows(0, 0)
            round_(0, 0, ffn=False)
            with dve.Fori(0, S // 2 - 1) as i:
                round_(i * 2 + 1, 1)
                round_(i * 2 + 2, 0)
            round_(S - 1, 1, nxt=False)
            finish(S - 1, 1)

        @block.tensor
        def _(pe):
            n = [0]

            def step(ins):
                n[0] += 1
                ins.then_inc(prep_pe, 1)

            mm, tr = nc.tensor.matmul, nc.tensor.transpose
            pe.wait_ge(w_loaded, 16 * NLOAD)
            pe.wait_ge(prep_pool, POOL_CONST)
            step(mm(ps_f[0:RANK, 0:DM], fbT[:, :], raw_v[:, :], start=True, stop=True))
            assert n[0] == PE_FV
            for j in range(NJ):
                step(tr([ps_y, ps_i][j // 4][0:RANK, (j % 4) * P:(j % 4 + 1) * P], raw_u[:, j, :], ident[:, :]))
            assert n[0] == PE_UT
            pe.wait_ge(prep_dve, DVE_UT)
            for j in range(NJ):
                if j >= 2:
                    pe.wait_ge(prep_dve, DVE_TERN + 4 * (j - 1))
                step(mm(ps_proj[j % 2][:, 0:DM], uT[:, j, :], fv[:, :], start=True, stop=True))
            for g in range(2):
                for k in range(2):
                    for j in range(KD):
                        i = tr([ps_y, ps_i][g][:, k * DM + j * P:k * DM + (j + 1) * P],
                               raw_out[:, j, (2 * g + k) * P:(2 * g + k + 1) * P], ident[:, :])
                step(i)
            assert n[0] == PE_WO + 1, n[0]
            pe.wait_ge(prep_dve, DVE_MX)
            for j in range(KD):
                i = mm(ps_f[:, j * P:(j + 1) * P], ones[:, :], dnd[:, j], start=True, stop=True)
            step(i)
            step(tr(ps_d[0:NS, 0:P], mxa[:, :], ident[:, :]))
            assert n[0] == PE_MX, n[0]
            pe.wait_ge(prep_dve, DVE_MXD)
            step(mm(ps_d[:, 0:NS], ones[0:NS, :], mxd[:, :], start=True, stop=True))
            assert n[0] == PE_MXB, n[0]
            for g, (src, _, _, _, _) in enumerate(groups):
                if g >= NB:
                    if groups[g - NB][4] is None:
                        pe.wait_ge(prep_act, ACT_NORMS + g - NB + 1)
                    else:
                        pe.wait_ge(prep_dve, DVE_LOW + g - NB + 1)
                for k, a in enumerate(src):
                    rows = a.shape[0]
                    i = tr(prep_banks[g % NB][:, k * P:k * P + rows], a, ident[0:rows, 0:rows])
                step(i)
            pe.wait_ge(prep_dve, DVE_ALL)
            pe.wait_ge(prep_act, ACT_ALL)

            def input_transpose(s, part):
                pe.wait_ge(xh_done if part == HI else xl_done, at(s, 1, 0))
                for k in range(KD):
                    for c in range(NC):
                        i = tr(half(ps_t[1], KD * T)[:, k * T + c * P:k * T + (c + 1) * P],
                               (xh if part == HI else xl)[:, c, k * P:(k + 1) * P], ident16[:, :])
                i.then_inc(xT_ready, 1)

            def three(ps, lhs, rhs, kk):
                for a, (wp, xp) in enumerate(PASSES):
                    for k in range(kk):
                        i = mm(ps, lhs(wp, xp, k), rhs(wp, xp, k), start=(a == 0 and k == 0),
                               stop=(a == 2 and k == kk - 1))
                return i

            def dt_product(s):
                pe.wait_ge(xhT_copied, at(s, 1, 0))
                pe.wait_ge(xlT_copied, at(s, 1, 0))
                for c in range(NC):
                    i = three(ps_t[0][:, c * NH:(c + 1) * NH],
                              lambda wp, xp, k: xnT[:, xp, k, c * P:(c + 1) * P],
                              lambda wp, xp, k: w_in[:, wp, k, NPROJ - NH:NPROJ], KD)
                i.then_inc(dt_mm, 1)

            def cumulate(s):
                pe.wait_ge(dt_step, at(s, NDT, 16))
                a = dtw[:, 8].rearrange("p c h -> p (c h)")
                mm(ps_t[1][:, 0:NC * NH], tri[:, :], a, start=True, stop=True)
                mm(ps_t[1][:, NC * NH:2 * NC * NH], ones[:, :], a, start=True, stop=True).then_inc(dt_mm2, 1)

            def cum_rows(s):
                pe.wait_ge(dt_step, at(s, NDT, 22))
                tr(ps_t[0][:, :].bitcast(BF16)[0:NR, 0:P], cp3[:, :, :, :].rearrange("p a b c -> p (a b c)"),
                   identb[:, :]).then_inc(dt_mm2, 1)

            def project(s, k):
                kind, m = PROJ[k]
                if k >= 2:
                    kind2, m2 = PROJ[k - 2]
                    if kind2 == "c":
                        pe.wait_ge(conv_step, at(s, 3 * NM, 3 * CONV_ORDER.index(m2) + 2))
                    else:
                        pe.wait_ge(z_done, at(s, NC, m2))
                if kind == "c":
                    i = three(ps_proj[k % 2][:, :], lambda wp, xp, kk: w_in[:, wp, kk, DI + m * P:DI + (m + 1) * P],
                              lambda wp, xp, kk: xnT[:, xp, kk, :], KD)
                else:
                    i = three(ps_proj[k % 2][:, :], lambda wp, xp, kk: xnT[:, xp, kk, m * P:(m + 1) * P],
                              lambda wp, xp, kk: w_in[:, wp, kk, 0:DI], KD)
                i.then_inc(proj_done, 1)

            XB, XC = 4, 5

            def b_transpose(s):
                pe.wait_ge(xc_done, at(s, NM, 0))
                for c in range(NC):
                    i = tr(ps_t[0][:, c * P:(c + 1) * P], xc[:, XB, c * P:(c + 1) * P], ident[:, :])
                i.then_inc(bt_mm, 1)

            def g_product(s):
                pe.wait_ge(xc_done, at(s, NM, 1))
                for c in range(NC):
                    i = mm(ps_t[1][:, c * P:(c + 1) * P], xc[:, XB, c * P:(c + 1) * P], xc[:, XC, c * P:(c + 1) * P],
                           start=True, stop=True)
                i.then_inc(g_mm, 1)

            def decay_logs(s, q, c, g):
                if c == 0 and g == 0:
                    pe.wait_ge(dt_step, at(s, NDT, 24))
                else:
                    pe.wait_ge(l_done, at(s, 2 * NC, 2 * c + g - 1))
                rows = pick[:, c * NH + 4 * g:c * NH + 4 * g + 4, :]
                for h in range(4):
                    mm(ps_d[:, h * P:(h + 1) * P], pick[:, c * NH + 4 * g + h, :], cT[:, q], start=(h == 0), stop=False)
                mm(ps_d[:, :], identb[:, :], above[:, :, :].rearrange("p h t -> p (h t)"), start=False, stop=False)
                mm(ps_d[:, :], ncT[:, q], rows.rearrange("k h p -> k (h p)"), start=False, stop=True).then_inc(d_mm, 1)

            def x_transpose(s, c):
                if c == 0:
                    pe.wait_ge(bt_copied, at(s, 1, 0))
                    pe.wait_ge(xc_done, at(s, NM, NM - 1))
                elif c == 1:
                    pe.wait_ge(xdt_done, at(s, 2 * NC, 1))
                elif c == 2:
                    pe.wait_ge(xdt_done, at(s, 2 * NC, 3))
                else:
                    pe.wait_ge(x2_done, at(s, NC, 0))
                for m in range(DI // P):
                    i = tr(ps_t[0][:, m * P:(m + 1) * P], xc[:, m, c * P:(c + 1) * P], ident[:, :])
                i.then_inc(xt_mm, 1)

            def intra(s, c):
                pe.wait_ge(m_done, at(s, 2 * NC, 2 * c + 1))
                pe.wait_ge(xdt_done, at(s, 2 * NC, 2 * c))
                if c:
                    pe.wait_ge(y_done, at(s, NC, c - 1))
                elif type(s) is not int or s:
                    pe.wait_ge(y_done, at(s - 1, NC, NC - 1))
                for h in range(NH):
                    i = mm(ps_y[:, h * HD:(h + 1) * HD], Mb[:, 2 * (c % 2) + h // 4, h % 4, :],
                           Xdt[:, c % 2, h * HD:(h + 1) * HD], start=True, stop=True)
                i.then_inc(intra_mm, 1)

            def inter(s, c):
                pe.wait_ge(h_done, at(s, NC - 1, c - 1))
                mm(ps_i[:, :], xc[:, XC, c * P:(c + 1) * P], hst[:, (c - 1) % 2], start=True, stop=True).then_inc(inter_mm, 1)

            def state(s, c):
                pe.wait_ge(xst_done, at(s, NC - 1, c))
                if c:
                    pe.wait_ge(ti_done, at(s, NC - 1, c - 1))
                elif type(s) is not int or s:
                    pe.wait_ge(ti_done, at(s - 1, NC - 1, NC - 2))
                mm(ps_i[:, :], Bt[:, c, :], Xst[:, c % 2], start=True, stop=True).then_inc(state_mm, 1)

            def gate_transpose(s, c):
                pe.wait_ge(ygh_done, at(s, NC, c))
                pe.wait_ge(ygl_done, at(s, NC, c))
                dst = half(ps_t[1], 2 * DI)
                for part, src in ((HI, ygh), (LO, ygl)):
                    for m in range(DI // P):
                        i = tr(dst[:, part * DI + m * P:part * DI + (m + 1) * P], src[:, c % 2, m * P:(m + 1) * P], ident16[:, :])
                i.then_inc(yT_mm, 1)

            def out_product(s, c):
                pe.wait_ge(yT_copied, at(s, NC, c))
                three(ps_t[0][:, 0:DM], lambda wp, xp, k: ygT[:, c % 2, xp, k, :],
                      lambda wp, xp, k: w_o[:, wp, k, :], DI // P).then_inc(o_mm, 1)

            def transpose2(s, c):
                pe.wait_ge(x2h_done, at(s, NC, c))
                pe.wait_ge(x2l_done, at(s, NC, c))
                dst = half(ps_t[1], 2 * KD * P)
                for part, src in ((HI, x2h), (LO, x2l)):
                    for k in range(KD):
                        i = tr(dst[:, (part * KD + k) * P:(part * KD + k + 1) * P], src[:, c % 2, k * P:(k + 1) * P], ident16[:, :])
                i.then_inc(x2T_mm, 1)

            def up(s, q, j):
                if j == 0:
                    pe.wait_ge(x2T_copied, at(s, NC, NC - 1))
                else:
                    pe.wait_ge(r_done, at(s, NJ, j - 1))
                three(ps_f[:, :], lambda wp, xp, k: w_up[:, wp, k, j * P:(j + 1) * P],
                      lambda wp, xp, k: xn2T[:, q, xp, k, :], KD).then_inc(up_mm, 1)

            def down(s, c):
                if c == 0:
                    pe.wait_ge(r_done, at(s, NJ, NJ - 1))
                    pe.wait_ge(rh_done, at(s, NJ, NJ - 1))
                    pe.wait_ge(rl_done, at(s, NJ, NJ - 1))
                else:
                    pe.wait_ge(ot_done, at(s, NC, c - 1))
                for part in (HI, LO):
                    for j in range(NJ):
                        i = mm(ps_f[:, 0:DM], rT[:, part, j, c * P:(c + 1) * P], w_dn[:, j, :],
                               start=(part == HI and j == 0), stop=(part == LO and j == NJ - 1))
                i.then_inc(dn_mm, 1)

            def round_(s, q, ffn=True, nxt=True):
                p = 1 - q
                project(s, 0)
                if ffn:
                    pe.wait_ge(x2T_copied, at(s - 1, NC, 1))
                    transpose2(s - 1, 2)
                project(s, 1)
                if ffn:
                    pe.wait_ge(x2T_copied, at(s - 1, NC, 2))
                    gate_transpose(s - 1, 3)
                project(s, 2)
                if ffn:
                    pe.wait_ge(dt_step, at(s, NDT, 24))
                    out_product(s - 1, 3)
                project(s, 3)
                project(s, 4)
                project(s, 5)
                if ffn:
                    transpose2(s - 1, 3)
                project(s, 6)
                if ffn:
                    up(s - 1, p, 0)
                project(s, 7)
                if ffn:
                    up(s - 1, p, 1)
                project(s, 8)
                if ffn:
                    up(s - 1, p, 2)
                project(s, 9)
                if ffn:
                    pe.wait_ge(x2_done, at(s - 1, NC, 3))
                else:
                    pe.wait_ge(dt_step, at(s, NDT, 24))
                b_transpose(s)
                if ffn:
                    up(s - 1, p, 3)
                    pe.wait_ge(x2T_copied, at(s - 1, NC, 3))
                g_product(s)
                if ffn:
                    up(s - 1, p, 4)
                decay_logs(s, q, 0, 0)
                if ffn:
                    up(s - 1, p, 5)
                decay_logs(s, q, 0, 1)
                x_transpose(s, 0)
                if ffn:
                    up(s - 1, p, 6)
                for c in range(NC):
                    if c < NC - 1:
                        decay_logs(s, q, c + 1, 0)
                    if c == 0 and ffn:
                        up(s - 1, p, 7)
                    if c:
                        inter(s, c)
                    intra(s, c)
                    if c < NC - 1:
                        decay_logs(s, q, c + 1, 1)
                        x_transpose(s, c + 1)
                    if c < NC - 1:
                        state(s, c)
                    if c == 0:
                        if nxt:
                            pe.wait_ge(g_done, at(s, 1, 0))
                            input_transpose(s + 1, HI)
                    if c == 1:
                        if nxt:
                            pe.wait_ge(xhT_copied, at(s + 1, 1, 0))
                        else:
                            pe.wait_ge(g_done, at(s, 1, 0))
                        gate_transpose(s, 0)
                    if c == 2:
                        if nxt:
                            pe.wait_ge(xlT_copied, at(s + 1, 1, 0))
                        gate_transpose(s, 1)
                    if c == 3:
                        pe.wait_ge(x2T_copied, at(s, NC, 0))
                        if nxt:
                            cumulate(s + 1)
                            pe.wait_ge(dt_exp, at(s + 1, 3, 1))
                        gate_transpose(s, 2)
                    if ffn:
                        down(s - 1, c)
                    if c:
                        if c < NC - 1:
                            pe.wait_ge(xdt_done, at(s, 2 * NC, 2 * (c + 1) + 1))
                        elif nxt:
                            pe.wait_ge(dt_step, at(s + 1, NDT, 0))
                        else:
                            pe.wait_ge(x2_done, at(s, NC, 1))
                        out_product(s, c - 1)
                    if c == 1 and nxt:
                        pe.wait_ge(yT_copied, at(s, NC, 0))
                        input_transpose(s + 1, LO)
                    if c == 2:
                        if nxt:
                            pe.wait_ge(x2_done, at(s, NC, 1))
                            dt_product(s + 1)
                    if c > 1:
                        pe.wait_ge(yT_copied, at(s, NC, c - 1))
                        transpose2(s, c - 2)
                if nxt:
                    pe.wait_ge(x2_done, at(s, NC, 2))
                    cum_rows(s + 1)

            def finish(s, q):
                pe.wait_ge(x2T_copied, at(s, NC, 1))
                transpose2(s, 2)
                pe.wait_ge(x2T_copied, at(s, NC, 2))
                gate_transpose(s, 3)
                pe.wait_ge(x2_done, at(s, NC, 2))
                out_product(s, 3)
                transpose2(s, 3)
                for j in range(NJ):
                    up(s, q, j)
                for c in range(NC):
                    down(s, c)

            input_transpose(0, HI)
            pe.wait_ge(xhT_copied, 1)
            input_transpose(0, LO)
            dt_product(0)
            cumulate(0)
            cum_rows(0)
            round_(0, 0, ffn=False)
            with pe.Fori(0, S // 2 - 1) as i:
                round_(i * 2 + 1, 1)
                round_(i * 2 + 2, 0)
            round_(S - 1, 1, nxt=False)
            finish(S - 1, 1)


_INS = ["u", "in_proj_w", "conv_w", "conv_b", "dt_bias", "A_log", "D", "norm_w", "out_proj_w"]
_FFN = ["fast_b", "w_fc", "w_proj", "u", "v", "gate"]


def kernel(**inputs):
    import numpy as _np
    import concourse.bacc as _bacc
    from concourse import mybir as _mybir
    from concourse.bass_utils import run_bass_kernel_spmd as _run

    nc = _bacc.Bacc("TRN2", target_bir_lowering=False, num_devices=1)
    arrays, args = {}, []
    for name in ["L0_attn_" + n for n in _INS] + ["L0_ffn_" + n for n in _FFN]:
        a = _np.ascontiguousarray(inputs[name])
        a = a.reshape(a.shape or (1,))
        arrays[f"in_{name}"] = a
        args.append(nc.dram_tensor(f"in_{name}", a.shape, _mybir.dt.from_np(a.dtype), kind="ExternalInput").ap())
    shape = inputs["L0_attn_u"].shape
    args.append(nc.dram_tensor("out_0", shape, _mybir.dt.float32, kind="ExternalOutput").ap())
    build(nc, *args)
    r = _run(nc, [arrays], core_ids=[0])
    return r.results[0]["out_0"]
```

```python
from contextlib import ExitStack

import numpy as np
import concourse.bass as bass
from concourse import mybir

ALU = mybir.AluOpType
ACT = mybir.ActivationFunctionType
F32 = mybir.dt.float32
F16 = mybir.dt.float16
BF16 = mybir.dt.bfloat16
I32 = mybir.dt.int32
AX_X = mybir.AxisListType.X

P = 128
DM = 256
KD = DM // P
T = 512
NC = T // P
DI = 512
NH, HD = 8, 64
NST = 128
CONV = DI + 2 * NST
NM = CONV // P
TAPS = 4
NPROJ = 2 * DI + 2 * NST + NH
HID = 1024
NJ = HID // P
NLP = NJ - 2
RANK = 16
EPS = 1e-5
XS = 1024.0
FLOOR = -104.0
ABOVE = -30000.0
HI, LO = 0, 1
PASSES = ((HI, HI), (HI, LO), (LO, HI))
PROJ = (("c", 4), ("c", 5), ("c", 0), ("c", 1), ("c", 2), ("z", 0), ("c", 3), ("z", 1), ("z", 2), ("z", 3))
CONV_ORDER = [m for kind, m in PROJ if kind == "c"]
NDT = 25

NLOAD = 15
POOL_CONST, POOL_ALL = 16, 17
ACT_SUMS, ACT_NORMS, ACT_GROUPS, ACT_ALL = 15, 23, 37, 38
PE_FV, PE_UT, PE_WO, PE_MX, PE_MXB = 1, 9, 18, 21, 22
DVE_UT, DVE_TERN, DVE_WEFF, DVE_MX, DVE_MXD, DVE_P2, DVE_SCALES, DVE_LOW, DVE_ALL = 4, 7, 39, 59, 61, 63, 65, 78, 89


def build(nc, u, in_proj_w, conv_w, conv_b, dt_bias, A_log, D, norm_w, out_proj_w,
          fast_b, w_fc, w_proj, lr_u, lr_v, gate, out):
    S = u.shape[0]
    with ExitStack() as ctx:
        def sb(name, shape, dt=F32):
            return ctx.enter_context(nc.sbuf_tensor(name, shape, dt))

        def sem(name):
            return ctx.enter_context(nc.semaphore(name))

        def bank(name):
            return ctx.enter_context(nc.psum_tensor(name, [P, 512], F32))
        ps_proj = [bank("ps_proj0"), bank("ps_proj1")]
        ps_t = [bank("ps_t0"), bank("ps_t1")]
        ps_d, ps_y, ps_i, ps_f = bank("ps_d"), bank("ps_y"), bank("ps_i"), bank("ps_f")
        proj_banks = [ps_proj[0], ps_d, ps_proj[1], ps_y, ps_i]
        NPB = len(proj_banks)
        d_banks, down_banks = [ps_d, ps_proj[0]], [ps_f, ps_proj[1]]
        up_banks = [down_banks[j >= 3 and j % 2] for j in range(NJ)]

        def half(b, n):
            return b[:, :].bitcast(F16)[:, 0:n]

        w_in = sb("w_in", [P, 2, KD, NPROJ], F16)
        w_up = sb("w_up", [P, 2, KD, HID], F16)
        w_dn = sb("w_dn", [P, NJ, DM], F16)
        w_o = sb("w_o", [P, 2, DI // P, DM], F16)
        ident = sb("ident", [P, P])
        ident16 = sb("ident16", [P, P], F16)
        identb = sb("identb", [P, P], BF16)
        tri = sb("tri", [P, P])
        ones = sb("ones", [P, P])
        NR = 3 * NC * NH
        pick = sb("pick", [NR, NC * NH, P], BF16)
        above = sb("above", [P, 4, P], BF16)
        cw = sb("cw", [P, NM, TAPS])
        cwu = sb("cwu", [P, NM, TAPS])
        cb = sb("cb", [P, NM])
        dtb = sb("dtb", [P, NH])
        alog = sb("alog", [P, 3, NH])
        aexp = sb("aexp", [P, 3, NH])
        a_neg = sb("a_neg", [P, NH])
        d_bc = sb("d_bc", [P, NH])
        nw = sb("nw", [P, DI // P])
        gate_bc = sb("gate_bc", [P, 1])
        u_in = sb("u_in", [P, 1])
        u_relu = sb("u_relu", [P, 1])
        u_out = sb("u_out", [P, 1])
        g_gate = sb("g_gate", [P, 1])
        dn_bc = sb("dn_bc", [P, DM])
        mhalf = sb("mhalf", [P, NC])
        epsb = sb("epsb", [P, NC])
        xsb = sb("xsb", [P, NC])
        epsd = sb("epsd", [P, 1])
        pause = sb("pause", [P, 1])
        x_sb = sb("x_sb", [P, 2, NC, DM])
        st1 = sb("st1", [P, NC, 6])
        mv1 = sb("mv1", [P, NC, 2])
        va1 = sb("va1", [P, NC])
        rs1 = sb("rs1", [P, NC])
        rs1s = sb("rs1s", [P, NC])
        xn = sb("xn", [P, NC, DM])
        xh = sb("xh", [P, NC, DM], F16)
        xl = sb("xl", [P, NC, DM], F16)
        xnT = sb("xnT", [P, 2, KD, T], F16)
        dtw = sb("dtw", [P, 9, NC, NH])
        dt_ = sb("dt_", [P, 2, NC, NH])
        ecs = sb("ecs", [P, 2, 2, NC, NH])
        ede = sb("ede", [P, 2, NC, NH])
        cp3 = sb("cp3", [P, NC, 3, NH], BF16)
        cT = sb("cT", [NR, 2, P], BF16)
        ncT = sb("ncT", [NR, 2, P], BF16)
        acc = sb("acc", [P, 4, T])
        xc = sb("xc", [P, NM, T])
        sz = sb("sz", [P, NC, DI])
        Bt = sb("Bt", [P, NC, P])
        Gm = sb("Gm", [P, NC, P])
        tok = sb("tok", [P, 6, DI])
        Xdt, XD, Xst = tok[:, 0:2], tok[:, 2:4], tok[:, 4:6]
        Lb = sb("Lb", [P, 2, 512])
        Mb = sb("Mb", [P, 4, 4, P])
        hst = sb("hst", [P, 2, DI])
        hd = sb("hd", [P, DI])
        ti = sb("ti", [P, DI])
        ti2 = sb("ti2", [P, DI])
        yb = sb("yb", [P, 2, DI])
        ysq = sb("ysq", [P, DI])
        ssq = sb("ssq", [P, NC])
        rv = sb("rv", [P, 3, NC])
        yg = sb("yg", [P, 2, DI])
        ygh = sb("ygh", [P, 2, DI], F16)
        ygl = sb("ygl", [P, 2, DI], F16)
        ygT = sb("ygT", [P, 2, 2, DI // P, P], F16)
        x2 = sb("x2", [P, 2, NC, DM])
        st2 = sb("st2", [P, NC, 6])
        mv2 = sb("mv2", [P, NC, 2])
        rv2 = sb("rv2", [P, 3, NC])
        xn2 = sb("xn2", [P, 2, DM])
        x2h = sb("x2h", [P, 2, DM], F16)
        x2l = sb("x2l", [P, 2, DM], F16)
        xn2T = sb("xn2T", [P, 2, 2, KD, T], F16)
        r = sb("r", [P, 2, T])
        r2 = sb("r2", [P, 2, T])
        rT = sb("rT", [P, 2, NJ, T], F16)
        ot = sb("ot", [P, 2, DM])
        ob = sb("ob", [P, 2, DM])
        NT = NPROJ // P
        raw_in = tok[:, :, :].rearrange("p a b -> p (a b)")[:, 0:(NT + 1) * DM].rearrange("p (j n) -> p j n", n=DM)
        raw_out = Lb
        wo32 = Mb[:, 0:2, :, :].rearrange("p a b c -> p (a b c)").rearrange("p (m n) -> p m n", m=DI // P)
        raw_fc = sz[:, :, :].rearrange("p a b -> p (a b)").rearrange("p (j n) -> p j n", j=NJ)
        raw_dn = rT[:, 0, :, :].rearrange("p a b -> p (a b)").bitcast(F32).rearrange("p (j n) -> p j n", j=KD)
        weff = rT[:, 1, :, :].rearrange("p a b -> p (a b)").bitcast(F32).rearrange("p (j n) -> p j n", j=NJ)
        tern_a = xc[:, 0:4, :].rearrange("p a b -> p (a b)").rearrange("p (j n) -> p j n", j=NJ)
        raw_u = sb("raw_u", [P, NJ, RANK])
        raw_v = sb("raw_v", [RANK, DM])
        fbT = sb("fbT", [RANK, RANK])
        fv = sb("fv", [RANK, DM])
        uT = hst[0:RANK].rearrange("p a b -> p (a b)").rearrange("p (j n) -> p j n", j=NJ)
        NS = 5
        mx = sb("mx", [P, 8, 16])
        mxa = sb("mxa", [P, NS])
        mxT = sb("mxT", [NS, P])
        mxm = sb("mxm", [NS, 1])
        mxd = sb("mxd", [NS, NS])
        mxb = sb("mxb", [P, NS])
        p2 = sb("p2", [P, NS])
        ip2 = sb("ip2", [P, NS])
        rp = sb("rp", [P, NS])
        sw = sb("sw", [P, NS])
        fcs = sb("fcs", [P, 4, NJ])
        dns = sb("dns", [P, 6, KD])
        junk = r[:, :, :].rearrange("p a b -> p (a b)")
        tern_b = r2[:, :, :].rearrange("p a b -> p (a b)")
        dnd = sb("dnd", [P, KD, P])

        w_loaded, zeroed = sem("w_loaded"), sem("zeroed")
        x_loaded = [sem("x_loaded_even"), sem("x_loaded_odd")]
        stored = [sem("stored_even"), sem("stored_odd")]
        prep_pool, prep_act, prep_dve, prep_pe = sem("prep_pool"), sem("prep_act"), sem("prep_dve"), sem("prep_pe")
        st1_done, mv1_done, rs1_step, xn_done = sem("st1_done"), sem("mv1_done"), sem("rs1_step"), sem("xn_done")
        xh_done, xl_done = sem("xh_done"), sem("xl_done")
        xT_ready, xhT_copied, xlT_copied = sem("xT_ready"), sem("xhT_copied"), sem("xlT_copied")
        dt_mm, dt_mm2, dt_step, dt_exp = sem("dt_mm"), sem("dt_mm2"), sem("dt_step"), sem("dt_exp")
        proj_done, acc_init, conv_step, xc_done, z_done = (
            sem("proj_done"), sem("acc_init"), sem("conv_step"), sem("xc_done"), sem("z_done"))
        bt_mm, bt_copied, g_mm, g_done = sem("bt_mm"), sem("bt_copied"), sem("g_mm"), sem("g_done")
        d_mm, l_done, m_done = sem("d_mm"), sem("l_done"), sem("m_done")
        xt_mm, xdt_done, xst_done = sem("xt_mm"), sem("xdt_done"), sem("xst_done")
        intra_mm, inter_mm, state_mm = sem("intra_mm"), sem("inter_mm"), sem("state_mm")
        ti_done, ti2_done, h_done, hd_done = sem("ti_done"), sem("ti2_done"), sem("h_done"), sem("hd_done")
        y_done, ssq_done, rv_step, yg_done, ygh_done, ygl_done = (
            sem("y_done"), sem("ssq_done"), sem("rv_step"), sem("yg_done"), sem("ygh_done"), sem("ygl_done"))
        yT_mm, yT_copied, o_mm, x2_done = sem("yT_mm"), sem("yT_copied"), sem("o_mm"), sem("x2_done")
        st2_done, mv2_done, rv2_step, xn2_done = sem("st2_done"), sem("mv2_done"), sem("rv2_step"), sem("xn2_done")
        x2h_done, x2l_done, x2T_mm, x2T_copied = sem("x2h_done"), sem("x2l_done"), sem("x2T_mm"), sem("x2T_copied")
        up_mm, r_done, r2_done, rh_done, rl_done, rlv_done = (
            sem("up_mm"), sem("r_done"), sem("r2_done"), sem("rh_done"), sem("rl_done"), sem("rlv_done"))
        dn_mm, ot_done, ob_done = sem("dn_mm"), sem("ot_done"), sem("ob_done")

        xs = u.rearrange("s (c p) d -> s p c d", p=P)
        outs = out.rearrange("s (c p) d -> s c p d", p=P)

        groups = []
        for k in range(KD):
            for m0, m1 in ((0, 4), (4, 8), (8, NT + 1)):
                src = [raw_in[0:(P if m < NT else NPROJ - NT * P), m, k * P:(k + 1) * P] for m in range(m0, m1)]
                e = min(m1 * P, NPROJ)
                groups.append((src, e - m0 * P, w_in[:, HI, k, m0 * P:e], w_in[:, LO, k, m0 * P:e], 0))
        for k in range(KD):
            for j in range(0, NJ, 4):
                src = [weff[:, j + a, k * P:(k + 1) * P] for a in range(4)]
                groups.append((src, 4 * P, w_up[:, HI, k, j * P:(j + 4) * P], w_up[:, LO, k, j * P:(j + 4) * P], 3))
        for j in range(0, NJ, 2):
            src = [raw_dn[:, k, (j + a) * P:(j + a + 1) * P] for a in range(2) for k in range(KD)]
            groups.append((src, 4 * P, w_dn[:, j:j + 2, :].rearrange("p a b -> p (a b)"), None, None))
        prep_banks = ps_proj + ps_t
        NB = len(prep_banks)

        block = ctx.enter_context(nc.Block())

        def at(s, n, k):
            return s * n + (k + 1)

        def conv_end(k):
            return 3 * (k - k % 2) + 4 + k % 2

        @block.sync
        def _(sp):
            def load_x(s, q):
                sp.dma_start(x_sb[:, q], xs[s]).then_inc(x_loaded[q], 16)

            def store(s, c):
                sp.wait_ge(ob_done, at(s, NC, c))
                sp.dma_start(outs[s, c], ob[:, c % 2]).then_inc(stored[c % 2], 16)

            sp.wait_ge(zeroed, 1)
            with nc.allow_non_contiguous_dma(reason="small weights, once"):
                for dst, src in (
                    (raw_fc, w_fc.rearrange("(j p) n -> p j n", p=P)),
                    (raw_u[:, :, :], lr_u.rearrange("(j p) n -> p j n", p=P)),
                    (raw_v[:, :], lr_v),
                    (fbT[:, :], fast_b.rearrange("a b -> b a")),
                    (gate_bc[:, :], gate.rearrange("(a b) -> a b", a=1).to_broadcast([P, 1])),
                    (raw_in[:, 0:NT, :], in_proj_w[0:NT * P, :].rearrange("(j p) n -> p j n", p=P)),
                    (raw_in[0:NPROJ - NT * P, NT, :], in_proj_w[NT * P:NPROJ, :]),
                    (raw_out[:, :, :], out_proj_w.rearrange("(j p) n -> p j n", p=P)),
                    (raw_dn, w_proj.rearrange("(j p) n -> p j n", p=P)),
                    (nw[:, :], norm_w.rearrange("(j p) -> p j", p=P)),
                    (cw[:, :, :], conv_w.rearrange("(j p) o t -> p j (o t)", p=P)),
                    (cb[:, :], conv_b.rearrange("(j p) -> p j", p=P)),
                    (dtb[:, :], dt_bias.rearrange("(a b) -> a b", a=1).to_broadcast([P, NH])),
                    (alog[:, :, :].rearrange("p a b -> p (a b)"),
                     A_log.rearrange("a b -> (a b)").rearrange("(a b) -> a b", a=1).to_broadcast([P, 3 * NH])),
                    (d_bc[:, :], D.rearrange("(a b) -> a b", a=1).to_broadcast([P, NH])),
                ):
                    sp.dma_start(dst, src).then_inc(w_loaded, 16)
            load_x(0, 0)
            load_x(1, 1)
            with sp.Fori(0, S // 2 - 1) as i:
                for q in range(2):
                    s = i * 2 + q
                    sp.wait_ge(x2_done, at(s, NC, NC - 1))
                    load_x(s + 2, q)
                    for c in range(NC):
                        store(s, c)
            for s in range(S - 2, S):
                for c in range(NC):
                    store(s, c)
            for done in stored:
                sp.wait_ge(done, S * NC // 2 * 16)

        @block.gpsimd
        def _(pool):
            n = [0]

            def step(ins):
                n[0] += 1
                ins.then_inc(prep_pool, 1)
                pool.wait_ge(prep_pool, n[0])

            nc.gpsimd.memset(raw_in[:, NT, :], 0.0).then_inc(zeroed, 1)
            step(nc.gpsimd.memset(mhalf[:, :], -0.5))
            step(nc.gpsimd.memset(epsb[:, :], EPS))
            step(nc.gpsimd.memset(xsb[:, :], XS))
            step(nc.gpsimd.memset(epsd[:, :], EPS * DI))
            step(nc.gpsimd.memset(ones[:, :], 1.0))
            step(nc.gpsimd.memset(ident[:, :], 0.0))
            step(nc.gpsimd.affine_select(out=ident[:, :], in_=ident[:, :], compare_op=ALU.not_equal, fill=1.0,
                                         base=0, pattern=[[-1, P]], channel_multiplier=1))
            step(nc.gpsimd.affine_select(out=tri[:, :], in_=ones[:, :], compare_op=ALU.is_ge, fill=0.0,
                                         base=0, pattern=[[1, P]], channel_multiplier=-1))
            step(nc.gpsimd.tensor_copy(ident16[:, :], ident[:, :]))
            step(nc.gpsimd.tensor_copy(identb[:, :], ident[:, :]))
            step(nc.gpsimd.memset(above[:, :, :], 0.0))
            step(nc.gpsimd.affine_select(out=above[:, :, :], in_=above[:, :, :], compare_op=ALU.is_ge, fill=ABOVE,
                                         base=0, pattern=[[0, 4], [1, P]], channel_multiplier=-1))
            step(nc.gpsimd.memset(pick[:, :, :], 0.0))
            pk = pick[:, :, :].rearrange("k (c h) p -> k c h p", c=NC)
            for part in range(3):
                step(nc.gpsimd.affine_select(out=pk, in_=pk, compare_op=ALU.not_equal, fill=1.0,
                                             base=-part * NH, pattern=[[-3 * NH, NC], [-1, NH], [0, P]],
                                             channel_multiplier=1))
            pool.wait_ge(prep_dve, DVE_P2)
            step(nc.gpsimd.tensor_tensor(rp[:, :], p2[:, :], mhalf[:, 0:1].to_broadcast([P, NS]), ALU.pow))

            def input_stats(s):
                pool.wait_ge(mv1_done, at(s, NC, NC - 1))
                nc.gpsimd.tensor_tensor(va1[:, :], mv1[:, :, 1], epsb[:, :], ALU.add).then_inc(rs1_step, 1)
                pool.wait_ge(rs1_step, at(s, 3, 0))
                nc.gpsimd.tensor_tensor(rs1[:, :], va1[:, :], mhalf[:, :], ALU.pow).then_inc(rs1_step, 1)
                pool.wait_ge(rs1_step, at(s, 3, 1))
                nc.gpsimd.tensor_tensor(rs1s[:, :], rs1[:, :], xsb[:, :], ALU.mult).then_inc(rs1_step, 1)

            def input_low(s):
                pool.wait_ge(xh_done, at(s, 1, 0))
                nc.gpsimd.tensor_tensor(xl[:, :, :], xn[:, :, :], xh[:, :, :], ALU.subtract).then_inc(xl_done, 1)

            def x_state(s, q, c):
                if c == 0:
                    pool.wait_ge(dt_exp, at(s, 3, 2))
                pool.wait_ge(xdt_done, at(s, 2 * NC, 2 * c))
                nc.gpsimd.tensor_tensor(
                    Xst[:, c % 2].rearrange("p (h d) -> p h d", h=NH), Xdt[:, c % 2].rearrange("p (h d) -> p h d", h=NH),
                    ede[:, q, c].unsqueeze(2).to_broadcast([P, NH, HD]), ALU.mult).then_inc(xst_done, 1)

            def decay_state(s, q, c):
                pool.wait_ge(h_done, at(s, NC - 1, c - 1))
                nc.gpsimd.tensor_tensor(
                    hd[:, :].rearrange("p (h d) -> p h d", h=NH), hst[:, (c - 1) % 2].rearrange("p (h d) -> p h d", h=NH),
                    ecs[:, q, 1, c].unsqueeze(2).to_broadcast([P, NH, HD]), ALU.mult).then_inc(hd_done, 1)

            def add_skip(s, c):
                pool.wait_ge(ti_done, at(s, NC - 1, c - 1))
                pool.wait_ge(xdt_done, at(s, 2 * NC, 2 * c + 1))
                nc.gpsimd.tensor_tensor(ti2[:, :], ti[:, :], XD[:, c % 2], ALU.add).then_inc(ti2_done, 1)

            def rms(s, c):
                pool.wait_ge(ssq_done, at(s, NC, c))
                nc.gpsimd.tensor_tensor(rv[:, 0, c:c + 1], ssq[:, c:c + 1], epsd[:, :], ALU.add).then_inc(rv_step, 1)
                pool.wait_ge(rv_step, at(s, 3 * NC, 3 * c))
                nc.gpsimd.tensor_tensor(rv[:, 1, c:c + 1], rv[:, 0, c:c + 1], mhalf[:, 0:1], ALU.pow).then_inc(rv_step, 1)
                pool.wait_ge(rv_step, at(s, 3 * NC, 3 * c + 1))
                nc.gpsimd.tensor_tensor(rv[:, 2, c:c + 1], rv[:, 1, c:c + 1], g_gate[:, :], ALU.mult).then_inc(rv_step, 1)

            def gate_low(s, c):
                pool.wait_ge(ygh_done, at(s, NC, c))
                nc.gpsimd.tensor_tensor(ygl[:, c % 2], yg[:, c % 2], ygh[:, c % 2], ALU.subtract).then_inc(ygl_done, 1)

            def stats2(s, c):
                pool.wait_ge(mv2_done, at(s, NC, c))
                nc.gpsimd.tensor_tensor(rv2[:, 0, c:c + 1], mv2[:, c, 1:2], epsb[:, 0:1], ALU.add).then_inc(rv2_step, 1)
                pool.wait_ge(rv2_step, at(s, 3 * NC, 3 * c))
                nc.gpsimd.tensor_tensor(rv2[:, 1, c:c + 1], rv2[:, 0, c:c + 1], mhalf[:, 0:1], ALU.pow).then_inc(rv2_step, 1)
                pool.wait_ge(rv2_step, at(s, 3 * NC, 3 * c + 1))
                nc.gpsimd.tensor_tensor(rv2[:, 2, c:c + 1], rv2[:, 1, c:c + 1], xsb[:, 0:1], ALU.mult).then_inc(rv2_step, 1)

            def low2(s, c):
                pool.wait_ge(x2h_done, at(s, NC, c))
                nc.gpsimd.tensor_tensor(x2l[:, c % 2], xn2[:, c % 2], x2h[:, c % 2], ALU.subtract).then_inc(x2l_done, 1)

            def relu_low(s, j):
                pool.wait_ge(rh_done, at(s, NJ, j))
                nc.gpsimd.tensor_tensor(rT[:, LO, j], r2[:, j % 2], rT[:, HI, j], ALU.subtract).then_inc(rl_done, 1)

            def result(s, q, c):
                pool.wait_ge(ot_done, at(s, NC, c))
                if c >= 2:
                    pool.wait_ge(stored[c % 2], (s * (NC // 2) + c // 2) * 16)
                nc.gpsimd.tensor_tensor(ob[:, c % 2], ot[:, c % 2], x2[:, q, c], ALU.add).then_inc(ob_done, 1)

            def results_stored(s):
                for done in stored:
                    pool.wait_ge(done, (s + 1) * (NC // 2) * 16)

            def round_(s, q, ffn=True, nxt=True):
                if ffn:
                    low2(s - 1, 2)
                    stats2(s - 1, 3)
                    low2(s - 1, 3)
                    relu_low(s - 1, 0)
                if nxt:
                    input_stats(s + 1)
                if ffn:
                    relu_low(s - 1, 1)
                x_state(s, q, 0)
                if ffn:
                    relu_low(s - 1, 2)
                    relu_low(s - 1, 3)
                if nxt:
                    input_low(s + 1)
                if ffn:
                    relu_low(s - 1, 4)
                for c in range(NC):
                    if c:
                        add_skip(s, c)
                    if c >= 2:
                        low2(s, c - 2)
                    if c == 0 and ffn:
                        relu_low(s - 1, 5)
                    rms(s, c)
                    if c < NC - 2:
                        x_state(s, q, c + 1)
                    if c < NC - 2:
                        decay_state(s, q, c + 1)
                    gate_low(s, c)
                    if c:
                        stats2(s, c - 1)
                        if ffn:
                            result(s - 1, 1 - q, c - 1)
                if ffn:
                    result(s - 1, 1 - q, 3)
                    results_stored(s - 1)

            def finish(s, q):
                low2(s, 2)
                stats2(s, 3)
                low2(s, 3)
                for j in range(NLP):
                    relu_low(s, j)
                for c in range(NC):
                    result(s, q, c)

            input_stats(0)
            input_low(0)
            round_(0, 0, ffn=False)
            with pool.Fori(0, S // 2 - 1) as i:
                round_(i * 2 + 1, 1)
                round_(i * 2 + 2, 0)
            round_(S - 1, 1, nxt=False)
            finish(S - 1, 1)

        @block.scalar
        def _(act):
            n = [0]

            def step(ins):
                n[0] += 1
                ins.then_inc(prep_act, 1)

            act.wait_ge(w_loaded, 16 * NLOAD)
            for j in range(NJ):
                step(nc.scalar.activation(junk[:, 0:DM], raw_fc[:, j], ACT.Abs, accum_out=fcs[:, 0, j:j + 1]))
                act.wait_ge(prep_act, n[0])
            for j in range(KD):
                step(nc.scalar.activation(junk[:, 0:HID], raw_dn[:, j], ACT.Abs, accum_out=dns[:, 0, j:j + 1]))
                act.wait_ge(prep_act, n[0])
            for j in range(DI // P):
                step(nc.scalar.activation(junk[:, 0:DM], raw_in[:, j], ACT.Square, accum_out=mx[:, 1, j:j + 1]))
                act.wait_ge(prep_act, n[0])
            step(nc.scalar.activation(aexp[:, :, :].rearrange("p a b -> p (a b)"),
                                      alog[:, :, :].rearrange("p a b -> p (a b)"), ACT.Exp))
            assert n[0] == ACT_SUMS
            act.wait_ge(prep_dve, DVE_WEFF)
            for j in range(NJ):
                act.wait_ge(prep_act, n[0])
                step(nc.scalar.activation(junk[:, 0:DM], weff[:, j], ACT.Square, accum_out=mx[:, 4, j:j + 1]))
            assert n[0] == ACT_NORMS
            act.wait_ge(prep_dve, DVE_SCALES)
            for g, (_, w, high, _, sc) in enumerate(groups):
                act.wait_ge(prep_pe, PE_MXB + g + 1)
                if sc is None:
                    step(nc.scalar.activation(high, prep_banks[g % NB][:, 0:w], ACT.Copy))
                else:
                    step(nc.scalar.activation(high, prep_banks[g % NB][:, 0:w], ACT.Copy, scale=sw[:, sc:sc + 1]))
            assert n[0] == ACT_GROUPS
            step(nc.scalar.activation(w_o[:, HI, :, :].rearrange("p a b -> p (a b)"),
                                      wo32.rearrange("p a b -> p (a b)"), ACT.Copy, scale=sw[:, 2:3]))
            assert n[0] == ACT_ALL

            def input_high(s):
                act.wait_ge(xn_done, at(s, NC, NC - 1))
                nc.scalar.activation(xh[:, :, :].rearrange("p a b -> p (a b)"),
                                     xn[:, :, :].rearrange("p a b -> p (a b)"), ACT.Copy).then_inc(xh_done, 1)

            def input_copy(s, part):
                act.wait_ge(xT_ready, at(s, 2, part))
                nc.scalar.activation(xnT[:, part].rearrange("p a b -> p (a b)"), half(ps_t[1], KD * T),
                                     ACT.Copy).then_inc(xhT_copied if part == HI else xlT_copied, 1)

            def dt_exp_abs(s):
                act.wait_ge(dt_step, at(s, NDT, 1))
                nc.scalar.activation(dtw[:, 2], dtw[:, 1], ACT.Exp, scale=-1.0).then_inc(dt_exp, 1)

            def decays(s, q):
                act.wait_ge(dt_step, at(s, NDT, 18))
                nc.scalar.activation(ecs[:, q], ps_t[1][:, 0:2 * NC * NH].rearrange("p (a c h) -> p a c h", a=2, c=NC),
                                     ACT.Exp).then_inc(dt_exp, 1)
                nc.scalar.activation(ede[:, q], dtw[:, 6], ACT.Exp).then_inc(dt_exp, 1)

            def conv_init(s, k):
                m = CONV_ORDER[k]
                act.wait_ge(proj_done, at(s, len(PROJ), PROJ.index(("c", m))))
                if k >= 4:
                    act.wait_ge(xc_done, at(s, NM, k - 4))
                nc.scalar.activation(acc[:, k % 4], proj_banks[PROJ.index(("c", m)) % NPB][:, :], ACT.Identity,
                                     scale=cwu[:, m, 3:4], bias=cb[:, m:m + 1]).then_inc(acc_init, 1)

            def conv_silu(s, k):
                act.wait_ge(conv_step, at(s, 3 * NM, conv_end(k)))
                nc.scalar.activation(xc[:, CONV_ORDER[k]], acc[:, k % 4], ACT.Silu).then_inc(xc_done, 1)

            def gate_silu(s, c):
                act.wait_ge(proj_done, at(s, len(PROJ), PROJ.index(("z", c))))
                nc.scalar.activation(sz[:, c], proj_banks[PROJ.index(("z", c)) % NPB][:, :], ACT.Silu,
                                     scale=u_in[:, :]).then_inc(z_done, 1)

            def b_copy(s):
                act.wait_ge(bt_mm, at(s, 1, 0))
                nc.scalar.activation(Bt[:, :, :].rearrange("p a b -> p (a b)"), ps_t[0][:, :], ACT.Copy).then_inc(bt_copied, 1)

            def g_copy(s):
                act.wait_ge(g_mm, at(s, 1, 0))
                nc.scalar.activation(Gm[:, :, :].rearrange("p c t -> p (c t)"), ps_t[1][:, :], ACT.Copy).then_inc(g_done, 1)

            def gate_copy(s, c):
                act.wait_ge(yT_mm, at(s, NC, c))
                nc.scalar.activation(ygT[:, c % 2].rearrange("p a b t -> p (a b t)"), half(ps_t[1], 2 * DI),
                                     ACT.Copy).then_inc(yT_copied, 1)

            def decay_matrix(s, c, g):
                act.wait_ge(d_mm, at(s, 2 * NC, 2 * c + g))
                if c or g:
                    k = 2 * c + g
                    if k >= 2:
                        act.wait_ge(m_done, at(s, 2 * NC, k - 2))
                nc.scalar.activation(Lb[:, g], d_banks[g][:, :], ACT.Exp).then_inc(l_done, 1)

            def state_copy(s):
                act.wait_ge(state_mm, at(s, NC - 1, 0))
                nc.scalar.activation(hst[:, 0], ps_i[:, :], ACT.Copy).then_inc(h_done, 1)

            def square(s, c):
                act.wait_ge(y_done, at(s, NC, c))
                nc.scalar.activation(ysq[:, :], yb[:, c % 2], ACT.Square, accum_out=ssq[:, c:c + 1]).then_inc(ssq_done, 1)

            def gate_high(s, c):
                act.wait_ge(yg_done, at(s, NC, c))
                nc.scalar.activation(ygh[:, c % 2], yg[:, c % 2], ACT.Copy).then_inc(ygh_done, 1)

            def high2(s, c):
                act.wait_ge(xn2_done, at(s, NC, c))
                nc.scalar.activation(x2h[:, c % 2], xn2[:, c % 2], ACT.Copy).then_inc(x2h_done, 1)

            def copy2(s, q, c):
                act.wait_ge(x2T_mm, at(s, NC, c))
                nc.scalar.activation(xn2T[:, q, :, :, c * P:(c + 1) * P],
                                     half(ps_t[1], 2 * KD * P).rearrange("p (a b t) -> p a b t", a=2, b=KD),
                                     ACT.Copy).then_inc(x2T_copied, 1)

            def relu(s, j):
                act.wait_ge(up_mm, at(s, NJ, j))
                nc.scalar.activation(r[:, j % 2], up_banks[j][:, :], ACT.Relu, scale=u_relu[:, :]).then_inc(r_done, 1)

            def relu_high(s, j):
                act.wait_ge(r2_done, at(s, NJ, j))
                nc.scalar.activation(rT[:, HI, j], r2[:, j % 2], ACT.Copy).then_inc(rh_done, 1)

            def round_(s, q, ffn=True, nxt=True):
                if ffn:
                    gate_copy(s - 1, 3)
                    high2(s - 1, 2)
                conv_init(s, 2)
                conv_init(s, 3)
                conv_silu(s, 0)
                conv_silu(s, 1)
                if ffn:
                    copy2(s - 1, 1 - q, 2)
                conv_init(s, 4)
                gate_silu(s, 0)
                conv_init(s, 5)
                if ffn:
                    high2(s - 1, 3)
                conv_silu(s, 2)
                conv_silu(s, 3)
                gate_silu(s, 1)
                if ffn:
                    copy2(s - 1, 1 - q, 3)
                gate_silu(s, 2)
                if ffn:
                    relu(s - 1, 0)
                conv_silu(s, 4)
                conv_silu(s, 5)
                gate_silu(s, 3)
                if ffn:
                    relu_high(s - 1, 0)
                    relu(s - 1, 1)
                b_copy(s)
                g_copy(s)
                if ffn:
                    relu_high(s - 1, 1)
                    relu(s - 1, 2)
                decay_matrix(s, 0, 0)
                decay_matrix(s, 0, 1)
                if ffn:
                    relu_high(s - 1, 2)
                    relu(s - 1, 3)
                    relu(s - 1, 4)
                    relu_high(s - 1, 3)
                if nxt:
                    input_high(s + 1)
                if ffn:
                    relu_high(s - 1, 4)
                for c in range(NC):
                    if c >= 2:
                        high2(s, c - 2)
                    if c < NC - 1:
                        decay_matrix(s, c + 1, 0)
                    if c == 2 and nxt:
                        dt_exp_abs(s + 1)
                    if c == 0 and ffn:
                        relu(s - 1, 5)
                    if c and c < NC - 1:
                        decay_matrix(s, c + 1, 1)
                    square(s, c)
                    if c == 0:
                        decay_matrix(s, c + 1, 1)
                    if c:
                        gate_copy(s, c - 1)
                        if c == 3 and nxt:
                            conv_init(s + 1, 0)
                            conv_init(s + 1, 1)
                    else:
                        if ffn:
                            relu_high(s - 1, 5)
                        if nxt:
                            input_copy(s + 1, HI)
                        state_copy(s)
                        if ffn:
                            relu(s - 1, 6)
                            relu_high(s - 1, 6)
                            relu(s - 1, 7)
                    if c == 3 and nxt:
                        decays(s + 1, 1 - q)
                    gate_high(s, c)
                    if c == 0:
                        if ffn:
                            relu_high(s - 1, 7)
                        if nxt:
                            input_copy(s + 1, LO)
                    if c >= 2:
                        copy2(s, q, c - 2)

            def finish(s, q):
                gate_copy(s, 3)
                high2(s, 2)
                copy2(s, q, 2)
                high2(s, 3)
                copy2(s, q, 3)
                for j in range(NJ):
                    relu(s, j)
                    relu_high(s, j)

            act.wait_ge(prep_dve, DVE_ALL)
            input_high(0)
            input_copy(0, HI)
            input_copy(0, LO)
            dt_exp_abs(0)
            decays(0, 0)
            conv_init(0, 0)
            conv_init(0, 1)
            round_(0, 0, ffn=False)
            with act.Fori(0, S // 2 - 1) as i:
                round_(i * 2 + 1, 1)
                round_(i * 2 + 2, 0)
            round_(S - 1, 1, nxt=False)
            finish(S - 1, 1)

        @block.vector
        def _(dve):
            n = [0]

            def step(ins):
                n[0] += 1
                ins.then_inc(prep_dve, 1)
                dve.wait_ge(prep_dve, n[0])

            V = nc.vector
            dve.wait_ge(w_loaded, 16 * NLOAD)
            dve.wait_ge(prep_pool, POOL_CONST)
            step(V.tensor_reduce(mx[:, 0, 0:1], raw_in[:, :, :].rearrange("p a b -> p (a b)"), AX_X, ALU.max,
                                 apply_absolute_value=True))
            dve.wait_ge(prep_pe, PE_FV)
            step(V.tensor_copy(fv[:, :], ps_f[0:RANK, 0:DM]))
            dve.wait_ge(prep_pe, PE_UT)
            step(V.tensor_copy(uT[:, 0:4, :].rearrange("p a b -> p (a b)"), ps_y[0:RANK, :]))
            step(V.tensor_copy(uT[:, 4:8, :].rearrange("p a b -> p (a b)"), ps_i[0:RANK, :]))
            assert n[0] == DVE_UT
            dve.wait_ge(prep_act, ACT_SUMS)
            step(V.tensor_scalar(fcs[:, 1, :], fcs[:, 0, :], 1.0 / DM, 1e-5, ALU.mult, ALU.max))
            step(V.tensor_scalar(fcs[:, 2, :], fcs[:, 1, :], 0.5, None, ALU.mult))
            step(V.tensor_scalar(fcs[:, 3, :], fcs[:, 1, :], -0.5, None, ALU.mult))
            for j in range(NJ):
                step(V.tensor_scalar(tern_a[:, j], raw_fc[:, j], fcs[:, 2, j:j + 1], fcs[:, 1, j:j + 1], ALU.is_gt, ALU.mult))
                step(V.tensor_scalar(tern_b[:, 0:DM], raw_fc[:, j], fcs[:, 3, j:j + 1], fcs[:, 1, j:j + 1], ALU.is_lt, ALU.mult))
                step(V.tensor_tensor(tern_a[:, j], tern_a[:, j], tern_b[:, 0:DM], ALU.subtract))
                dve.wait_ge(prep_pe, PE_UT + j + 1)
                step(V.scalar_tensor_tensor(weff[:, j], ps_proj[j % 2][:, 0:DM], gate_bc[:, :], tern_a[:, j], ALU.mult, ALU.add))
            assert n[0] == DVE_WEFF, n[0]
            step(V.tensor_reduce(mx[:, 3, 0:1], weff.rearrange("p a b -> p (a b)"), AX_X, ALU.max, apply_absolute_value=True))
            step(V.tensor_scalar(dns[:, 1, :], dns[:, 0, :], 1.0 / HID, 1e-5, ALU.mult, ALU.max))
            step(V.tensor_scalar(dns[:, 2, :], dns[:, 1, :], 0.5, None, ALU.mult))
            step(V.tensor_scalar(dns[:, 3, :], dns[:, 1, :], -0.5, None, ALU.mult))
            for j in range(KD):
                step(V.tensor_scalar(tern_b[:, 0:HID], raw_dn[:, j], dns[:, 3, j:j + 1], None, ALU.is_lt))
                step(V.scalar_tensor_tensor(raw_dn[:, j], raw_dn[:, j], dns[:, 2, j:j + 1], tern_b[:, 0:HID], ALU.is_gt, ALU.subtract))
                step(V.tensor_scalar(dnd[:, j], ident[:, :], dns[:, 1, j:j + 1], None, ALU.mult))
            for g in range(2):
                dve.wait_ge(prep_pe, PE_WO + g)
                for k in range(2):
                    m = 2 * g + k
                    step(V.tensor_scalar(wo32[:, m], [ps_y, ps_i][g][:, k * DM:(k + 1) * DM], nw[:, m:m + 1], None, ALU.mult))
            step(V.tensor_reduce(mx[:, 2, 0:1], wo32.rearrange("p a b -> p (a b)"), AX_X, ALU.max, apply_absolute_value=True))
            dve.wait_ge(prep_act, ACT_NORMS)
            for k in (0, 2, 3):
                step(V.tensor_copy(mxa[:, k:k + 1], mx[:, k, 0:1]))
            step(V.tensor_reduce(mxa[:, 1:2], mx[:, 1, 0:DI // P], AX_X, ALU.max))
            step(V.tensor_reduce(mxa[:, 4:5], mx[:, 4, 0:NJ], AX_X, ALU.max))
            assert n[0] == DVE_MX, n[0]
            dve.wait_ge(prep_pe, PE_MX)
            step(V.tensor_reduce(mxm[:, :], ps_d[0:NS, 0:P], AX_X, ALU.max))
            step(V.tensor_scalar(mxd[:, :], ident[0:NS, 0:NS], mxm[:, :], None, ALU.mult))
            assert n[0] == DVE_MXD, n[0]
            dve.wait_ge(prep_pe, PE_MXB)
            step(V.tensor_scalar(mxb[:, :], ps_d[:, 0:NS], 1e-30, None, ALU.max))
            step(V.tensor_scalar(p2[:, :].bitcast(I32), mxb[:, :].bitcast(I32), 0x7F800000, None, ALU.bitwise_and))
            assert n[0] == DVE_P2, n[0]
            step(V.reciprocal(ip2[:, :], p2[:, :]))
            step(V.tensor_scalar(sw[:, :], ip2[:, :], 8192.0, None, ALU.mult))
            assert n[0] == DVE_SCALES, n[0]
            step(V.tensor_scalar(u_in[:, :], p2[:, 0:1], 1.0 / 8192 / XS, None, ALU.mult))
            dve.wait_ge(prep_pool, POOL_ALL)
            step(V.tensor_scalar(g_gate[:, :], rp[:, 1:2], 64.0 * DI ** 0.5, None, ALU.mult))
            step(V.tensor_scalar(mx[:, 5, 0:1], g_gate[:, :], sw[:, 2:3], DI ** -0.5, ALU.mult, ALU.mult))
            step(V.reciprocal(u_out[:, :], mx[:, 5, 0:1]))
            step(V.tensor_scalar(mx[:, 5, 1:2], rp[:, 4:5], 8.0, None, ALU.mult))
            step(V.tensor_scalar(u_relu[:, :], p2[:, 3:4], 1.0 / 8192 / XS, mx[:, 5, 1:2], ALU.mult, ALU.mult))
            step(V.tensor_scalar(mx[:, 5, 2:3], mx[:, 5, 1:2], mx[:, 5, 1:2], None, ALU.mult))
            step(V.reciprocal(mx[:, 5, 3:4], mx[:, 5, 2:3]))
            step(V.tensor_scalar(dn_bc[:, :], ps_f[:, 0:DM], mx[:, 5, 3:4], None, ALU.mult))
            step(V.tensor_tensor(a_neg[:, :], aexp[:, 0, :], aexp[:, 1, :], ALU.add))
            step(V.tensor_tensor(a_neg[:, :], a_neg[:, :], aexp[:, 2, :], ALU.add))
            step(V.tensor_scalar(a_neg[:, :], a_neg[:, :], -1.0 / 3, None, ALU.mult))
            step(V.tensor_scalar(cwu[:, :, :].rearrange("p a b -> p (a b)"), cw[:, :, :].rearrange("p a b -> p (a b)"),
                                 u_in[:, :], None, ALU.mult))
            assert n[0] == DVE_LOW, n[0]
            for g, (_, w, high, low, sc) in enumerate(groups):
                if sc is not None:
                    dve.wait_ge(prep_act, ACT_NORMS + g + 1)
                    step(V.scalar_tensor_tensor(low, prep_banks[g % NB][:, 0:w], sw[:, sc:sc + 1], high,
                                                ALU.mult, ALU.subtract))
            dve.wait_ge(prep_act, ACT_ALL)
            step(V.scalar_tensor_tensor(w_o[:, LO, :, :].rearrange("p a b -> p (a b)"),
                                        wo32.rearrange("p a b -> p (a b)"), sw[:, 2:3],
                                        w_o[:, HI, :, :].rearrange("p a b -> p (a b)"), ALU.mult, ALU.subtract))
            assert n[0] == DVE_ALL, n[0]

            def input_stats(s, q):
                dve.wait_ge(x_loaded[q], s * 8 + (8 if q else 16))
                for c in range(NC):
                    V.bn_stats(st1[:, c], x_sb[:, q, c]).then_inc(st1_done, 1)
                dve.wait_ge(st1_done, at(s, NC, NC - 1))
                V.memset(pause[:, :], 0.0)
                for c in range(NC):
                    V.bn_aggr(mv1[:, c], st1[:, c]).then_inc(mv1_done, 1)

            def input_norm(s, q):
                dve.wait_ge(rs1_step, at(s, 3, 2))
                if type(s) is not int or s:
                    dve.wait_ge(xl_done, at(s - 1, 1, 0))
                for c in range(NC):
                    V.tensor_scalar(xn[:, c], x_sb[:, q, c], mv1[:, c, 0:1], rs1s[:, c:c + 1],
                                    ALU.subtract, ALU.mult).then_inc(xn_done, 1)

            DX, AXX, EX, RX, S1, Q1, DE, PL, A1 = range(9)

            def w(k):
                return dtw[:, k]

            def heads(t):
                return t[:, :].unsqueeze(1).to_broadcast([P, NC, NH])

            def dt_steps(s, q, k0, k1):
                raw = ps_t[0][:, 0:NC * NH].rearrange("p (c h) -> p c h", c=NC)
                cum = ps_t[1][:, 0:NC * NH].rearrange("p (c h) -> p c h", c=NC)
                tot = ps_t[1][:, NC * NH:2 * NC * NH].rearrange("p (c h) -> p c h", c=NC)
                rows = ps_t[0][:, :].bitcast(BF16)[0:NR, 0:P]
                for k in range(k0, k1):
                    if k == 0:
                        dve.wait_ge(dt_mm, at(s, 1, 0))
                    elif k == 17:
                        dve.wait_ge(dt_mm2, at(s, 2, 0))
                    elif k == 23:
                        dve.wait_ge(dt_mm2, at(s, 2, 1))
                    else:
                        if k == 3:
                            dve.wait_ge(dt_exp, at(s, 3, 0))
                        dve.wait_ge(dt_step, at(s, NDT, k - 1))
                    if k == 0:
                        i = V.scalar_tensor_tensor(w(DX), raw, u_in[:, :], heads(dtb), ALU.mult, ALU.add)
                    elif k == 1:
                        i = V.scalar_tensor_tensor(w(AXX), w(DX), -1.0, w(DX), ALU.mult, ALU.max)
                    elif k == 2:
                        i = V.tensor_scalar(w(RX), w(DX), 0.0, None, ALU.max)
                    elif k == 3:
                        i = V.tensor_scalar(w(S1), w(EX), 2.0, None, ALU.add)
                    elif k == 4:
                        i = V.reciprocal(w(Q1), w(S1))
                    elif k == 5:
                        i = V.tensor_tensor(w(S1), w(EX), w(Q1), ALU.mult)
                    elif k == 6:
                        i = V.tensor_tensor(w(Q1), w(S1), w(S1), ALU.mult)
                    elif k == 7:
                        i = V.tensor_scalar(w(PL), w(Q1), 1.0 / 13, None, ALU.mult)
                    elif k < 13:
                        i = V.scalar_tensor_tensor(w(PL), w(PL), 1.0 / (11, 9, 7, 5, 3)[k - 8], w(Q1), ALU.add, ALU.mult)
                    elif k == 13:
                        i = V.scalar_tensor_tensor(w(PL), w(PL), 1.0, w(S1), ALU.add, ALU.mult)
                    elif k == 14:
                        i = V.scalar_tensor_tensor(dt_[:, q], w(PL), 2.0, w(RX), ALU.mult, ALU.add)
                    elif k == 15:
                        i = V.tensor_tensor(w(A1), dt_[:, q], heads(a_neg), ALU.mult)
                    elif k == 16:
                        i = V.tensor_scalar(w(A1), w(A1), FLOOR, None, ALU.max)
                    elif k == 17:
                        i = V.tensor_copy(w(PL), cum)
                    elif k == 18:
                        i = V.tensor_tensor(w(DE), tot, w(PL), ALU.subtract)
                    elif k == 19:
                        i = V.tensor_copy(cp3[:, :, 0, :], w(PL))
                    elif k == 20:
                        i = V.tensor_tensor(w(RX), w(PL), cp3[:, :, 0, :], ALU.subtract)
                    elif k == 21:
                        i = V.tensor_copy(cp3[:, :, 1, :], w(RX))
                    elif k == 22:
                        i = V.tensor_tensor(cp3[:, :, 2, :], w(RX), cp3[:, :, 1, :], ALU.subtract)
                    elif k == 23:
                        i = V.tensor_copy(cT[:, q], rows)
                    else:
                        i = V.tensor_scalar(ncT[:, q], rows, -1.0, None, ALU.mult)
                    i.then_inc(dt_step, 1)

            def conv(s, k, taps=(1, 2, 3)):
                for d in taps:
                    for a in (0, 1):
                        m = CONV_ORDER[k + a]
                        if d == 1:
                            dve.wait_ge(acc_init, at(s, NM, k + a))
                        else:
                            dve.wait_ge(conv_step, at(s, 3 * NM, 3 * k + 2 * (d - 2) + a))
                        V.scalar_tensor_tensor(
                            acc[:, (k + a) % 4, d:T], proj_banks[PROJ.index(("c", m)) % NPB][:, 0:T - d],
                            cwu[:, m, 3 - d:4 - d], acc[:, (k + a) % 4, d:T], ALU.mult, ALU.add).then_inc(conv_step, 1)

            def weigh(s, c, g):
                if c == 0 and g == 0:
                    dve.wait_ge(g_done, at(s, 1, 0))
                dve.wait_ge(l_done, at(s, 2 * NC, 2 * c + g))
                if c >= 2:
                    dve.wait_ge(intra_mm, at(s, NC, c - 2))
                V.tensor_tensor(Mb[:, 2 * (c % 2) + g], Lb[:, g].rearrange("p (h t) -> p h t", h=4),
                                Gm[:, c].unsqueeze(1).to_broadcast([P, 4, P]), ALU.mult).then_inc(m_done, 1)

            def x_tokens(s, q, c):
                xt = ps_t[0][:, :].rearrange("p (h d) -> p h d", h=NH)
                dve.wait_ge(xt_mm, at(s, NC, c))
                if c >= 2:
                    dve.wait_ge(intra_mm, at(s, NC, c - 2))
                    dve.wait_ge(xst_done, at(s, NC - 1, c - 2))
                V.tensor_tensor(Xdt[:, c % 2].rearrange("p (h d) -> p h d", h=NH), xt,
                                dt_[:, q, c].unsqueeze(2).to_broadcast([P, NH, HD]), ALU.mult).then_inc(xdt_done, 1)

            def skip(s, q, c):
                xt = ps_t[0][:, :].rearrange("p (h d) -> p h d", h=NH)
                V.tensor_tensor(XD[:, c % 2].rearrange("p (h d) -> p h d", h=NH), xt,
                                d_bc[:, :].unsqueeze(2).to_broadcast([P, NH, HD]), ALU.mult).then_inc(xdt_done, 1)

            def from_state(s, q, c):
                dve.wait_ge(inter_mm, at(s, NC - 1, c - 1))
                V.tensor_tensor(ti[:, :].rearrange("p (h d) -> p h d", h=NH), ps_i[:, :].rearrange("p (h d) -> p h d", h=NH),
                                ecs[:, q, 0, c].unsqueeze(2).to_broadcast([P, NH, HD]), ALU.mult).then_inc(ti_done, 1)

            def y_sum(s, c):
                dve.wait_ge(intra_mm, at(s, NC, c))
                if c:
                    dve.wait_ge(ti2_done, at(s, NC - 1, c - 1))
                else:
                    dve.wait_ge(xdt_done, at(s, 2 * NC, 1))
                V.tensor_tensor(yb[:, c % 2], ps_y[:, :], ti2[:, :] if c else XD[:, 0], ALU.add).then_inc(y_done, 1)

            def next_state(s, c):
                dve.wait_ge(state_mm, at(s, NC - 1, c))
                dve.wait_ge(hd_done, at(s, NC - 2, c - 1))
                V.tensor_tensor(hst[:, c % 2], ps_i[:, :], hd[:, :], ALU.add).then_inc(h_done, 1)

            def gated(s, c):
                dve.wait_ge(rv_step, at(s, 3 * NC, 3 * c + 2))
                if c == 0:
                    dve.wait_ge(z_done, at(s, NC, NC - 1))
                V.scalar_tensor_tensor(yg[:, c % 2], yb[:, c % 2], rv[:, 2, c:c + 1], sz[:, c], ALU.mult,
                                       ALU.mult).then_inc(yg_done, 1)

            def residual(s, q, c):
                dve.wait_ge(o_mm, at(s, NC, c))
                V.scalar_tensor_tensor(x2[:, q, c], ps_t[0][:, 0:DM], u_out[:, :], x_sb[:, q, c], ALU.mult,
                                       ALU.add).then_inc(x2_done, 1)

            def moments(s, q, c):
                dve.wait_ge(x2_done, at(s, NC, c))
                V.bn_stats(st2[:, c], x2[:, q, c]).then_inc(st2_done, 1)

            def moments_sum(s, q, c):
                dve.wait_ge(st2_done, at(s, NC, c))
                V.memset(pause[:, :], 0.0)
                V.bn_aggr(mv2[:, c], st2[:, c]).then_inc(mv2_done, 1)

            def norm2(s, q, c):
                dve.wait_ge(rv2_step, at(s, 3 * NC, 3 * c + 2))
                V.tensor_scalar(xn2[:, c % 2], x2[:, q, c], mv2[:, c, 0:1], rv2[:, 2, c:c + 1],
                                ALU.subtract, ALU.mult).then_inc(xn2_done, 1)

            def relu_square(s, j):
                dve.wait_ge(r_done, at(s, NJ, j))
                if j >= 2:
                    dve.wait_ge(rl_done, at(s, NLP, j - 2))
                V.tensor_tensor(r2[:, j % 2], r[:, j % 2], r[:, j % 2], ALU.mult).then_inc(r2_done, 1)

            def relu_low(s, j):
                dve.wait_ge(rh_done, at(s, NJ, j))
                V.tensor_tensor(rT[:, LO, j], r2[:, j % 2], rT[:, HI, j], ALU.subtract).then_inc(rlv_done, 1)

            def down_scale(s, c):
                dve.wait_ge(dn_mm, at(s, NC, c))
                if c >= 2:
                    dve.wait_ge(ob_done, at(s, NC, c - 2))
                V.tensor_tensor(ot[:, c % 2], down_banks[c % 2][:, 0:DM], dn_bc[:, :], ALU.mult).then_inc(ot_done, 1)

            def round_(s, q, ffn=True, nxt=True):
                p = 1 - q
                dt_steps(s, q, 23, 25)
                if ffn:
                    norm2(s - 1, p, 2)
                conv(s, 2, (1,))
                if ffn:
                    residual(s - 1, p, 3)
                    moments(s - 1, p, 3)
                    moments_sum(s - 1, p, 3)
                conv(s, 2, (2, 3))
                if ffn:
                    norm2(s - 1, p, 3)
                conv(s, 4)
                if nxt:
                    input_stats(s + 1, p)
                if ffn:
                    relu_square(s - 1, 0)
                    relu_square(s - 1, 1)
                if ffn:
                    relu_square(s - 1, 2)
                x_tokens(s, q, 0)
                weigh(s, 0, 0)
                weigh(s, 0, 1)
                skip(s, q, 0)
                if ffn:
                    relu_square(s - 1, 3)
                if nxt:
                    input_norm(s + 1, p)
                if ffn:
                    relu_square(s - 1, 4)
                dt = (lambda k0, k1: dt_steps(s + 1, p, k0, k1)) if nxt else (lambda k0, k1: None)
                for c in range(NC - 1):
                    if c:
                        from_state(s, q, c)
                    if c == 1 and ffn:
                        for j in range(NLP, NJ):
                            relu_low(s - 1, j)
                    if c == 2:
                        dt(0, 2)
                        norm2(s, q, 0)
                        dt(2, 3)
                    if c:
                        weigh(s, c + 1, 0)
                    y_sum(s, c)
                    if c == 0:
                        weigh(s, 1, 0)
                        if ffn:
                            relu_square(s - 1, 5)
                    if c == 2:
                        dt(3, 4)
                    weigh(s, c + 1, 1)
                    if c == 2:
                        dt(4, 5)
                    if c:
                        next_state(s, c)
                    if c == 2:
                        dt(5, 6)
                    x_tokens(s, q, c + 1)
                    skip(s, q, c + 1)
                    if c == 2:
                        dt(6, 7)
                    if c == 0 and ffn:
                        relu_square(s - 1, 6)
                    gated(s, c)
                    if c == 0 and ffn:
                        relu_square(s - 1, 7)
                    if c == 2:
                        dt(7, 8)
                    if c:
                        if ffn:
                            down_scale(s - 1, c - 1)
                        if c == 2:
                            dt(8, 9)
                        residual(s, q, c - 1)
                        if c == 2:
                            dt(9, 10)
                        moments(s, q, c - 1)
                        if c == 2:
                            dt(10, 11)
                        moments_sum(s, q, c - 1)
                        if c == 2:
                            dt(11, 12)
                from_state(s, q, 3)
                dt(12, 13)
                norm2(s, q, 1)
                dt(13, 14)
                y_sum(s, 3)
                dt(14, 17)
                gated(s, 3)
                if nxt:
                    conv(s + 1, 0, (1,))
                dt(17, 19)
                if ffn:
                    down_scale(s - 1, 2)
                dt(19, 20)
                residual(s, q, 2)
                dt(20, 21)
                moments(s, q, 2)
                dt(21, 23)
                moments_sum(s, q, 2)
                if nxt:
                    conv(s + 1, 0, (2, 3))
                if ffn:
                    down_scale(s - 1, 3)

            def finish(s, q):
                norm2(s, q, 2)
                residual(s, q, 3)
                moments(s, q, 3)
                moments_sum(s, q, 3)
                norm2(s, q, 3)
                for j in range(NJ):
                    relu_square(s, j)
                for j in range(NLP, NJ):
                    relu_low(s, j)
                for c in range(NC):
                    down_scale(s, c)

            input_stats(0, 0)
            input_norm(0, 0)
            dt_steps(0, 0, 0, 23)
            conv(0, 0)
            round_(0, 0, ffn=False)
            with dve.Fori(0, S // 2 - 1) as i:
                round_(i * 2 + 1, 1)
                round_(i * 2 + 2, 0)
            round_(S - 1, 1, nxt=False)
            finish(S - 1, 1)

        @block.tensor
        def _(pe):
            n = [0]

            def step(ins):
                n[0] += 1
                ins.then_inc(prep_pe, 1)

            mm, tr = nc.tensor.matmul, nc.tensor.transpose
            pe.wait_ge(w_loaded, 16 * NLOAD)
            pe.wait_ge(prep_pool, POOL_CONST)
            step(mm(ps_f[0:RANK, 0:DM], fbT[:, :], raw_v[:, :], start=True, stop=True))
            assert n[0] == PE_FV
            for j in range(NJ):
                step(tr([ps_y, ps_i][j // 4][0:RANK, (j % 4) * P:(j % 4 + 1) * P], raw_u[:, j, :], ident[:, :]))
            assert n[0] == PE_UT
            pe.wait_ge(prep_dve, DVE_UT)
            for j in range(NJ):
                if j >= 2:
                    pe.wait_ge(prep_dve, DVE_TERN + 4 * (j - 1))
                step(mm(ps_proj[j % 2][:, 0:DM], uT[:, j, :], fv[:, :], start=True, stop=True))
            for g in range(2):
                for k in range(2):
                    for j in range(KD):
                        i = tr([ps_y, ps_i][g][:, k * DM + j * P:k * DM + (j + 1) * P],
                               raw_out[:, j, (2 * g + k) * P:(2 * g + k + 1) * P], ident[:, :])
                step(i)
            assert n[0] == PE_WO + 1, n[0]
            pe.wait_ge(prep_dve, DVE_MX)
            for j in range(KD):
                i = mm(ps_f[:, j * P:(j + 1) * P], ones[:, :], dnd[:, j], start=True, stop=True)
            step(i)
            step(tr(ps_d[0:NS, 0:P], mxa[:, :], ident[:, :]))
            assert n[0] == PE_MX, n[0]
            pe.wait_ge(prep_dve, DVE_MXD)
            step(mm(ps_d[:, 0:NS], ones[0:NS, :], mxd[:, :], start=True, stop=True))
            assert n[0] == PE_MXB, n[0]
            for g, (src, _, _, _, _) in enumerate(groups):
                if g >= NB:
                    if groups[g - NB][4] is None:
                        pe.wait_ge(prep_act, ACT_NORMS + g - NB + 1)
                    else:
                        pe.wait_ge(prep_dve, DVE_LOW + g - NB + 1)
                for k, a in enumerate(src):
                    rows = a.shape[0]
                    i = tr(prep_banks[g % NB][:, k * P:k * P + rows], a, ident[0:rows, 0:rows])
                step(i)
            pe.wait_ge(prep_dve, DVE_ALL)
            pe.wait_ge(prep_act, ACT_ALL)

            def input_transpose(s, part):
                pe.wait_ge(xh_done if part == HI else xl_done, at(s, 1, 0))
                for k in range(KD):
                    for c in range(NC):
                        i = tr(half(ps_t[1], KD * T)[:, k * T + c * P:k * T + (c + 1) * P],
                               (xh if part == HI else xl)[:, c, k * P:(k + 1) * P], ident16[:, :])
                i.then_inc(xT_ready, 1)

            def three(ps, lhs, rhs, kk):
                for a, (wp, xp) in enumerate(PASSES):
                    for k in range(kk):
                        i = mm(ps, lhs(wp, xp, k), rhs(wp, xp, k), start=(a == 0 and k == 0),
                               stop=(a == 2 and k == kk - 1))
                return i

            def dt_product(s):
                pe.wait_ge(xhT_copied, at(s, 1, 0))
                pe.wait_ge(xlT_copied, at(s, 1, 0))
                for c in range(NC):
                    i = three(ps_t[0][:, c * NH:(c + 1) * NH],
                              lambda wp, xp, k: xnT[:, xp, k, c * P:(c + 1) * P],
                              lambda wp, xp, k: w_in[:, wp, k, NPROJ - NH:NPROJ], KD)
                i.then_inc(dt_mm, 1)

            def cumulate(s):
                pe.wait_ge(dt_step, at(s, NDT, 16))
                a = dtw[:, 8].rearrange("p c h -> p (c h)")
                mm(ps_t[1][:, 0:NC * NH], tri[:, :], a, start=True, stop=True)
                mm(ps_t[1][:, NC * NH:2 * NC * NH], ones[:, :], a, start=True, stop=True).then_inc(dt_mm2, 1)

            def cum_rows(s):
                pe.wait_ge(dt_step, at(s, NDT, 22))
                tr(ps_t[0][:, :].bitcast(BF16)[0:NR, 0:P], cp3[:, :, :, :].rearrange("p a b c -> p (a b c)"),
                   identb[:, :]).then_inc(dt_mm2, 1)

            def project(s, k):
                kind, m = PROJ[k]
                if k >= NPB:
                    kind2, m2 = PROJ[k - NPB]
                    if kind2 == "c":
                        pe.wait_ge(conv_step, at(s, 3 * NM, conv_end(CONV_ORDER.index(m2))))
                    else:
                        pe.wait_ge(z_done, at(s, NC, m2))
                elif type(s) is not int or s:
                    if k == 0:
                        pe.wait_ge(l_done, at(s - 1, 2 * NC, 2 * NC - 1))
                    elif k == 2:
                        pe.wait_ge(dt_step, at(s, NDT, 24))
                    elif k == 3:
                        pe.wait_ge(y_done, at(s - 1, NC, NC - 1))
                    elif k == 4:
                        pe.wait_ge(ti_done, at(s - 1, NC - 1, NC - 2))
                if kind == "c":
                    i = three(proj_banks[k % NPB][:, :], lambda wp, xp, kk: w_in[:, wp, kk, DI + m * P:DI + (m + 1) * P],
                              lambda wp, xp, kk: xnT[:, xp, kk, :], KD)
                else:
                    i = three(proj_banks[k % NPB][:, :], lambda wp, xp, kk: xnT[:, xp, kk, m * P:(m + 1) * P],
                              lambda wp, xp, kk: w_in[:, wp, kk, 0:DI], KD)
                i.then_inc(proj_done, 1)

            XB, XC = 4, 5

            def b_transpose(s):
                pe.wait_ge(xc_done, at(s, NM, 0))
                for c in range(NC):
                    i = tr(ps_t[0][:, c * P:(c + 1) * P], xc[:, XB, c * P:(c + 1) * P], ident[:, :])
                i.then_inc(bt_mm, 1)

            def g_product(s):
                pe.wait_ge(xc_done, at(s, NM, 1))
                for c in range(NC):
                    i = mm(ps_t[1][:, c * P:(c + 1) * P], xc[:, XB, c * P:(c + 1) * P], xc[:, XC, c * P:(c + 1) * P],
                           start=True, stop=True)
                i.then_inc(g_mm, 1)

            def decay_logs(s, q, c, g):
                if c == 0:
                    pe.wait_ge(dt_step, at(s, NDT, 24))
                    pe.wait_ge(z_done, at(s, NC, NC - 1))
                    pe.wait_ge(xc_done, at(s, NM, NM - 1))
                else:
                    pe.wait_ge(l_done, at(s, 2 * NC, 2 * c + g - 2))
                rows = pick[:, c * NH + 4 * g:c * NH + 4 * g + 4, :]
                for h in range(4):
                    mm(d_banks[g][:, h * P:(h + 1) * P], pick[:, c * NH + 4 * g + h, :], cT[:, q], start=(h == 0), stop=False)
                mm(d_banks[g][:, :], identb[:, :], above[:, :, :].rearrange("p h t -> p (h t)"), start=False, stop=False)
                mm(d_banks[g][:, :], ncT[:, q], rows.rearrange("k h p -> k (h p)"), start=False, stop=True).then_inc(d_mm, 1)

            def x_transpose(s, c, nxt=True):
                if c == 0:
                    pe.wait_ge(bt_copied, at(s, 1, 0))
                    pe.wait_ge(xc_done, at(s, NM, NM - 1))
                elif c < 3:
                    pe.wait_ge(xdt_done, at(s, 2 * NC, 2 * c - 1))
                elif nxt:
                    pe.wait_ge(dt_step, at(s + 1, NDT, 0))
                else:
                    pe.wait_ge(x2_done, at(s, NC, 0))
                for m in range(DI // P):
                    i = tr(ps_t[0][:, m * P:(m + 1) * P], xc[:, m, c * P:(c + 1) * P], ident[:, :])
                i.then_inc(xt_mm, 1)

            def intra(s, c):
                pe.wait_ge(m_done, at(s, 2 * NC, 2 * c + 1))
                pe.wait_ge(xdt_done, at(s, 2 * NC, 2 * c))
                if c:
                    pe.wait_ge(y_done, at(s, NC, c - 1))
                elif type(s) is not int or s:
                    pe.wait_ge(y_done, at(s - 1, NC, NC - 1))
                for h in range(NH):
                    i = mm(ps_y[:, h * HD:(h + 1) * HD], Mb[:, 2 * (c % 2) + h // 4, h % 4, :],
                           Xdt[:, c % 2, h * HD:(h + 1) * HD], start=True, stop=True)
                i.then_inc(intra_mm, 1)

            def inter(s, c):
                pe.wait_ge(h_done, at(s, NC - 1, c - 1))
                mm(ps_i[:, :], xc[:, XC, c * P:(c + 1) * P], hst[:, (c - 1) % 2], start=True, stop=True).then_inc(inter_mm, 1)

            def state(s, c):
                pe.wait_ge(xst_done, at(s, NC - 1, c))
                if c:
                    pe.wait_ge(ti_done, at(s, NC - 1, c - 1))
                elif type(s) is not int or s:
                    pe.wait_ge(ti_done, at(s - 1, NC - 1, NC - 2))
                mm(ps_i[:, :], Bt[:, c, :], Xst[:, c % 2], start=True, stop=True).then_inc(state_mm, 1)

            def gate_transpose(s, c):
                pe.wait_ge(ygh_done, at(s, NC, c))
                pe.wait_ge(ygl_done, at(s, NC, c))
                dst = half(ps_t[1], 2 * DI)
                for part, src in ((HI, ygh), (LO, ygl)):
                    for m in range(DI // P):
                        i = tr(dst[:, part * DI + m * P:part * DI + (m + 1) * P], src[:, c % 2, m * P:(m + 1) * P], ident16[:, :])
                i.then_inc(yT_mm, 1)

            def out_product(s, c):
                pe.wait_ge(yT_copied, at(s, NC, c))
                three(ps_t[0][:, 0:DM], lambda wp, xp, k: ygT[:, c % 2, xp, k, :],
                      lambda wp, xp, k: w_o[:, wp, k, :], DI // P).then_inc(o_mm, 1)

            def transpose2(s, c):
                pe.wait_ge(x2h_done, at(s, NC, c))
                pe.wait_ge(x2l_done, at(s, NC, c))
                dst = half(ps_t[1], 2 * KD * P)
                for part, src in ((HI, x2h), (LO, x2l)):
                    for k in range(KD):
                        i = tr(dst[:, (part * KD + k) * P:(part * KD + k + 1) * P], src[:, c % 2, k * P:(k + 1) * P], ident16[:, :])
                i.then_inc(x2T_mm, 1)

            def up(s, q, j):
                if j == 0:
                    pe.wait_ge(x2T_copied, at(s, NC, NC - 1))
                elif j != 3:
                    pe.wait_ge(r_done, at(s, NJ, j - 1 if j < 3 else j - 2))
                three(up_banks[j][:, :], lambda wp, xp, k: w_up[:, wp, k, j * P:(j + 1) * P],
                      lambda wp, xp, k: xn2T[:, q, xp, k, :], KD).then_inc(up_mm, 1)

            def down(s, c):
                if c == 0:
                    pe.wait_ge(r_done, at(s, NJ, NJ - 1))
                    pe.wait_ge(rh_done, at(s, NJ, NJ - 1))
                    pe.wait_ge(rl_done, at(s, NLP, NLP - 1))
                    pe.wait_ge(rlv_done, at(s, NJ - NLP, NJ - NLP - 1))
                elif c >= 2:
                    pe.wait_ge(ot_done, at(s, NC, c - 2))
                for part in (HI, LO):
                    for j in range(NJ):
                        i = mm(down_banks[c % 2][:, 0:DM], rT[:, part, j, c * P:(c + 1) * P], w_dn[:, j, :],
                               start=(part == HI and j == 0), stop=(part == LO and j == NJ - 1))
                i.then_inc(dn_mm, 1)

            def round_(s, q, ffn=True, nxt=True):
                p = 1 - q
                if ffn:
                    pe.wait_ge(x2T_copied, at(s - 1, NC, 1))
                    gate_transpose(s - 1, 3)
                project(s, 2)
                if ffn:
                    pe.wait_ge(dt_step, at(s, NDT, 24))
                    pe.wait_ge(yT_copied, at(s - 1, NC, 3))
                    out_product(s - 1, 3)
                project(s, 3)
                if ffn:
                    transpose2(s - 1, 2)
                project(s, 4)
                project(s, 5)
                project(s, 6)
                project(s, 7)
                if ffn:
                    pe.wait_ge(x2T_copied, at(s - 1, NC, 2))
                    transpose2(s - 1, 3)
                project(s, 8)
                if ffn:
                    up(s - 1, p, 0)
                project(s, 9)
                if ffn:
                    up(s - 1, p, 1)
                    pe.wait_ge(x2_done, at(s - 1, NC, 3))
                else:
                    pe.wait_ge(dt_step, at(s, NDT, 24))
                b_transpose(s)
                if ffn:
                    pe.wait_ge(x2T_copied, at(s - 1, NC, 3))
                g_product(s)
                if ffn:
                    up(s - 1, p, 2)
                decay_logs(s, q, 0, 0)
                decay_logs(s, q, 0, 1)
                x_transpose(s, 0)
                if ffn:
                    up(s - 1, p, 3)
                    up(s - 1, p, 4)
                for c in range(NC):
                    if c:
                        inter(s, c)
                    intra(s, c)
                    if c == 2 and nxt:
                        pe.wait_ge(x2_done, at(s, NC, 0))
                        dt_product(s + 1)
                    if c < NC - 1:
                        decay_logs(s, q, c + 1, 0)
                        if c == 0 and ffn:
                            up(s - 1, p, 5)
                        decay_logs(s, q, c + 1, 1)
                    if c == 0 and nxt:
                        pe.wait_ge(g_done, at(s, 1, 0))
                        input_transpose(s + 1, HI)
                    elif c == 1:
                        if nxt:
                            pe.wait_ge(xlT_copied, at(s + 1, 1, 0))
                        else:
                            pe.wait_ge(g_done, at(s, 1, 0))
                        gate_transpose(s, 0)
                    elif c == 2:
                        pe.wait_ge(yT_copied, at(s, NC, 0))
                        gate_transpose(s, 1)
                    elif c == 3:
                        pe.wait_ge(x2T_copied, at(s, NC, 0))
                        gate_transpose(s, 2)
                    if c < NC - 1:
                        state(s, c)
                        x_transpose(s, c + 1, nxt)
                    if c == 0:
                        if ffn:
                            up(s - 1, p, 6)
                            up(s - 1, p, 7)
                        if nxt:
                            pe.wait_ge(xhT_copied, at(s + 1, 1, 0))
                            input_transpose(s + 1, LO)
                    else:
                        if c == 3 and nxt:
                            project(s + 1, 0)
                            project(s + 1, 1)
                        if ffn:
                            down(s - 1, c - 1)
                        if c == 3 and nxt:
                            pe.wait_ge(yT_copied, at(s, NC, 2))
                            cumulate(s + 1)
                        if c < 3:
                            pe.wait_ge(xdt_done, at(s, 2 * NC, 2 * c + 3))
                        else:
                            pe.wait_ge(x2_done, at(s, NC, 1))
                        out_product(s, c - 1)
                        if c == 2:
                            pe.wait_ge(yT_copied, at(s, NC, 1))
                            transpose2(s, 0)
                        if c == 3:
                            if nxt:
                                pe.wait_ge(dt_exp, at(s + 1, 3, 1))
                            else:
                                pe.wait_ge(yT_copied, at(s, NC, 2))
                            transpose2(s, 1)
                if nxt:
                    pe.wait_ge(x2_done, at(s, NC, 2))
                    cum_rows(s + 1)
                if ffn:
                    down(s - 1, 3)

            def finish(s, q):
                pe.wait_ge(x2T_copied, at(s, NC, 1))
                gate_transpose(s, 3)
                pe.wait_ge(yT_copied, at(s, NC, 3))
                transpose2(s, 2)
                pe.wait_ge(x2_done, at(s, NC, 2))
                out_product(s, 3)
                pe.wait_ge(x2T_copied, at(s, NC, 2))
                transpose2(s, 3)
                for j in range(NJ):
                    up(s, q, j)
                for c in range(NC):
                    down(s, c)

            input_transpose(0, HI)
            pe.wait_ge(xhT_copied, 1)
            input_transpose(0, LO)
            dt_product(0)
            cumulate(0)
            cum_rows(0)
            project(0, 0)
            project(0, 1)
            round_(0, 0, ffn=False)
            with pe.Fori(0, S // 2 - 1) as i:
                round_(i * 2 + 1, 1)
                round_(i * 2 + 2, 0)
            round_(S - 1, 1, nxt=False)
            finish(S - 1, 1)


_INS = ["u", "in_proj_w", "conv_w", "conv_b", "dt_bias", "A_log", "D", "norm_w", "out_proj_w"]
_FFN = ["fast_b", "w_fc", "w_proj", "u", "v", "gate"]


def kernel(**inputs):
    import numpy as _np
    import concourse.bacc as _bacc
    from concourse import mybir as _mybir
    from concourse.bass_utils import run_bass_kernel_spmd as _run

    nc = _bacc.Bacc("TRN2", target_bir_lowering=False, num_devices=1)
    arrays, args = {}, []
    for name in ["L0_attn_" + n for n in _INS] + ["L0_ffn_" + n for n in _FFN]:
        a = _np.ascontiguousarray(inputs[name])
        a = a.reshape(a.shape or (1,))
        arrays[f"in_{name}"] = a
        args.append(nc.dram_tensor(f"in_{name}", a.shape, _mybir.dt.from_np(a.dtype), kind="ExternalInput").ap())
    shape = inputs["L0_attn_u"].shape
    args.append(nc.dram_tensor("out_0", shape, _mybir.dt.float32, kind="ExternalOutput").ap())
    build(nc, *args)
    r = _run(nc, [arrays], core_ids=[0])
    return r.results[0]["out_0"]
```

```python
from contextlib import ExitStack

import numpy as np
import concourse.bass as bass
from concourse import mybir

ALU = mybir.AluOpType
ACT = mybir.ActivationFunctionType
F32 = mybir.dt.float32
F16 = mybir.dt.float16
BF16 = mybir.dt.bfloat16
I32 = mybir.dt.int32
AX_X = mybir.AxisListType.X

P = 128
DM = 256
KD = DM // P
T = 512
NC = T // P
DI = 512
NH, HD = 8, 64
NST = 128
CONV = DI + 2 * NST
NM = CONV // P
TAPS = 4
NPROJ = 2 * DI + 2 * NST + NH
HID = 1024
NJ = HID // P
NLP = NJ - 2
RANK = 16
EPS = 1e-5
XS = 1024.0
FLOOR = -104.0
ABOVE = -30000.0
HI, LO = 0, 1
PASSES = ((HI, HI), (HI, LO), (LO, HI))
PROJ = (("c", 4), ("c", 5), ("c", 0), ("c", 1), ("c", 2), ("z", 0), ("c", 3), ("z", 1), ("z", 2), ("z", 3))
CONV_ORDER = [m for kind, m in PROJ if kind == "c"]
NMIX, NFFN = 7, 6
NDT = 25

POOL_IDENT, POOL_CONST, POOL_PICK, POOL_IN, POOL_ALL, POOL_TERN = 7, 12, 16, 15, 23, 22
ACT_Z, ACT_EXP, ACT_IN, ACT_UT, ACT_FC, ACT_SUMS, ACT_WO, ACT_DN, ACT_NORMS, ACT_UP = 4, 5, 11, 14, 24, 16, 25, 30, 38, 42
PE_GROUPS, PE_MX_IN, PE_MXB_IN, PE_WO, PE_MX_WO, PE_MXB_WO = 6, 7, 8, 13, 14, 15
PE_FV, PE_UT, PE_DNS, PE_MX_UP, PE_MXB_UP = 9, 11, 16, 21, 22
DVE_PICK, DVE_MX_IN, DVE_MXD_IN, DVE_P2_IN, DVE_IN, DVE_LOW_IN, DVE_WO32 = 1, 3, 5, 7, 11, 17, 24
DVE_MX_WO, DVE_MXD_WO, DVE_WO, DVE_SUMS, DVE_DN, DVE_WEFF, DVE_MX_UP, DVE_MXD_UP, DVE_LOW_UP, DVE_ALL = 25, 27, 41, 34, 43, 67, 69, 71, 79, 84


def build(nc, u, in_proj_w, conv_w, conv_b, dt_bias, A_log, D, norm_w, out_proj_w,
          fast_b, w_fc, w_proj, lr_u, lr_v, gate, out):
    S = u.shape[0]
    with ExitStack() as ctx:
        def sb(name, shape, dt=F32):
            return ctx.enter_context(nc.sbuf_tensor(name, shape, dt))

        def sem(name):
            return ctx.enter_context(nc.semaphore(name))

        def bank(name):
            return ctx.enter_context(nc.psum_tensor(name, [P, 512], F32))
        ps_proj = [bank("ps_proj0"), bank("ps_proj1")]
        ps_t = [bank("ps_t0"), bank("ps_t1")]
        ps_d, ps_y, ps_i, ps_f = bank("ps_d"), bank("ps_y"), bank("ps_i"), bank("ps_f")
        proj_banks = [ps_proj[0], ps_d, ps_proj[1], ps_y, ps_i]
        NPB = len(proj_banks)
        d_banks, down_banks = [ps_d, ps_proj[0]], [ps_f, ps_proj[1], ps_f, ps_f]
        up_banks = [ps_proj[1] if j >= 3 and j % 2 else ps_f for j in range(NJ)]

        def half(b, n):
            return b[:, :].bitcast(F16)[:, 0:n]

        w_in = sb("w_in", [P, 2, KD, NPROJ], F16)
        w_up = sb("w_up", [P, 2, KD, HID], F16)
        w_dn = sb("w_dn", [P, NJ, DM], F16)
        w_o = sb("w_o", [P, 2, DI // P, DM], F16)
        ident = sb("ident", [P, P])
        ident16 = sb("ident16", [P, P], F16)
        identb = sb("identb", [P, P], BF16)
        tri = sb("tri", [P, P])
        ones = sb("ones", [P, P])
        NR = 3 * NC * NH
        pick = sb("pick", [NR, NC * NH, P], BF16)
        above = sb("above", [P, 4, P], BF16)
        cw = sb("cw", [P, NM, TAPS])
        cwu = sb("cwu", [P, NM, TAPS])
        cb = sb("cb", [P, NM])
        dtb = sb("dtb", [P, NH])
        alog = sb("alog", [P, 3, NH])
        aexp = sb("aexp", [P, 3, NH])
        a_neg = sb("a_neg", [P, NH])
        d_bc = sb("d_bc", [P, NH])
        nw = sb("nw", [P, DI // P])
        gate_bc = sb("gate_bc", [P, 1])
        u_in = sb("u_in", [P, 1])
        u_relu = sb("u_relu", [P, 1])
        u_out = sb("u_out", [P, 1])
        g_gate = sb("g_gate", [P, 1])
        dn_bc = sb("dn_bc", [P, DM])
        mhalf = sb("mhalf", [P, NC])
        epsb = sb("epsb", [P, NC])
        xsb = sb("xsb", [P, NC])
        epsd = sb("epsd", [P, 1])
        pause = sb("pause", [P, 1])
        x_sb = sb("x_sb", [P, 2, NC, DM])
        st1 = sb("st1", [P, NC, 6])
        mv1 = sb("mv1", [P, NC, 2])
        va1 = sb("va1", [P, NC])
        rs1 = sb("rs1", [P, NC])
        rs1s = sb("rs1s", [P, NC])
        xn = sb("xn", [P, NC, DM])
        xh = sb("xh", [P, NC, DM], F16)
        xl = sb("xl", [P, NC, DM], F16)
        xnT = sb("xnT", [P, 2, KD, T], F16)
        dtw = sb("dtw", [P, 9, NC, NH])
        dt_ = sb("dt_", [P, 2, NC, NH])
        ecs = sb("ecs", [P, 2, 2, NC, NH])
        ede = sb("ede", [P, 2, NC, NH])
        cp3 = sb("cp3", [P, NC, 3, NH], BF16)
        cT = sb("cT", [NR, 2, P], BF16)
        ncT = sb("ncT", [NR, 2, P], BF16)
        acc = sb("acc", [P, 4, T])
        xc = sb("xc", [P, NM, T])
        sz = sb("sz", [P, NC, DI])
        Bt = sb("Bt", [P, NC, P])
        Gm = sb("Gm", [P, NC, P])
        tok = sb("tok", [P, 6, DI])
        Xdt, XD, Xst = tok[:, 0:2], tok[:, 2:4], tok[:, 4:6]
        Lb = sb("Lb", [P, 2, 512])
        Mb = sb("Mb", [P, 4, 4, P])
        hst = sb("hst", [P, 2, DI])
        hd = sb("hd", [P, DI])
        ti = sb("ti", [P, DI])
        ti2 = sb("ti2", [P, DI])
        yb = sb("yb", [P, 2, DI])
        ysq = sb("ysq", [P, DI])
        ssq = sb("ssq", [P, NC])
        rv = sb("rv", [P, 3, NC])
        yg = sb("yg", [P, 2, DI])
        ygh = sb("ygh", [P, 2, DI], F16)
        ygl = sb("ygl", [P, 2, DI], F16)
        ygT = sb("ygT", [P, 2, 2, DI // P, P], F16)
        x2 = sb("x2", [P, 2, NC, DM])
        st2 = sb("st2", [P, NC, 6])
        mv2 = sb("mv2", [P, NC, 2])
        rv2 = sb("rv2", [P, 3, NC])
        xn2 = sb("xn2", [P, 2, DM])
        x2h = sb("x2h", [P, 2, DM], F16)
        x2l = sb("x2l", [P, 2, DM], F16)
        xn2T = sb("xn2T", [P, 2, 2, KD, T], F16)
        r = sb("r", [P, 2, T])
        r2 = sb("r2", [P, 2, T])
        rT = sb("rT", [P, 2, NJ, T], F16)
        ot = sb("ot", [P, 2, DM])
        ob = sb("ob", [P, 2, DM])
        NT = NPROJ // P
        raw_in = tok[:, :, :].rearrange("p a b -> p (a b)")[:, 0:(NT + 1) * DM].rearrange("p (j n) -> p j n", n=DM)
        raw_out = Lb
        wo32 = Mb[:, 0:2, :, :].rearrange("p a b c -> p (a b c)").rearrange("p (m n) -> p m n", m=DI // P)
        raw_dn = rT[:, 0, :, :].rearrange("p a b -> p (a b)").bitcast(F32).rearrange("p (j n) -> p j n", j=KD)
        weff = rT[:, 1, :, :].rearrange("p a b -> p (a b)").bitcast(F32).rearrange("p (j n) -> p j n", j=NJ)
        raw_u = sb("raw_u", [P, NJ, RANK])
        raw_v = sb("raw_v", [RANK, DM])
        fbT = sb("fbT", [RANK, RANK])
        fv = sb("fv", [RANK, DM])
        uT = xn2T[0:RANK, 1].rearrange("p a b t -> p (a b t)").bitcast(F32).rearrange("p (j n) -> p j n", j=NJ)
        NS = 5
        mx = sb("mx", [P, 8, 16])
        mxa = sb("mxa", [P, NS])
        mxm = sb("mxm", [NS, 1])
        mxd = sb("mxd", [NS, NS])
        mxb = sb("mxb", [P, NS])
        p2 = sb("p2", [P, NS])
        ip2 = sb("ip2", [P, NS])
        rp = sb("rp", [P, NS])
        sw = sb("sw", [P, NS])
        fcs = sb("fcs", [P, 4, NJ])
        dns = sb("dns", [P, 6, KD])
        junk = r[:, :, :].rearrange("p a b -> p (a b)")
        tern = r2[:, :, :].rearrange("p a b -> p (a b)")
        late_banks = [ps_proj[1], ps_f]
        last_banks = [ps_y, ps_f, ps_i]
        dnd = sb("dnd", [P, KD, P])

        in_loaded, mixer_loaded, ffn_loaded, zeroed = sem("in_loaded"), sem("mixer_loaded"), sem("ffn_loaded"), sem("zeroed")
        x_loaded = [sem("x_loaded_even"), sem("x_loaded_odd")]
        stored = [sem("stored_even"), sem("stored_odd")]
        prep_pool, prep_act, prep_dve, prep_pe = sem("prep_pool"), sem("prep_act"), sem("prep_dve"), sem("prep_pe")
        st1_done, mv1_done, rs1_step, xn_done = sem("st1_done"), sem("mv1_done"), sem("rs1_step"), sem("xn_done")
        xh_done, xl_done = sem("xh_done"), sem("xl_done")
        xT_ready, xhT_copied, xlT_copied = sem("xT_ready"), sem("xhT_copied"), sem("xlT_copied")
        dt_mm, dt_mm2, dt_step, dt_exp = sem("dt_mm"), sem("dt_mm2"), sem("dt_step"), sem("dt_exp")
        proj_done, acc_init, conv_step, xc_done, z_done = (
            sem("proj_done"), sem("acc_init"), sem("conv_step"), sem("xc_done"), sem("z_done"))
        bt_mm, bt_copied, g_mm, g_done = sem("bt_mm"), sem("bt_copied"), sem("g_mm"), sem("g_done")
        d_mm, l_done, m_done = sem("d_mm"), sem("l_done"), sem("m_done")
        xt_mm, xdt_done, xst_done = sem("xt_mm"), sem("xdt_done"), sem("xst_done")
        intra_mm, inter_mm, state_mm = sem("intra_mm"), sem("inter_mm"), sem("state_mm")
        ti_done, ti2_done, h_done, hd_done = sem("ti_done"), sem("ti2_done"), sem("h_done"), sem("hd_done")
        y_done, ssq_done, rv_step, yg_done, ygh_done, ygl_done = (
            sem("y_done"), sem("ssq_done"), sem("rv_step"), sem("yg_done"), sem("ygh_done"), sem("ygl_done"))
        yT_mm, yT_copied, o_mm, x2_done = sem("yT_mm"), sem("yT_copied"), sem("o_mm"), sem("x2_done")
        st2_done, mv2_done, rv2_step, xn2_done = sem("st2_done"), sem("mv2_done"), sem("rv2_step"), sem("xn2_done")
        x2h_done, x2l_done, x2T_mm, x2T_copied = sem("x2h_done"), sem("x2l_done"), sem("x2T_mm"), sem("x2T_copied")
        up_mm, r_done, r2_done, rh_done, rl_done, rlv_done = (
            sem("up_mm"), sem("r_done"), sem("r2_done"), sem("rh_done"), sem("rl_done"), sem("rlv_done"))
        lr_mm = sem("lr_mm")
        dn_mm, ot_done, ob_done = sem("dn_mm"), sem("ot_done"), sem("ob_done")

        xs = u.rearrange("s (c p) d -> s p c d", p=P)
        outs = out.rearrange("s (c p) d -> s c p d", p=P)

        in_groups, up_groups, dn_groups = [], [], []
        for k in range(KD):
            for m0, m1 in ((0, 4), (4, 8), (8, NT + 1)):
                src = [raw_in[0:(P if m < NT else NPROJ - NT * P), m, k * P:(k + 1) * P] for m in range(m0, m1)]
                e = min(m1 * P, NPROJ)
                in_groups.append((src, e - m0 * P, w_in[:, HI, k, m0 * P:e], w_in[:, LO, k, m0 * P:e]))
        for k in range(KD):
            for j in range(0, NJ, 4):
                src = [weff[:, j + a, k * P:(k + 1) * P] for a in range(4)]
                up_groups.append((src, 4 * P, w_up[:, HI, k, j * P:(j + 4) * P], w_up[:, LO, k, j * P:(j + 4) * P]))
        for j in range(0, NJ, 2):
            src = [raw_dn[:, k, (j + a) * P:(j + a + 1) * P] for a in range(2) for k in range(KD)]
            dn_groups.append((src, w_dn[:, j:j + 2, :].rearrange("p a b -> p (a b)")))
        in_banks = ps_proj + [ps_y, ps_i, ps_f, ps_d]

        block = ctx.enter_context(nc.Block())

        def at(s, n, k):
            return s * n + (k + 1)

        def conv_end(k):
            return 3 * (k - k % 2) + 4 + k % 2

        @block.sync
        def _(sp):
            def load_x(s, q):
                sp.dma_start(x_sb[:, q], xs[s]).then_inc(x_loaded[q], 16)

            def store(s, c):
                sp.wait_ge(ob_done, at(s, NC, c))
                sp.dma_start(outs[s, c], ob[:, c % 2]).then_inc(stored[c % 2], 16)

            load_x(0, 0)
            sp.wait_ge(zeroed, 1)
            with nc.allow_non_contiguous_dma(reason="small weights, once"):
                for loaded, dst, src in (
                    (in_loaded, raw_in[:, 0:NT, :], in_proj_w[0:NT * P, :].rearrange("(j p) n -> p j n", p=P)),
                    (in_loaded, raw_in[0:NPROJ - NT * P, NT, :], in_proj_w[NT * P:NPROJ, :]),
                    (mixer_loaded, cw[:, :, :], conv_w.rearrange("(j p) o t -> p j (o t)", p=P)),
                    (mixer_loaded, cb[:, :], conv_b.rearrange("(j p) -> p j", p=P)),
                    (mixer_loaded, dtb[:, :], dt_bias.rearrange("(a b) -> a b", a=1).to_broadcast([P, NH])),
                    (mixer_loaded, alog[:, :, :].rearrange("p a b -> p (a b)"),
                     A_log.rearrange("a b -> (a b)").rearrange("(a b) -> a b", a=1).to_broadcast([P, 3 * NH])),
                    (mixer_loaded, d_bc[:, :], D.rearrange("(a b) -> a b", a=1).to_broadcast([P, NH])),
                    (mixer_loaded, nw[:, :], norm_w.rearrange("(j p) -> p j", p=P)),
                    (mixer_loaded, raw_out[:, :, :], out_proj_w.rearrange("(j p) n -> p j n", p=P)),
                    (ffn_loaded, weff, w_fc.rearrange("(j p) n -> p j n", p=P)),
                    (ffn_loaded, raw_dn, w_proj.rearrange("(j p) n -> p j n", p=P)),
                    (ffn_loaded, raw_u[:, :, :], lr_u.rearrange("(j p) n -> p j n", p=P)),
                    (ffn_loaded, raw_v[:, :], lr_v),
                    (ffn_loaded, fbT[:, :], fast_b.rearrange("a b -> b a")),
                    (ffn_loaded, gate_bc[:, :], gate.rearrange("(a b) -> a b", a=1).to_broadcast([P, 1])),
                ):
                    sp.dma_start(dst, src).then_inc(loaded, 16)
            load_x(1, 1)
            with sp.Fori(0, S // 2 - 1) as i:
                for q in range(2):
                    s = i * 2 + q
                    sp.wait_ge(x2_done, at(s, NC, NC - 1))
                    load_x(s + 2, q)
                    for c in range(NC):
                        store(s, c)
            for s in range(S - 2, S):
                for c in range(NC):
                    store(s, c)
            for done in stored:
                sp.wait_ge(done, (S * NC // 2 + 1) * 16)

        @block.gpsimd
        def _(pool):
            n = [0]

            def step(ins):
                n[0] += 1
                ins.then_inc(prep_pool, 1)
                pool.wait_ge(prep_pool, n[0])

            nc.gpsimd.memset(raw_in[:, NT, :], 0.0).then_inc(zeroed, 1)
            for slot, free in enumerate(stored):
                nc.gpsimd.memset(ob[:, slot], 0.0).then_inc(free, 16)
            step(nc.gpsimd.memset(mhalf[:, :], -0.5))
            step(nc.gpsimd.memset(epsb[:, :], EPS))
            step(nc.gpsimd.memset(xsb[:, :], XS))
            step(nc.gpsimd.memset(epsd[:, :], EPS * DI))
            step(nc.gpsimd.memset(ones[:, :], 1.0))
            step(nc.gpsimd.memset(ident[:, :], 0.0))
            step(nc.gpsimd.affine_select(out=ident[:, :], in_=ident[:, :], compare_op=ALU.not_equal, fill=1.0,
                                         base=0, pattern=[[-1, P]], channel_multiplier=1))
            assert n[0] == POOL_IDENT, ("POOL_IDENT", n[0])
            step(nc.gpsimd.affine_select(out=tri[:, :], in_=ones[:, :], compare_op=ALU.is_ge, fill=0.0,
                                         base=0, pattern=[[1, P]], channel_multiplier=-1))
            step(nc.gpsimd.tensor_copy(ident16[:, :], ident[:, :]))
            step(nc.gpsimd.tensor_copy(identb[:, :], ident[:, :]))
            step(nc.gpsimd.memset(above[:, :, :], 0.0))
            step(nc.gpsimd.affine_select(out=above[:, :, :], in_=above[:, :, :], compare_op=ALU.is_ge, fill=ABOVE,
                                         base=0, pattern=[[0, 4], [1, P]], channel_multiplier=-1))
            assert n[0] == POOL_CONST, ("POOL_CONST", n[0])

            def pick_rows(part):
                pk = pick[:, :, :].rearrange("k (c h) p -> k c h p", c=NC)
                step(nc.gpsimd.affine_select(out=pk, in_=pk, compare_op=ALU.not_equal, fill=1.0,
                                             base=-part * NH, pattern=[[-3 * NH, NC], [-1, NH], [0, P]],
                                             channel_multiplier=1))

            def inverse_root(a, b):
                step(nc.gpsimd.tensor_tensor(rp[:, a:b], p2[:, a:b], mhalf[:, 0:1].to_broadcast([P, b - a]), ALU.pow))

            def ternary(w, scales, j, tmp):
                step(nc.gpsimd.tensor_scalar(tmp, w, scales[:, 3, j:j + 1], None, ALU.is_lt))
                step(nc.gpsimd.tensor_scalar(w, w, scales[:, 2, j:j + 1], None, ALU.is_gt))
                step(nc.gpsimd.tensor_tensor(w, w, tmp, ALU.subtract))

            def prepare(k):
                if k == 4:
                    pool.wait_ge(prep_dve, DVE_MXD_UP + 2)
                    inverse_root(3, 5)
                    assert n[0] == POOL_ALL, ("POOL_ALL", n[0])

            def input_stats(s):
                pool.wait_ge(mv1_done, at(s, NC, NC - 1))
                nc.gpsimd.tensor_tensor(va1[:, :], mv1[:, :, 1], epsb[:, :], ALU.add).then_inc(rs1_step, 1)
                pool.wait_ge(rs1_step, at(s, 3, 0))
                nc.gpsimd.tensor_tensor(rs1[:, :], va1[:, :], mhalf[:, :], ALU.pow).then_inc(rs1_step, 1)
                pool.wait_ge(rs1_step, at(s, 3, 1))
                nc.gpsimd.tensor_tensor(rs1s[:, :], rs1[:, :], xsb[:, :], ALU.mult).then_inc(rs1_step, 1)

            def input_low(s):
                pool.wait_ge(xh_done, at(s, 1, 0))
                nc.gpsimd.tensor_tensor(xl[:, :, :], xn[:, :, :], xh[:, :, :], ALU.subtract).then_inc(xl_done, 1)

            def x_state(s, q, c):
                if c == 0:
                    pool.wait_ge(dt_exp, at(s, 3, 2))
                pool.wait_ge(xdt_done, at(s, 2 * NC, 2 * c))
                nc.gpsimd.tensor_tensor(
                    Xst[:, c % 2].rearrange("p (h d) -> p h d", h=NH), Xdt[:, c % 2].rearrange("p (h d) -> p h d", h=NH),
                    ede[:, q, c].unsqueeze(2).to_broadcast([P, NH, HD]), ALU.mult).then_inc(xst_done, 1)

            def decay_state(s, q, c):
                pool.wait_ge(h_done, at(s, NC - 1, c - 1))
                nc.gpsimd.tensor_tensor(
                    hd[:, :].rearrange("p (h d) -> p h d", h=NH), hst[:, (c - 1) % 2].rearrange("p (h d) -> p h d", h=NH),
                    ecs[:, q, 1, c].unsqueeze(2).to_broadcast([P, NH, HD]), ALU.mult).then_inc(hd_done, 1)

            def add_skip(s, c):
                pool.wait_ge(ti_done, at(s, NC - 1, c - 1))
                pool.wait_ge(xdt_done, at(s, 2 * NC, 2 * c + 1))
                nc.gpsimd.tensor_tensor(ti2[:, :], ti[:, :], XD[:, c % 2], ALU.add).then_inc(ti2_done, 1)

            def rms(s, c):
                pool.wait_ge(ssq_done, at(s, NC, c))
                nc.gpsimd.tensor_tensor(rv[:, 0, c:c + 1], ssq[:, c:c + 1], epsd[:, :], ALU.add).then_inc(rv_step, 1)
                pool.wait_ge(rv_step, at(s, 3 * NC, 3 * c))
                nc.gpsimd.tensor_tensor(rv[:, 1, c:c + 1], rv[:, 0, c:c + 1], mhalf[:, 0:1], ALU.pow).then_inc(rv_step, 1)
                pool.wait_ge(rv_step, at(s, 3 * NC, 3 * c + 1))
                nc.gpsimd.tensor_tensor(rv[:, 2, c:c + 1], rv[:, 1, c:c + 1], g_gate[:, :], ALU.mult).then_inc(rv_step, 1)

            def gate_low(s, c):
                pool.wait_ge(ygh_done, at(s, NC, c))
                nc.gpsimd.tensor_tensor(ygl[:, c % 2], yg[:, c % 2], ygh[:, c % 2], ALU.subtract).then_inc(ygl_done, 1)

            def stats2(s, c):
                pool.wait_ge(mv2_done, at(s, NC, c))
                nc.gpsimd.tensor_tensor(rv2[:, 0, c:c + 1], mv2[:, c, 1:2], epsb[:, 0:1], ALU.add).then_inc(rv2_step, 1)
                pool.wait_ge(rv2_step, at(s, 3 * NC, 3 * c))
                nc.gpsimd.tensor_tensor(rv2[:, 1, c:c + 1], rv2[:, 0, c:c + 1], mhalf[:, 0:1], ALU.pow).then_inc(rv2_step, 1)
                pool.wait_ge(rv2_step, at(s, 3 * NC, 3 * c + 1))
                nc.gpsimd.tensor_tensor(rv2[:, 2, c:c + 1], rv2[:, 1, c:c + 1], xsb[:, 0:1], ALU.mult).then_inc(rv2_step, 1)

            def low2(s, c):
                pool.wait_ge(x2h_done, at(s, NC, c))
                nc.gpsimd.tensor_tensor(x2l[:, c % 2], xn2[:, c % 2], x2h[:, c % 2], ALU.subtract).then_inc(x2l_done, 1)

            def relu_low(s, j):
                pool.wait_ge(rh_done, at(s, NJ, j))
                nc.gpsimd.tensor_tensor(rT[:, LO, j], r2[:, j % 2], rT[:, HI, j], ALU.subtract).then_inc(rl_done, 1)

            def result(s, q, c):
                pool.wait_ge(ot_done, at(s, NC, c))
                pool.wait_ge(stored[c % 2], (s * (NC // 2) + c // 2 + 1) * 16)
                nc.gpsimd.tensor_tensor(ob[:, c % 2], ot[:, c % 2], x2[:, q, c], ALU.add).then_inc(ob_done, 1)

            def round_(s, q, ffn=True, nxt=True, hook=lambda k: None):
                if ffn:
                    low2(s - 1, 2)
                    stats2(s - 1, 3)
                    low2(s - 1, 3)
                    relu_low(s - 1, 0)
                if nxt:
                    input_stats(s + 1)
                if ffn:
                    relu_low(s - 1, 1)
                x_state(s, q, 0)
                if ffn:
                    relu_low(s - 1, 2)
                    relu_low(s - 1, 3)
                if nxt:
                    input_low(s + 1)
                if ffn:
                    relu_low(s - 1, 4)
                for c in range(NC):
                    if c:
                        add_skip(s, c)
                    if c >= 2:
                        low2(s, c - 2)
                    if c == 0 and ffn:
                        relu_low(s - 1, 5)
                    rms(s, c)
                    if c < NC - 2:
                        x_state(s, q, c + 1)
                    if c < NC - 2:
                        decay_state(s, q, c + 1)
                    gate_low(s, c)
                    if c:
                        stats2(s, c - 1)
                        if ffn:
                            result(s - 1, 1 - q, c - 1)
                    hook(c + 1)
                if ffn:
                    result(s - 1, 1 - q, 3)

            def finish(s, q):
                low2(s, 2)
                stats2(s, 3)
                low2(s, 3)
                for j in range(NLP):
                    relu_low(s, j)
                for c in range(NC):
                    result(s, q, c)

            pool.wait_ge(prep_dve, DVE_PICK)
            input_stats(0)
            pick_rows(0)
            input_low(0)
            pick_rows(1)
            pool.wait_ge(prep_dve, DVE_P2_IN)
            inverse_root(0, 2)
            assert n[0] == POOL_IN, ("POOL_IN", n[0])
            pick_rows(2)
            assert n[0] == POOL_PICK, ("POOL_PICK", n[0])
            pool.wait_ge(ffn_loaded, 16 * NFFN)
            pool.wait_ge(prep_dve, DVE_SUMS)
            for j in range(KD):
                ternary(raw_dn[:, j], dns, j, tern[:, :])
            assert n[0] == POOL_TERN, ("POOL_TERN", n[0])
            round_(0, 0, ffn=False, hook=prepare)
            with pool.Fori(0, S // 2 - 1) as i:
                round_(i * 2 + 1, 1)
                round_(i * 2 + 2, 0)
            round_(S - 1, 1, nxt=False)
            finish(S - 1, 1)

        @block.scalar
        def _(act):
            n = [0]

            def step(ins):
                n[0] += 1
                ins.then_inc(prep_act, 1)

            def down_weights(g):
                act.wait_ge(prep_pe, PE_DNS + g + 1)
                step(nc.scalar.activation(dn_groups[g][1], late_banks[g % 2][:, :], ACT.Copy))

            def squares(j0, j1):
                for j in range(j0, j1):
                    act.wait_ge(prep_act, n[0])
                    step(nc.scalar.activation(junk[:, 0:DM], weff[:, j], ACT.Square, accum_out=mx[:, 4, j:j + 1]))

            def prepare(k):
                if k == 0:
                    act.wait_ge(prep_dve, DVE_MXD_WO + 4)
                    step(nc.scalar.activation(w_o[:, HI, :, :].rearrange("p a b -> p (a b)"),
                                              wo32.rearrange("p a b -> p (a b)"), ACT.Copy, scale=sw[:, 2:3]))
                    assert n[0] == ACT_WO, ("ACT_WO", n[0])
                elif k == 0.5:
                    act.wait_ge(prep_pe, PE_DNS)
                    step(nc.scalar.activation(dn_bc[:, :], ps_f[:, 0:DM], ACT.Copy))
                    down_weights(0)
                elif k == 1:
                    down_weights(1)
                    down_weights(2)
                elif k == 1.5:
                    down_weights(3)
                    assert n[0] == ACT_DN, ("ACT_DN", n[0])
                elif k == 2:
                    act.wait_ge(prep_dve, DVE_DN + 3 * (NJ // 2))
                    squares(0, NJ // 2)
                elif k == 3:
                    act.wait_ge(prep_dve, DVE_WEFF)
                    squares(NJ // 2, NJ)
                    assert n[0] == ACT_NORMS, ("ACT_NORMS", n[0])
                elif k == 4:
                    act.wait_ge(prep_dve, DVE_MXD_UP + 4)
                    for g, (_, w, high, _) in enumerate(up_groups):
                        act.wait_ge(prep_pe, PE_MXB_UP + g + 1)
                        step(nc.scalar.activation(high, last_banks[g % 3][:, 0:w], ACT.Copy, scale=sw[:, 3:4]))
                    assert n[0] == ACT_UP, ("ACT_UP", n[0])

            def input_high(s):
                act.wait_ge(xn_done, at(s, NC, NC - 1))
                nc.scalar.activation(xh[:, :, :].rearrange("p a b -> p (a b)"),
                                     xn[:, :, :].rearrange("p a b -> p (a b)"), ACT.Copy).then_inc(xh_done, 1)

            def input_copy(s, part):
                act.wait_ge(xT_ready, at(s, 2, part))
                nc.scalar.activation(xnT[:, part].rearrange("p a b -> p (a b)"), half(ps_t[1], KD * T),
                                     ACT.Copy).then_inc(xhT_copied if part == HI else xlT_copied, 1)

            def dt_exp_abs(s):
                act.wait_ge(dt_step, at(s, NDT, 1))
                nc.scalar.activation(dtw[:, 2], dtw[:, 1], ACT.Exp, scale=-1.0).then_inc(dt_exp, 1)

            def decays(s, q):
                act.wait_ge(dt_step, at(s, NDT, 18))
                nc.scalar.activation(ecs[:, q], ps_t[1][:, 0:2 * NC * NH].rearrange("p (a c h) -> p a c h", a=2, c=NC),
                                     ACT.Exp).then_inc(dt_exp, 1)
                nc.scalar.activation(ede[:, q], dtw[:, 6], ACT.Exp).then_inc(dt_exp, 1)

            def conv_init(s, k):
                m = CONV_ORDER[k]
                act.wait_ge(proj_done, at(s, len(PROJ), PROJ.index(("c", m))))
                if k >= 4:
                    act.wait_ge(xc_done, at(s, NM, k - 4))
                nc.scalar.activation(acc[:, k % 4], proj_banks[PROJ.index(("c", m)) % NPB][:, :], ACT.Identity,
                                     scale=cwu[:, m, 3:4], bias=cb[:, m:m + 1]).then_inc(acc_init, 1)

            def conv_silu(s, k):
                act.wait_ge(conv_step, at(s, 3 * NM, conv_end(k)))
                nc.scalar.activation(xc[:, CONV_ORDER[k]], acc[:, k % 4], ACT.Silu).then_inc(xc_done, 1)

            def gate_silu(s, c):
                act.wait_ge(proj_done, at(s, len(PROJ), PROJ.index(("z", c))))
                nc.scalar.activation(sz[:, c], proj_banks[PROJ.index(("z", c)) % NPB][:, :], ACT.Silu,
                                     scale=u_in[:, :]).then_inc(z_done, 1)

            def b_copy(s):
                act.wait_ge(bt_mm, at(s, 1, 0))
                nc.scalar.activation(Bt[:, :, :].rearrange("p a b -> p (a b)"), ps_t[0][:, :], ACT.Copy).then_inc(bt_copied, 1)

            def g_copy(s):
                act.wait_ge(g_mm, at(s, 1, 0))
                nc.scalar.activation(Gm[:, :, :].rearrange("p c t -> p (c t)"), ps_t[1][:, :], ACT.Copy).then_inc(g_done, 1)

            def gate_copy(s, c):
                act.wait_ge(yT_mm, at(s, NC, c))
                nc.scalar.activation(ygT[:, c % 2].rearrange("p a b t -> p (a b t)"), half(ps_t[1], 2 * DI),
                                     ACT.Copy).then_inc(yT_copied, 1)

            def decay_matrix(s, c, g):
                act.wait_ge(d_mm, at(s, 2 * NC, 2 * c + g))
                if c:
                    act.wait_ge(m_done, at(s, 2 * NC, 2 * c + g - 2))
                nc.scalar.activation(Lb[:, g], d_banks[g][:, :], ACT.Exp).then_inc(l_done, 1)

            def state_copy(s):
                act.wait_ge(state_mm, at(s, NC - 1, 0))
                nc.scalar.activation(hst[:, 0], ps_i[:, :], ACT.Copy).then_inc(h_done, 1)

            def square(s, c):
                act.wait_ge(y_done, at(s, NC, c))
                nc.scalar.activation(ysq[:, :], yb[:, c % 2], ACT.Square, accum_out=ssq[:, c:c + 1]).then_inc(ssq_done, 1)

            def gate_high(s, c):
                act.wait_ge(yg_done, at(s, NC, c))
                nc.scalar.activation(ygh[:, c % 2], yg[:, c % 2], ACT.Copy).then_inc(ygh_done, 1)

            def high2(s, c):
                act.wait_ge(xn2_done, at(s, NC, c))
                nc.scalar.activation(x2h[:, c % 2], xn2[:, c % 2], ACT.Copy).then_inc(x2h_done, 1)

            def copy2(s, q, c):
                act.wait_ge(x2T_mm, at(s, NC, c))
                nc.scalar.activation(xn2T[:, q, :, :, c * P:(c + 1) * P],
                                     half(ps_t[1], 2 * KD * P).rearrange("p (a b t) -> p a b t", a=2, b=KD),
                                     ACT.Copy).then_inc(x2T_copied, 1)

            def relu(s, j, last=False):
                act.wait_ge(up_mm, at(s, NJ, j))
                bank = down_banks[j % 2] if last else up_banks[j]
                nc.scalar.activation(r[:, j % 2], bank[:, :], ACT.Relu, scale=u_relu[:, :]).then_inc(r_done, 1)

            def relu_high(s, j):
                act.wait_ge(r2_done, at(s, NJ, j))
                nc.scalar.activation(rT[:, HI, j], r2[:, j % 2], ACT.Copy).then_inc(rh_done, 1)

            def round_(s, q, ffn=True, nxt=True, hook=lambda k: None):
                if ffn:
                    gate_copy(s - 1, 3)
                    high2(s - 1, 2)
                conv_init(s, 3)
                hook(0)
                conv_silu(s, 0)
                conv_silu(s, 1)
                if ffn:
                    copy2(s - 1, 1 - q, 2)
                conv_init(s, 4)
                if ffn:
                    high2(s - 1, 3)
                conv_init(s, 5)
                if ffn:
                    copy2(s - 1, 1 - q, 3)
                gate_silu(s, 0)
                conv_silu(s, 2)
                conv_silu(s, 3)
                gate_silu(s, 1)
                gate_silu(s, 2)
                if ffn:
                    relu(s - 1, 0)
                conv_silu(s, 4)
                conv_silu(s, 5)
                gate_silu(s, 3)
                if ffn:
                    relu_high(s - 1, 0)
                    relu(s - 1, 1)
                b_copy(s)
                g_copy(s)
                if ffn:
                    relu_high(s - 1, 1)
                    relu(s - 1, 2)
                decay_matrix(s, 0, 0)
                decay_matrix(s, 0, 1)
                hook(0.5)
                if ffn:
                    relu_high(s - 1, 2)
                    relu(s - 1, 3)
                    relu(s - 1, 4)
                    relu_high(s - 1, 3)
                if nxt:
                    input_high(s + 1)
                if ffn:
                    relu_high(s - 1, 4)
                for c in range(NC):
                    if c >= 2:
                        high2(s, c - 2)
                    if c < NC - 1:
                        decay_matrix(s, c + 1, 0)
                    if c == 0 and ffn:
                        relu(s - 1, 5)
                    if c and c < NC - 1:
                        decay_matrix(s, c + 1, 1)
                    if c == 2 and nxt:
                        dt_exp_abs(s + 1)
                    square(s, c)
                    if c == 0:
                        decay_matrix(s, c + 1, 1)
                    if c == 1:
                        hook(1.5)
                    if c:
                        gate_copy(s, c - 1)
                        if c == 3 and nxt:
                            conv_init(s + 1, 0)
                            conv_init(s + 1, 1)
                    else:
                        if ffn:
                            relu_high(s - 1, 5)
                        if nxt:
                            input_copy(s + 1, HI)
                        state_copy(s)
                        if ffn:
                            relu(s - 1, 6)
                            relu_high(s - 1, 6)
                            relu(s - 1, 7)
                    if c == 3 and nxt:
                        decays(s + 1, 1 - q)
                    gate_high(s, c)
                    if c == 0:
                        if ffn:
                            relu_high(s - 1, 7)
                        if nxt:
                            input_copy(s + 1, LO)
                    if c >= 2:
                        copy2(s, q, c - 2)
                    if c == 3 and nxt:
                        conv_init(s + 1, 2)
                    hook(c + 1)

            def finish(s, q):
                gate_copy(s, 3)
                high2(s, 2)
                copy2(s, q, 2)
                high2(s, 3)
                copy2(s, q, 3)
                relu(s, 0, last=True)
                for j in range(NJ):
                    if j < NJ - 1:
                        relu(s, j + 1, last=True)
                    relu_high(s, j)

            act.wait_ge(in_loaded, 16 * 2)
            for j in range(DI // P):
                step(nc.scalar.activation(junk[:, 0:DM], raw_in[:, j], ACT.Square, accum_out=mx[:, 1, j:j + 1]))
                act.wait_ge(prep_act, n[0])
            assert n[0] == ACT_Z, ("ACT_Z", n[0])
            act.wait_ge(mixer_loaded, 16 * NMIX)
            step(nc.scalar.activation(aexp[:, :, :].rearrange("p a b -> p (a b)"),
                                      alog[:, :, :].rearrange("p a b -> p (a b)"), ACT.Exp))
            assert n[0] == ACT_EXP, ("ACT_EXP", n[0])
            input_high(0)
            input_copy(0, HI)
            act.wait_ge(prep_dve, DVE_P2_IN + 2)
            for g, (_, w, high, _) in enumerate(in_groups):
                act.wait_ge(prep_pe, g + 1)
                step(nc.scalar.activation(high, in_banks[g][:, 0:w], ACT.Copy, scale=sw[:, 0:1]))
            assert n[0] == ACT_IN, ("ACT_IN", n[0])
            act.wait_ge(ffn_loaded, 16 * NFFN)
            act.wait_ge(prep_pe, PE_FV)
            step(nc.scalar.activation(fv[:, :], ps_t[0][0:RANK, 0:DM], ACT.Copy, scale=gate_bc[0:RANK, :]))
            for g in range(2):
                act.wait_ge(prep_pe, PE_FV + g + 1)
                step(nc.scalar.activation(uT[:, 4 * g:4 * g + 4, :].rearrange("p a b -> p (a b)"),
                                          ps_proj[g][0:RANK, :], ACT.Copy))
            assert n[0] == ACT_UT, ("ACT_UT", n[0])
            input_copy(0, LO)
            dt_exp_abs(0)
            for j in range(KD):
                act.wait_ge(prep_act, n[0])
                step(nc.scalar.activation(junk[:, 0:HID], raw_dn[:, j], ACT.Abs, accum_out=dns[:, 0, j:j + 1]))
            assert n[0] == ACT_SUMS, ("ACT_SUMS", n[0])
            for j in range(NJ):
                act.wait_ge(prep_act, n[0])
                step(nc.scalar.activation(junk[:, 0:DM], weff[:, j], ACT.Abs, accum_out=fcs[:, 0, j:j + 1]))
            assert n[0] == ACT_FC, ("ACT_FC", n[0])
            decays(0, 0)
            act.wait_ge(prep_dve, DVE_IN)
            conv_init(0, 0)
            conv_init(0, 1)
            conv_init(0, 2)
            round_(0, 0, ffn=False, hook=prepare)
            with act.Fori(0, S // 2 - 1) as i:
                round_(i * 2 + 1, 1)
                round_(i * 2 + 2, 0)
            round_(S - 1, 1, nxt=False)
            finish(S - 1, 1)

        @block.vector
        def _(dve):
            n = [0]

            def step(ins):
                n[0] += 1
                ins.then_inc(prep_dve, 1)
                dve.wait_ge(prep_dve, n[0])

            V = nc.vector
            def maxima(a, b, bank, mx_ready):
                k = b - a
                dve.wait_ge(prep_pe, mx_ready)
                step(V.tensor_reduce(mxm[0:k, :], bank[0:k, 0:P], AX_X, ALU.max))
                step(V.tensor_scalar(mxd[0:k, 0:k], ident[0:k, 0:k], mxm[0:k, :], None, ALU.mult))

            def powers(a, b, bank, mxb_ready):
                dve.wait_ge(prep_pe, mxb_ready)
                step(V.tensor_scalar(mxb[:, a:b], bank[:, 0:b - a], 1e-30, None, ALU.max))
                step(V.tensor_scalar(p2[:, a:b].bitcast(I32), mxb[:, a:b].bitcast(I32), 0x7F800000, None, ALU.bitwise_and))
                step(V.reciprocal(ip2[:, a:b], p2[:, a:b]))
                step(V.tensor_scalar(sw[:, a:b], ip2[:, a:b], 8192.0, None, ALU.mult))

            def low_part(bank, w, high, low, sc):
                step(V.scalar_tensor_tensor(low, bank[:, 0:w], sw[:, sc:sc + 1], high, ALU.mult, ALU.subtract))

            def row_scales(sums, w):
                step(V.tensor_scalar(sums[:, 1, :], sums[:, 0, :], 1.0 / w, 1e-5, ALU.mult, ALU.max))
                step(V.tensor_scalar(sums[:, 2, :], sums[:, 1, :], 0.5, None, ALU.mult))
                step(V.tensor_scalar(sums[:, 3, :], sums[:, 1, :], -0.5, None, ALU.mult))

            def effective_up(j0, j1):
                for j in range(j0, j1):
                    step(V.tensor_scalar(tern[:, 0:DM], weff[:, j], fcs[:, 3, j:j + 1], None, ALU.is_lt))
                    step(V.scalar_tensor_tensor(tern[:, DM:2 * DM], weff[:, j], fcs[:, 2, j:j + 1], tern[:, 0:DM],
                                                ALU.is_gt, ALU.subtract))
                    dve.wait_ge(lr_mm, j // 2 + 1)
                    step(V.scalar_tensor_tensor(weff[:, j], tern[:, DM:2 * DM], fcs[:, 1, j:j + 1],
                                                late_banks[j // 2 % 2][:, (j % 2) * DM:(j % 2 + 1) * DM], ALU.mult, ALU.add))

            def prepare(k):
                if k == 0:
                    dve.wait_ge(prep_pool, POOL_IN)
                    step(V.tensor_scalar(g_gate[:, :], rp[:, 1:2], 64.0 * DI ** 0.5, None, ALU.mult))
                    step(V.tensor_scalar(mx[:, 5, 0:1], g_gate[:, :], sw[:, 2:3], DI ** -0.5, ALU.mult, ALU.mult))
                    step(V.reciprocal(u_out[:, :], mx[:, 5, 0:1]))
                    dve.wait_ge(prep_act, ACT_WO)
                    step(V.scalar_tensor_tensor(w_o[:, LO, :, :].rearrange("p a b -> p (a b)"),
                                                wo32.rearrange("p a b -> p (a b)"), sw[:, 2:3],
                                                w_o[:, HI, :, :].rearrange("p a b -> p (a b)"), ALU.mult, ALU.subtract))
                    assert n[0] == DVE_WO, ("DVE_WO", n[0])
                    for j in range(KD):
                        step(V.tensor_scalar(dnd[:, j], ident[:, :], dns[:, 1, j:j + 1], None, ALU.mult))
                    assert n[0] == DVE_DN, ("DVE_DN", n[0])
                elif k == 2:
                    effective_up(0, NJ // 2)
                elif k == 3:
                    effective_up(NJ // 2, NJ)
                    assert n[0] == DVE_WEFF, ("DVE_WEFF", n[0])
                    step(V.tensor_reduce(mxa[:, 3:4], weff.rearrange("p a b -> p (a b)"), AX_X, ALU.max,
                                         apply_absolute_value=True))
                elif k == 4:
                    dve.wait_ge(prep_act, ACT_NORMS)
                    step(V.tensor_reduce(mxa[:, 4:5], mx[:, 4, 0:NJ], AX_X, ALU.max))
                    assert n[0] == DVE_MX_UP, ("DVE_MX_UP", n[0])
                    maxima(3, 5, ps_f, PE_MX_UP)
                    assert n[0] == DVE_MXD_UP, ("DVE_MXD_UP", n[0])
                    powers(3, 5, ps_f, PE_MXB_UP)
                elif k == 5:
                    for g, (_, w, high, low) in enumerate(up_groups):
                        dve.wait_ge(prep_act, ACT_NORMS + g + 1)
                        low_part(last_banks[g % 3], w, high, low, 3)
                    assert n[0] == DVE_LOW_UP, ("DVE_LOW_UP", n[0])
                    dve.wait_ge(prep_pool, POOL_ALL)
                    step(V.tensor_scalar(mx[:, 5, 1:2], rp[:, 4:5], 8.0, None, ALU.mult))
                    step(V.tensor_scalar(u_relu[:, :], p2[:, 3:4], 1.0 / 8192 / XS, mx[:, 5, 1:2], ALU.mult, ALU.mult))
                    step(V.tensor_scalar(mx[:, 5, 2:3], mx[:, 5, 1:2], mx[:, 5, 1:2], None, ALU.mult))
                    step(V.reciprocal(mx[:, 5, 3:4], mx[:, 5, 2:3]))
                    dve.wait_ge(prep_act, ACT_DN)
                    step(V.tensor_scalar(dn_bc[:, :], dn_bc[:, :], mx[:, 5, 3:4], None, ALU.mult))
                    assert n[0] == DVE_ALL, ("DVE_ALL", n[0])

            def input_stats(s, q):
                dve.wait_ge(x_loaded[q], s * 8 + (8 if q else 16))
                for c in range(NC):
                    V.bn_stats(st1[:, c], x_sb[:, q, c]).then_inc(st1_done, 1)
                dve.wait_ge(st1_done, at(s, NC, NC - 1))
                V.memset(pause[:, :], 0.0)
                for c in range(NC):
                    V.bn_aggr(mv1[:, c], st1[:, c]).then_inc(mv1_done, 1)

            def input_norm(s, q):
                dve.wait_ge(rs1_step, at(s, 3, 2))
                if type(s) is not int or s:
                    dve.wait_ge(xl_done, at(s - 1, 1, 0))
                for c in range(NC):
                    V.tensor_scalar(xn[:, c], x_sb[:, q, c], mv1[:, c, 0:1], rs1s[:, c:c + 1],
                                    ALU.subtract, ALU.mult).then_inc(xn_done, 1)

            DX, AXX, EX, RX, S1, Q1, DE, PL, A1 = range(9)

            def w(k):
                return dtw[:, k]

            def heads(t):
                return t[:, :].unsqueeze(1).to_broadcast([P, NC, NH])

            def dt_steps(s, q, k0, k1):
                raw = ps_t[0][:, 0:NC * NH].rearrange("p (c h) -> p c h", c=NC)
                cum = ps_t[1][:, 0:NC * NH].rearrange("p (c h) -> p c h", c=NC)
                tot = ps_t[1][:, NC * NH:2 * NC * NH].rearrange("p (c h) -> p c h", c=NC)
                rows = ps_t[0][:, :].bitcast(BF16)[0:NR, 0:P]
                for k in range(k0, k1):
                    if k == 0:
                        dve.wait_ge(dt_mm, at(s, 1, 0))
                    elif k == 17:
                        dve.wait_ge(dt_mm2, at(s, 2, 0))
                    elif k == 23:
                        dve.wait_ge(dt_mm2, at(s, 2, 1))
                    else:
                        if k == 3:
                            dve.wait_ge(dt_exp, at(s, 3, 0))
                        dve.wait_ge(dt_step, at(s, NDT, k - 1))
                    if k == 0:
                        i = V.scalar_tensor_tensor(w(DX), raw, u_in[:, :], heads(dtb), ALU.mult, ALU.add)
                    elif k == 1:
                        i = V.scalar_tensor_tensor(w(AXX), w(DX), -1.0, w(DX), ALU.mult, ALU.max)
                    elif k == 2:
                        i = V.tensor_scalar(w(RX), w(DX), 0.0, None, ALU.max)
                    elif k == 3:
                        i = V.tensor_scalar(w(S1), w(EX), 2.0, None, ALU.add)
                    elif k == 4:
                        i = V.reciprocal(w(Q1), w(S1))
                    elif k == 5:
                        i = V.tensor_tensor(w(S1), w(EX), w(Q1), ALU.mult)
                    elif k == 6:
                        i = V.tensor_tensor(w(Q1), w(S1), w(S1), ALU.mult)
                    elif k == 7:
                        i = V.tensor_scalar(w(PL), w(Q1), 1.0 / 13, None, ALU.mult)
                    elif k < 13:
                        i = V.scalar_tensor_tensor(w(PL), w(PL), 1.0 / (11, 9, 7, 5, 3)[k - 8], w(Q1), ALU.add, ALU.mult)
                    elif k == 13:
                        i = V.scalar_tensor_tensor(w(PL), w(PL), 1.0, w(S1), ALU.add, ALU.mult)
                    elif k == 14:
                        i = V.scalar_tensor_tensor(dt_[:, q], w(PL), 2.0, w(RX), ALU.mult, ALU.add)
                    elif k == 15:
                        i = V.tensor_tensor(w(A1), dt_[:, q], heads(a_neg), ALU.mult)
                    elif k == 16:
                        i = V.tensor_scalar(w(A1), w(A1), FLOOR, None, ALU.max)
                    elif k == 17:
                        i = V.tensor_copy(w(PL), cum)
                    elif k == 18:
                        i = V.tensor_tensor(w(DE), tot, w(PL), ALU.subtract)
                    elif k == 19:
                        i = V.tensor_copy(cp3[:, :, 0, :], w(PL))
                    elif k == 20:
                        i = V.tensor_tensor(w(RX), w(PL), cp3[:, :, 0, :], ALU.subtract)
                    elif k == 21:
                        i = V.tensor_copy(cp3[:, :, 1, :], w(RX))
                    elif k == 22:
                        i = V.tensor_tensor(cp3[:, :, 2, :], w(RX), cp3[:, :, 1, :], ALU.subtract)
                    elif k == 23:
                        i = V.tensor_copy(cT[:, q], rows)
                    else:
                        i = V.tensor_scalar(ncT[:, q], rows, -1.0, None, ALU.mult)
                    i.then_inc(dt_step, 1)

            def conv(s, k, taps=(1, 2, 3), tiles=(0, 1)):
                for d in taps:
                    for a in tiles:
                        m = CONV_ORDER[k + a]
                        if d == 1:
                            dve.wait_ge(acc_init, at(s, NM, k + a))
                        else:
                            dve.wait_ge(conv_step, at(s, 3 * NM, 3 * k + 2 * (d - 2) + a))
                        V.scalar_tensor_tensor(
                            acc[:, (k + a) % 4, d:T], proj_banks[PROJ.index(("c", m)) % NPB][:, 0:T - d],
                            cwu[:, m, 3 - d:4 - d], acc[:, (k + a) % 4, d:T], ALU.mult, ALU.add).then_inc(conv_step, 1)

            def weigh(s, c, g):
                if c == 0 and g == 0:
                    dve.wait_ge(g_done, at(s, 1, 0))
                dve.wait_ge(l_done, at(s, 2 * NC, 2 * c + g))
                if c >= 2:
                    dve.wait_ge(intra_mm, at(s, NC, c - 2))
                V.tensor_tensor(Mb[:, 2 * (c % 2) + g], Lb[:, g].rearrange("p (h t) -> p h t", h=4),
                                Gm[:, c].unsqueeze(1).to_broadcast([P, 4, P]), ALU.mult).then_inc(m_done, 1)

            def x_tokens(s, q, c):
                xt = ps_t[0][:, :].rearrange("p (h d) -> p h d", h=NH)
                dve.wait_ge(xt_mm, at(s, NC, c))
                if c >= 2:
                    dve.wait_ge(intra_mm, at(s, NC, c - 2))
                    dve.wait_ge(xst_done, at(s, NC - 1, c - 2))
                V.tensor_tensor(Xdt[:, c % 2].rearrange("p (h d) -> p h d", h=NH), xt,
                                dt_[:, q, c].unsqueeze(2).to_broadcast([P, NH, HD]), ALU.mult).then_inc(xdt_done, 1)

            def skip(s, q, c):
                xt = ps_t[0][:, :].rearrange("p (h d) -> p h d", h=NH)
                V.tensor_tensor(XD[:, c % 2].rearrange("p (h d) -> p h d", h=NH), xt,
                                d_bc[:, :].unsqueeze(2).to_broadcast([P, NH, HD]), ALU.mult).then_inc(xdt_done, 1)

            def from_state(s, q, c):
                dve.wait_ge(inter_mm, at(s, NC - 1, c - 1))
                V.tensor_tensor(ti[:, :].rearrange("p (h d) -> p h d", h=NH), ps_i[:, :].rearrange("p (h d) -> p h d", h=NH),
                                ecs[:, q, 0, c].unsqueeze(2).to_broadcast([P, NH, HD]), ALU.mult).then_inc(ti_done, 1)

            def y_sum(s, c):
                dve.wait_ge(intra_mm, at(s, NC, c))
                if c:
                    dve.wait_ge(ti2_done, at(s, NC - 1, c - 1))
                else:
                    dve.wait_ge(xdt_done, at(s, 2 * NC, 1))
                V.tensor_tensor(yb[:, c % 2], ps_y[:, :], ti2[:, :] if c else XD[:, 0], ALU.add).then_inc(y_done, 1)

            def next_state(s, c):
                dve.wait_ge(state_mm, at(s, NC - 1, c))
                dve.wait_ge(hd_done, at(s, NC - 2, c - 1))
                V.tensor_tensor(hst[:, c % 2], ps_i[:, :], hd[:, :], ALU.add).then_inc(h_done, 1)

            def gated(s, c):
                dve.wait_ge(rv_step, at(s, 3 * NC, 3 * c + 2))
                if c == 0:
                    dve.wait_ge(z_done, at(s, NC, NC - 1))
                V.scalar_tensor_tensor(yg[:, c % 2], yb[:, c % 2], rv[:, 2, c:c + 1], sz[:, c], ALU.mult,
                                       ALU.mult).then_inc(yg_done, 1)

            def residual(s, q, c):
                dve.wait_ge(o_mm, at(s, NC, c))
                V.scalar_tensor_tensor(x2[:, q, c], ps_t[0][:, 0:DM], u_out[:, :], x_sb[:, q, c], ALU.mult,
                                       ALU.add).then_inc(x2_done, 1)

            def moments(s, q, c):
                dve.wait_ge(x2_done, at(s, NC, c))
                V.bn_stats(st2[:, c], x2[:, q, c]).then_inc(st2_done, 1)

            def moments_sum(s, q, c):
                dve.wait_ge(st2_done, at(s, NC, c))
                V.memset(pause[:, :], 0.0)
                V.bn_aggr(mv2[:, c], st2[:, c]).then_inc(mv2_done, 1)

            def norm2(s, q, c):
                dve.wait_ge(rv2_step, at(s, 3 * NC, 3 * c + 2))
                V.tensor_scalar(xn2[:, c % 2], x2[:, q, c], mv2[:, c, 0:1], rv2[:, 2, c:c + 1],
                                ALU.subtract, ALU.mult).then_inc(xn2_done, 1)

            def relu_square(s, j):
                dve.wait_ge(r_done, at(s, NJ, j))
                if j >= 2:
                    dve.wait_ge(rl_done, at(s, NLP, j - 2))
                V.tensor_tensor(r2[:, j % 2], r[:, j % 2], r[:, j % 2], ALU.mult).then_inc(r2_done, 1)

            def relu_low(s, j):
                dve.wait_ge(rh_done, at(s, NJ, j))
                V.tensor_tensor(rT[:, LO, j], r2[:, j % 2], rT[:, HI, j], ALU.subtract).then_inc(rlv_done, 1)

            def down_scale(s, c):
                dve.wait_ge(dn_mm, at(s, NC, c))
                if c >= 2:
                    dve.wait_ge(ob_done, at(s, NC, c - 2))
                V.tensor_tensor(ot[:, c % 2], down_banks[c][:, 0:DM], dn_bc[:, :], ALU.mult).then_inc(ot_done, 1)

            def round_(s, q, ffn=True, nxt=True, hook=lambda k: None):
                p = 1 - q
                if ffn:
                    norm2(s - 1, p, 2)
                conv(s, 2, (1,), (0,))
                if ffn:
                    residual(s - 1, p, 3)
                    moments(s - 1, p, 3)
                conv(s, 2, (1,), (1,))
                if ffn:
                    moments_sum(s - 1, p, 3)
                conv(s, 2, (2,))
                conv(s, 2, (3,), (0,))
                if ffn:
                    norm2(s - 1, p, 3)
                conv(s, 2, (3,), (1,))
                hook(0)
                conv(s, 4)
                if nxt:
                    input_stats(s + 1, p)
                if ffn:
                    relu_square(s - 1, 0)
                    relu_square(s - 1, 1)
                if ffn:
                    relu_square(s - 1, 2)
                x_tokens(s, q, 0)
                weigh(s, 0, 0)
                weigh(s, 0, 1)
                skip(s, q, 0)
                if ffn:
                    relu_square(s - 1, 3)
                if nxt:
                    input_norm(s + 1, p)
                if ffn:
                    relu_square(s - 1, 4)
                dt = (lambda k0, k1: dt_steps(s + 1, p, k0, k1)) if nxt else (lambda k0, k1: None)
                for c in range(NC - 1):
                    if c:
                        from_state(s, q, c)
                    if c == 1 and ffn:
                        for j in range(NLP, NJ):
                            relu_low(s - 1, j)
                    if c == 2:
                        norm2(s, q, 0)
                        dt(0, 2)
                    if c:
                        weigh(s, c + 1, 0)
                    y_sum(s, c)
                    if c == 0:
                        weigh(s, 1, 0)
                        if ffn:
                            relu_square(s - 1, 5)
                    weigh(s, c + 1, 1)
                    x_tokens(s, q, c + 1)
                    skip(s, q, c + 1)
                    if c:
                        next_state(s, c)
                    if c == 2:
                        dt(2, 4)
                    if c == 0 and ffn:
                        relu_square(s - 1, 6)
                    gated(s, c)
                    if c == 0 and ffn:
                        relu_square(s - 1, 7)
                    if c == 2:
                        dt(4, 5)
                    if c:
                        if ffn:
                            down_scale(s - 1, c - 1)
                        if c == 2:
                            dt(5, 6)
                        residual(s, q, c - 1)
                        if c == 2:
                            dt(6, 7)
                        moments(s, q, c - 1)
                        if c == 2:
                            dt(7, 8)
                        moments_sum(s, q, c - 1)
                        if c == 2:
                            dt(8, 10)
                    hook(c + 1)
                from_state(s, q, 3)
                dt(10, 11)
                norm2(s, q, 1)
                dt(11, 14)
                y_sum(s, 3)
                dt(14, 17)
                gated(s, 3)
                if nxt:
                    conv(s + 1, 0, (1,))
                dt(17, 19)
                if ffn:
                    down_scale(s - 1, 2)
                dt(19, 20)
                residual(s, q, 2)
                dt(20, 21)
                moments(s, q, 2)
                dt(21, 23)
                moments_sum(s, q, 2)
                hook(4)
                if nxt:
                    conv(s + 1, 0, (2,))
                if ffn:
                    down_scale(s - 1, 3)
                dt(23, 25)
                if nxt:
                    conv(s + 1, 0, (3,))
                hook(5)

            def finish(s, q):
                norm2(s, q, 2)
                residual(s, q, 3)
                moments(s, q, 3)
                moments_sum(s, q, 3)
                norm2(s, q, 3)
                for j in range(NJ):
                    relu_square(s, j)
                for j in range(NLP, NJ):
                    relu_low(s, j)
                for c in range(NC):
                    down_scale(s, c)

            step(V.memset(pick[:, :, :], 0.0))
            assert n[0] == DVE_PICK, ("DVE_PICK", n[0])
            input_stats(0, 0)
            dve.wait_ge(in_loaded, 16 * 2)
            dve.wait_ge(zeroed, 1)
            step(V.tensor_reduce(mxa[:, 0:1], raw_in[:, :, :].rearrange("p a b -> p (a b)"), AX_X, ALU.max,
                                 apply_absolute_value=True))
            dve.wait_ge(prep_act, ACT_Z)
            step(V.tensor_reduce(mxa[:, 1:2], mx[:, 1, 0:DI // P], AX_X, ALU.max))
            assert n[0] == DVE_MX_IN, ("DVE_MX_IN", n[0])
            input_norm(0, 0)
            maxima(0, 2, ps_t[0], PE_MX_IN)
            assert n[0] == DVE_MXD_IN, ("DVE_MXD_IN", n[0])
            powers(0, 2, ps_t[0], PE_MXB_IN)
            assert n[0] == DVE_P2_IN + 2, ("DVE_P2_IN", n[0] - 2)
            dve.wait_ge(mixer_loaded, 16 * NMIX)
            step(V.tensor_scalar(u_in[:, :], p2[:, 0:1], 1.0 / 8192 / XS, None, ALU.mult))
            step(V.tensor_scalar(cwu[:, :, :].rearrange("p a b -> p (a b)"), cw[:, :, :].rearrange("p a b -> p (a b)"),
                                 u_in[:, :], None, ALU.mult))
            assert n[0] == DVE_IN, ("DVE_IN", n[0])
            for g, (_, cols, high, low) in enumerate(in_groups):
                dve.wait_ge(prep_act, ACT_EXP + g + 1)
                low_part(in_banks[g], cols, high, low, 0)
            assert n[0] == DVE_LOW_IN, ("DVE_LOW_IN", n[0])
            dve.wait_ge(prep_act, ACT_EXP)
            step(V.tensor_tensor(a_neg[:, :], aexp[:, 0, :], aexp[:, 1, :], ALU.add))
            step(V.tensor_tensor(a_neg[:, :], a_neg[:, :], aexp[:, 2, :], ALU.add))
            step(V.tensor_scalar(a_neg[:, :], a_neg[:, :], -1.0 / 3, None, ALU.mult))
            for g in range(2):
                dve.wait_ge(prep_pe, PE_WO - 1 + g)
                for k in range(2):
                    m = 2 * g + k
                    step(V.tensor_scalar(wo32[:, m], [ps_y, ps_i][g][:, k * DM:(k + 1) * DM], nw[:, m:m + 1], None, ALU.mult))
            assert n[0] == DVE_WO32, ("DVE_WO32", n[0])
            dt_steps(0, 0, 0, 3)
            step(V.tensor_reduce(mxa[:, 2:3], wo32.rearrange("p a b -> p (a b)"), AX_X, ALU.max, apply_absolute_value=True))
            assert n[0] == DVE_MX_WO, ("DVE_MX_WO", n[0])
            dt_steps(0, 0, 3, 17)
            maxima(2, 3, ps_f, PE_MX_WO)
            assert n[0] == DVE_MXD_WO, ("DVE_MXD_WO", n[0])
            dt_steps(0, 0, 17, 23)
            powers(2, 3, ps_f, PE_MXB_WO)
            dt_steps(0, 0, 23, 25)
            dve.wait_ge(prep_act, ACT_SUMS)
            row_scales(dns, HID)
            assert n[0] == DVE_SUMS, ("DVE_SUMS", n[0])
            conv(0, 0)
            dve.wait_ge(prep_act, ACT_FC)
            row_scales(fcs, DM)
            round_(0, 0, ffn=False, hook=prepare)
            with dve.Fori(0, S // 2 - 1) as i:
                round_(i * 2 + 1, 1)
                round_(i * 2 + 2, 0)
            round_(S - 1, 1, nxt=False)
            finish(S - 1, 1)

        @block.tensor
        def _(pe):
            n = [0]

            def step(ins):
                n[0] += 1
                ins.then_inc(prep_pe, 1)

            mm, tr = nc.tensor.matmul, nc.tensor.transpose
            def maxima(a, b, bank):
                step(tr(bank[0:b - a, 0:P], mxa[:, a:b], ident[:, :]))

            def spread(k, bank):
                step(mm(bank[:, 0:k], ones[0:k, :], mxd[0:k, 0:k], start=True, stop=True))

            def group(src, bank):
                for k, a in enumerate(src):
                    rows = a.shape[0]
                    i = tr(bank[:, k * P:k * P + rows], a, ident[0:rows, 0:rows])
                step(i)

            def low_rank(j):
                if j >= 4:
                    pe.wait_ge(prep_dve, DVE_DN + 3 * (j - 2))
                for a in range(2):
                    i = mm(late_banks[j // 2 % 2][:, a * DM:(a + 1) * DM], uT[:, j + a, :], fv[:, :], start=True, stop=True)
                i.then_inc(lr_mm, 1)

            def down_weights(g):
                pe.wait_ge(prep_act, ACT_WO + g)
                group(dn_groups[g][0], late_banks[g % 2])

            def prepare(k):
                if k == 0:
                    pe.wait_ge(prep_pool, POOL_PICK)
                elif k == 0.5:
                    pe.wait_ge(prep_dve, DVE_DN)
                    pe.wait_ge(xc_done, NM)
                    pe.wait_ge(z_done, NC)
                    for j in range(KD):
                        i = mm(ps_f[:, j * P:(j + 1) * P], ones[:, :], dnd[:, j], start=True, stop=True)
                    step(i)
                    assert n[0] == PE_DNS, ("PE_DNS", n[0])
                    pe.wait_ge(prep_pool, POOL_TERN)
                    down_weights(0)
                elif k == 1:
                    down_weights(1)
                    down_weights(2)
                elif k == 1.5:
                    down_weights(3)
                elif k == 2:
                    pe.wait_ge(prep_act, ACT_DN)
                    low_rank(0)
                    low_rank(2)
                elif k == 3:
                    low_rank(4)
                    low_rank(6)
                elif k == 4:
                    pe.wait_ge(prep_dve, DVE_MX_UP)
                    maxima(3, 5, ps_f)
                    assert n[0] == PE_MX_UP, ("PE_MX_UP", n[0])
                    pe.wait_ge(prep_dve, DVE_MXD_UP)
                    spread(2, ps_f)
                    assert n[0] == PE_MXB_UP, ("PE_MXB_UP", n[0])
                    pe.wait_ge(prep_dve, DVE_MXD_UP + 1)
                    pe.wait_ge(y_done, NC)
                    pe.wait_ge(ti_done, NC - 1)
                    for g, (src, _, _, _) in enumerate(up_groups):
                        if g >= 3:
                            pe.wait_ge(prep_dve, DVE_LOW_UP - 4 + g - 2)
                        group(src, last_banks[g % 3])
                    pe.wait_ge(prep_dve, DVE_LOW_UP)
                    pe.wait_ge(prep_act, ACT_UP)

            def input_transpose(s, part):
                pe.wait_ge(xh_done if part == HI else xl_done, at(s, 1, 0))
                for k in range(KD):
                    for c in range(NC):
                        i = tr(half(ps_t[1], KD * T)[:, k * T + c * P:k * T + (c + 1) * P],
                               (xh if part == HI else xl)[:, c, k * P:(k + 1) * P], ident16[:, :])
                i.then_inc(xT_ready, 1)

            def three(ps, lhs, rhs, kk):
                for a, (wp, xp) in enumerate(PASSES):
                    for k in range(kk):
                        i = mm(ps, lhs(wp, xp, k), rhs(wp, xp, k), start=(a == 0 and k == 0),
                               stop=(a == 2 and k == kk - 1))
                return i

            def dt_product(s):
                pe.wait_ge(xhT_copied, at(s, 1, 0))
                pe.wait_ge(xlT_copied, at(s, 1, 0))
                for c in range(NC):
                    i = three(ps_t[0][:, c * NH:(c + 1) * NH],
                              lambda wp, xp, k: xnT[:, xp, k, c * P:(c + 1) * P],
                              lambda wp, xp, k: w_in[:, wp, k, NPROJ - NH:NPROJ], KD)
                i.then_inc(dt_mm, 1)

            def cumulate(s):
                pe.wait_ge(dt_step, at(s, NDT, 16))
                a = dtw[:, 8].rearrange("p c h -> p (c h)")
                mm(ps_t[1][:, 0:NC * NH], tri[:, :], a, start=True, stop=True)
                mm(ps_t[1][:, NC * NH:2 * NC * NH], ones[:, :], a, start=True, stop=True).then_inc(dt_mm2, 1)

            def cum_rows(s):
                pe.wait_ge(dt_step, at(s, NDT, 22))
                tr(ps_t[0][:, :].bitcast(BF16)[0:NR, 0:P], cp3[:, :, :, :].rearrange("p a b c -> p (a b c)"),
                   identb[:, :]).then_inc(dt_mm2, 1)

            def project(s, k):
                kind, m = PROJ[k]
                if k >= NPB:
                    kind2, m2 = PROJ[k - NPB]
                    if kind2 == "c":
                        pe.wait_ge(conv_step, at(s, 3 * NM, conv_end(CONV_ORDER.index(m2))))
                    else:
                        pe.wait_ge(z_done, at(s, NC, m2))
                elif type(s) is not int or s:
                    if k == 0:
                        pe.wait_ge(l_done, at(s - 1, 2 * NC, 2 * NC - 1))
                    elif k == 2:
                        pe.wait_ge(dt_step, at(s, NDT, 16))
                    elif k == 3:
                        pe.wait_ge(y_done, at(s - 1, NC, NC - 1))
                    elif k == 4:
                        pe.wait_ge(ti_done, at(s - 1, NC - 1, NC - 2))
                if kind == "c":
                    i = three(proj_banks[k % NPB][:, :], lambda wp, xp, kk: w_in[:, wp, kk, DI + m * P:DI + (m + 1) * P],
                              lambda wp, xp, kk: xnT[:, xp, kk, :], KD)
                else:
                    i = three(proj_banks[k % NPB][:, :], lambda wp, xp, kk: xnT[:, xp, kk, m * P:(m + 1) * P],
                              lambda wp, xp, kk: w_in[:, wp, kk, 0:DI], KD)
                i.then_inc(proj_done, 1)

            XB, XC = 4, 5

            def b_transpose(s):
                pe.wait_ge(xc_done, at(s, NM, 0))
                for c in range(NC):
                    i = tr(ps_t[0][:, c * P:(c + 1) * P], xc[:, XB, c * P:(c + 1) * P], ident[:, :])
                i.then_inc(bt_mm, 1)

            def g_product(s):
                pe.wait_ge(xc_done, at(s, NM, 1))
                for c in range(NC):
                    i = mm(ps_t[1][:, c * P:(c + 1) * P], xc[:, XB, c * P:(c + 1) * P], xc[:, XC, c * P:(c + 1) * P],
                           start=True, stop=True)
                i.then_inc(g_mm, 1)

            def decay_logs(s, q, c, g):
                if c == 0:
                    pe.wait_ge(dt_step, at(s, NDT, 24))
                    pe.wait_ge(z_done, at(s, NC, NC - 1))
                    pe.wait_ge(xc_done, at(s, NM, NM - 1))
                else:
                    pe.wait_ge(l_done, at(s, 2 * NC, 2 * c + g - 2))
                rows = pick[:, c * NH + 4 * g:c * NH + 4 * g + 4, :]
                for h in range(4):
                    mm(d_banks[g][:, h * P:(h + 1) * P], pick[:, c * NH + 4 * g + h, :], cT[:, q], start=(h == 0), stop=False)
                mm(d_banks[g][:, :], identb[:, :], above[:, :, :].rearrange("p h t -> p (h t)"), start=False, stop=False)
                mm(d_banks[g][:, :], ncT[:, q], rows.rearrange("k h p -> k (h p)"), start=False, stop=True).then_inc(d_mm, 1)

            def x_transpose(s, c, nxt=True):
                if c == 0:
                    pe.wait_ge(bt_copied, at(s, 1, 0))
                    pe.wait_ge(xc_done, at(s, NM, NM - 1))
                elif c < 3:
                    pe.wait_ge(xdt_done, at(s, 2 * NC, 2 * c - 1))
                elif nxt:
                    pe.wait_ge(dt_step, at(s + 1, NDT, 0))
                else:
                    pe.wait_ge(x2_done, at(s, NC, 0))
                for m in range(DI // P):
                    i = tr(ps_t[0][:, m * P:(m + 1) * P], xc[:, m, c * P:(c + 1) * P], ident[:, :])
                i.then_inc(xt_mm, 1)

            def intra(s, c):
                pe.wait_ge(m_done, at(s, 2 * NC, 2 * c + 1))
                pe.wait_ge(xdt_done, at(s, 2 * NC, 2 * c))
                if c:
                    pe.wait_ge(y_done, at(s, NC, c - 1))
                elif type(s) is not int or s:
                    pe.wait_ge(y_done, at(s - 1, NC, NC - 1))
                for h in range(NH):
                    i = mm(ps_y[:, h * HD:(h + 1) * HD], Mb[:, 2 * (c % 2) + h // 4, h % 4, :],
                           Xdt[:, c % 2, h * HD:(h + 1) * HD], start=True, stop=True)
                i.then_inc(intra_mm, 1)

            def inter(s, c):
                pe.wait_ge(h_done, at(s, NC - 1, c - 1))
                mm(ps_i[:, :], xc[:, XC, c * P:(c + 1) * P], hst[:, (c - 1) % 2], start=True, stop=True).then_inc(inter_mm, 1)

            def state(s, c):
                pe.wait_ge(xst_done, at(s, NC - 1, c))
                if c:
                    pe.wait_ge(ti_done, at(s, NC - 1, c - 1))
                elif type(s) is not int or s:
                    pe.wait_ge(ti_done, at(s - 1, NC - 1, NC - 2))
                mm(ps_i[:, :], Bt[:, c, :], Xst[:, c % 2], start=True, stop=True).then_inc(state_mm, 1)

            def gate_transpose(s, c):
                pe.wait_ge(ygh_done, at(s, NC, c))
                pe.wait_ge(ygl_done, at(s, NC, c))
                dst = half(ps_t[1], 2 * DI)
                for part, src in ((HI, ygh), (LO, ygl)):
                    for m in range(DI // P):
                        i = tr(dst[:, part * DI + m * P:part * DI + (m + 1) * P], src[:, c % 2, m * P:(m + 1) * P], ident16[:, :])
                i.then_inc(yT_mm, 1)

            def out_product(s, c):
                pe.wait_ge(yT_copied, at(s, NC, c))
                three(ps_t[0][:, 0:DM], lambda wp, xp, k: ygT[:, c % 2, xp, k, :],
                      lambda wp, xp, k: w_o[:, wp, k, :], DI // P).then_inc(o_mm, 1)

            def transpose2(s, c):
                pe.wait_ge(x2h_done, at(s, NC, c))
                pe.wait_ge(x2l_done, at(s, NC, c))
                dst = half(ps_t[1], 2 * KD * P)
                for part, src in ((HI, x2h), (LO, x2l)):
                    for k in range(KD):
                        i = tr(dst[:, (part * KD + k) * P:(part * KD + k + 1) * P], src[:, c % 2, k * P:(k + 1) * P], ident16[:, :])
                i.then_inc(x2T_mm, 1)

            def up(s, q, j, last=False):
                if j == 0:
                    pe.wait_ge(x2T_copied, at(s, NC, NC - 1))
                elif last:
                    if j >= 2:
                        pe.wait_ge(r_done, at(s, NJ, j - 2))
                elif j != 3:
                    pe.wait_ge(r_done, at(s, NJ, j - 1 if j < 3 else j - 2))
                three((down_banks[j % 2] if last else up_banks[j])[:, :], lambda wp, xp, k: w_up[:, wp, k, j * P:(j + 1) * P],
                      lambda wp, xp, k: xn2T[:, q, xp, k, :], KD).then_inc(up_mm, 1)

            def down(s, c):
                if c == 0:
                    pe.wait_ge(r_done, at(s, NJ, NJ - 1))
                    pe.wait_ge(rh_done, at(s, NJ, NJ - 1))
                elif c >= 2:
                    pe.wait_ge(ot_done, at(s, NC, 2 * c - 4))
                for part in (HI, LO):
                    if c == 0 and part == LO:
                        pe.wait_ge(rl_done, at(s, NLP, NLP - 1))
                        pe.wait_ge(rlv_done, at(s, NJ - NLP, NJ - NLP - 1))
                    for j in range(NJ):
                        i = mm(down_banks[c][:, 0:DM], rT[:, part, j, c * P:(c + 1) * P], w_dn[:, j, :],
                               start=(part == HI and j == 0), stop=(part == LO and j == NJ - 1))
                i.then_inc(dn_mm, 1)

            def round_(s, q, ffn=True, nxt=True, hook=lambda k: None):
                p = 1 - q
                if ffn:
                    pe.wait_ge(x2T_copied, at(s - 1, NC, 1))
                    gate_transpose(s - 1, 3)
                project(s, 3)
                if ffn:
                    pe.wait_ge(dt_step, at(s, NDT, 24))
                    pe.wait_ge(yT_copied, at(s - 1, NC, 3))
                    out_product(s - 1, 3)
                project(s, 4)
                if ffn:
                    transpose2(s - 1, 2)
                project(s, 5)
                project(s, 6)
                project(s, 7)
                if ffn:
                    pe.wait_ge(x2T_copied, at(s - 1, NC, 2))
                    transpose2(s - 1, 3)
                project(s, 8)
                if ffn:
                    up(s - 1, p, 0)
                project(s, 9)
                if ffn:
                    up(s - 1, p, 1)
                    pe.wait_ge(x2_done, at(s - 1, NC, 3))
                else:
                    pe.wait_ge(dt_step, at(s, NDT, 24))
                b_transpose(s)
                if ffn:
                    pe.wait_ge(x2T_copied, at(s - 1, NC, 3))
                g_product(s)
                if ffn:
                    up(s - 1, p, 2)
                hook(0)
                decay_logs(s, q, 0, 0)
                decay_logs(s, q, 0, 1)
                x_transpose(s, 0)
                hook(0.5)
                if ffn:
                    up(s - 1, p, 3)
                    up(s - 1, p, 4)
                for c in range(NC):
                    if c:
                        inter(s, c)
                    if c < NC - 1:
                        decay_logs(s, q, c + 1, 0)
                    intra(s, c)
                    if c == 2 and nxt:
                        pe.wait_ge(x2_done, at(s, NC, 0))
                        dt_product(s + 1)
                    if c < NC - 1:
                        if c == 0 and ffn:
                            up(s - 1, p, 5)
                        decay_logs(s, q, c + 1, 1)
                    if c == 1:
                        hook(1.5)
                    if c == 0 and nxt:
                        pe.wait_ge(g_done, at(s, 1, 0))
                        input_transpose(s + 1, HI)
                    elif c == 1:
                        if nxt:
                            pe.wait_ge(xlT_copied, at(s + 1, 1, 0))
                        else:
                            pe.wait_ge(g_done, at(s, 1, 0))
                        gate_transpose(s, 0)
                    elif c == 2:
                        pe.wait_ge(yT_copied, at(s, NC, 0))
                        gate_transpose(s, 1)
                    elif c == 3:
                        pe.wait_ge(x2T_copied, at(s, NC, 0))
                        gate_transpose(s, 2)
                    if c < NC - 1:
                        state(s, c)
                        x_transpose(s, c + 1, nxt)
                    if c == 0:
                        if ffn:
                            up(s - 1, p, 6)
                            up(s - 1, p, 7)
                        if nxt:
                            pe.wait_ge(xhT_copied, at(s + 1, 1, 0))
                            input_transpose(s + 1, LO)
                    else:
                        if c == 3 and nxt:
                            project(s + 1, 0)
                            project(s + 1, 1)
                        if ffn:
                            down(s - 1, c - 1)
                        if c == 3 and nxt:
                            pe.wait_ge(yT_copied, at(s, NC, 2))
                            cumulate(s + 1)
                        if c < 3:
                            pe.wait_ge(xdt_done, at(s, 2 * NC, 2 * c + 3))
                        else:
                            pe.wait_ge(x2_done, at(s, NC, 1))
                        out_product(s, c - 1)
                        if c == 2:
                            pe.wait_ge(yT_copied, at(s, NC, 1))
                            transpose2(s, 0)
                        if c == 3:
                            if nxt:
                                project(s + 1, 2)
                                pe.wait_ge(dt_exp, at(s + 1, 3, 1))
                            else:
                                pe.wait_ge(yT_copied, at(s, NC, 2))
                            transpose2(s, 1)
                    if c < NC - 1:
                        hook(c + 1)
                if ffn:
                    down(s - 1, 3)
                if nxt:
                    pe.wait_ge(x2_done, at(s, NC, 2))
                    cum_rows(s + 1)
                hook(NC)

            def finish(s, q):
                pe.wait_ge(x2T_copied, at(s, NC, 1))
                gate_transpose(s, 3)
                pe.wait_ge(x2_done, at(s, NC, 2))
                out_product(s, 3)
                transpose2(s, 2)
                pe.wait_ge(x2T_copied, at(s, NC, 2))
                transpose2(s, 3)
                for j in range(NJ):
                    up(s, q, j, last=True)
                for c in range(NC):
                    down(s, c)

            pe.wait_ge(in_loaded, 16 * 2)
            pe.wait_ge(zeroed, 1)
            pe.wait_ge(prep_pool, POOL_IDENT)
            for (src, _, _, _), bank in zip(in_groups, in_banks):
                group(src, bank)
            assert n[0] == PE_GROUPS, ("PE_GROUPS", n[0])
            pe.wait_ge(prep_dve, DVE_MX_IN)
            maxima(0, 2, ps_t[0])
            assert n[0] == PE_MX_IN, ("PE_MX_IN", n[0])
            pe.wait_ge(prep_dve, DVE_MXD_IN)
            spread(2, ps_t[0])
            assert n[0] == PE_MXB_IN, ("PE_MXB_IN", n[0])
            pe.wait_ge(prep_pool, POOL_CONST)
            input_transpose(0, HI)
            pe.wait_ge(ffn_loaded, 16 * NFFN)
            pe.wait_ge(prep_dve, DVE_MXD_IN + 1)
            step(mm(ps_t[0][0:RANK, 0:DM], fbT[:, :], raw_v[:, :], start=True, stop=True))
            assert n[0] == PE_FV, ("PE_FV", n[0])
            for g in range(2):
                pe.wait_ge(prep_dve, DVE_IN + g + 1)
                for a in range(4):
                    i = tr(ps_proj[g][0:RANK, a * P:(a + 1) * P], raw_u[:, 4 * g + a, :], ident[:, :])
                step(i)
            assert n[0] == PE_UT, ("PE_UT", n[0])
            pe.wait_ge(prep_dve, DVE_LOW_IN - 2)
            pe.wait_ge(mixer_loaded, 16 * NMIX)
            for g in range(2):
                for k in range(2):
                    for j in range(KD):
                        i = tr([ps_y, ps_i][g][:, k * DM + j * P:k * DM + (j + 1) * P],
                               raw_out[:, j, (2 * g + k) * P:(2 * g + k + 1) * P], ident[:, :])
                step(i)
            assert n[0] == PE_WO, ("PE_WO", n[0])
            pe.wait_ge(xhT_copied, 1)
            input_transpose(0, LO)
            pe.wait_ge(prep_dve, DVE_LOW_IN)
            pe.wait_ge(prep_act, ACT_UT)
            dt_product(0)
            project(0, 0)
            pe.wait_ge(prep_dve, DVE_MX_WO)
            maxima(2, 3, ps_f)
            assert n[0] == PE_MX_WO, ("PE_MX_WO", n[0])
            project(0, 1)
            cumulate(0)
            pe.wait_ge(prep_dve, DVE_MXD_WO)
            spread(1, ps_f)
            assert n[0] == PE_MXB_WO, ("PE_MXB_WO", n[0])
            cum_rows(0)
            pe.wait_ge(prep_dve, DVE_WO32)
            project(0, 2)
            round_(0, 0, ffn=False, hook=prepare)
            with pe.Fori(0, S // 2 - 1) as i:
                round_(i * 2 + 1, 1)
                round_(i * 2 + 2, 0)
            round_(S - 1, 1, nxt=False)
            finish(S - 1, 1)


_INS = ["u", "in_proj_w", "conv_w", "conv_b", "dt_bias", "A_log", "D", "norm_w", "out_proj_w"]
_FFN = ["fast_b", "w_fc", "w_proj", "u", "v", "gate"]


def kernel(**inputs):
    import numpy as _np
    import concourse.bacc as _bacc
    from concourse import mybir as _mybir
    from concourse.bass_utils import run_bass_kernel_spmd as _run

    nc = _bacc.Bacc("TRN2", target_bir_lowering=False, num_devices=1)
    arrays, args = {}, []
    for name in ["L0_attn_" + n for n in _INS] + ["L0_ffn_" + n for n in _FFN]:
        a = _np.ascontiguousarray(inputs[name])
        a = a.reshape(a.shape or (1,))
        arrays[f"in_{name}"] = a
        args.append(nc.dram_tensor(f"in_{name}", a.shape, _mybir.dt.from_np(a.dtype), kind="ExternalInput").ap())
    shape = inputs["L0_attn_u"].shape
    args.append(nc.dram_tensor("out_0", shape, _mybir.dt.float32, kind="ExternalOutput").ap())
    build(nc, *args)
    r = _run(nc, [arrays], core_ids=[0])
    return r.results[0]["out_0"]
```
